# Optimizing a Trainium2 kernel written in Bass

```python
import numpy as np
import jax
import jax.numpy as jnp

def _softmax(x, axis=-1):
    return jax.nn.softmax(x, axis=axis)

def _gelu(x):
    return jax.nn.gelu(x, approximate=True)

def _silu(x):
    return jax.nn.silu(x)

def _sigmoid(x):
    return jax.nn.sigmoid(x)

def _layernorm(x, axis=-1, eps=1e-05):
    m = jnp.mean(x, axis=axis, keepdims=True)
    v = jnp.var(x, axis=axis, keepdims=True)
    return (x - m) / jnp.sqrt(v + eps)

def _scatter_add(tgt, idx, src, axis=0):
    return tgt.at[idx].add(src)

def _segment_sum(src, seg, n):
    return jax.ops.segment_sum(src, seg, n)
kernel_name = 'mk_macaron_d1_jaxref_r8_891ee3'

def setup_inputs(seed: int=0):
    np.random.seed(seed)
    _w = jnp.asarray

    def _L0_attn_setup():
        import jax, jax.numpy as jnp
        import numpy as np
        B, T, HID = (4, 256, 128)
        H, D, V = (8, 64, 128)
        EPS = 1e-05

        def _rotary(x, T, D):
            inv_freq = 1.0 / 10000.0 ** (jnp.arange(0, D, 2, dtype=jnp.float32) / D)
            t = jnp.arange(T, dtype=jnp.float32)
            freqs = t[:, None] * inv_freq[None, :]
            emb = jnp.concatenate([freqs, freqs], axis=-1)
            cos = jnp.cos(emb)[None, None, :, :]
            sin = jnp.sin(emb)[None, None, :, :]
            x1, x2 = jnp.split(x, 2, axis=-1)
            rot = jnp.concatenate([-x2, x1], axis=-1)
            return x * cos + rot * sin
        key = jax.random.key(seed)
        ks = jax.random.split(key, 7)
        sc = 0.02
        return {'x': jax.random.normal(ks[0], (B, T, HID), dtype=jnp.float32), 'Wq': jax.random.normal(ks[1], (H * D, HID), dtype=jnp.float32) * sc, 'Wk': jax.random.normal(ks[2], (H * D, HID), dtype=jnp.float32) * sc, 'Wv': jax.random.normal(ks[3], (H * V, HID), dtype=jnp.float32) * sc, 'Wg': jax.random.normal(ks[4], (H * V, HID), dtype=jnp.float32) * sc, 'Wo': jax.random.normal(ks[5], (HID, H * V), dtype=jnp.float32) * sc, 'gn_weight': jnp.ones((H * V,), dtype=jnp.float32), 'gn_bias': jnp.zeros((H * V,), dtype=jnp.float32)}
    _L0_attn_in = _L0_attn_setup()

    def _L0_ffn_setup():
        import jax, jax.numpy as jnp
        import numpy as np
        B, S, D = (2, 128, 128)
        H, HD = (16, 64)
        E_R = 31
        K_ACT = 3
        INTER = 128
        EPS = 1e-05
        BASE = 10000.0

        def _rmsnorm(x, gamma):
            rms = jnp.sqrt(jnp.mean(x * x, axis=-1, keepdims=True) + EPS)
            return x / rms * gamma

        def _rope(x, theta):
            seq = x.shape[2]
            angles = jnp.arange(seq, dtype=theta.dtype)[:, None] * theta
            cos = jnp.cos(angles)[None, None]
            sin = jnp.sin(angles)[None, None]
            x1, x2 = (x[..., 0::2], x[..., 1::2])
            return jnp.concatenate([x1 * cos - x2 * sin, x1 * sin + x2 * cos], axis=-1)

        def _forward(x, theta, gamma1, gamma2, q_w, q_b, k_w, k_b, v_w, v_b, o_w, o_b, router_w, router_b, sh_w1, sh_b1, sh_w2, sh_b2, re_w1, re_b1, re_w2, re_b2):
            b, s, d = x.shape
            xn = _rmsnorm(x, gamma1)
            q = (xn @ q_w + q_b).reshape(b, s, H, HD).transpose(0, 2, 1, 3)
            k = (xn @ k_w + k_b).reshape(b, s, H, HD).transpose(0, 2, 1, 3)
            v = (xn @ v_w + v_b).reshape(b, s, H, HD).transpose(0, 2, 1, 3)
            q = _rope(q, theta)
            k = _rope(k, theta)
            scale = 1.0 / np.sqrt(HD)
            scores = jnp.einsum('bhqd,bhkd->bhqk', q, k) * scale
            causal = jnp.tril(jnp.ones((s, s), dtype=bool))
            scores = jnp.where(causal, scores, -jnp.inf)
            attn = jax.nn.softmax(scores, axis=-1)
            ctx = jnp.einsum('bhqk,bhkd->bhqd', attn, v)
            ctx = ctx.transpose(0, 2, 1, 3).reshape(b, s, H * HD)
            attn_out = ctx @ o_w + o_b + xn
            an = _rmsnorm(attn_out, gamma2)
            shared = jax.nn.gelu(an @ sh_w1 + sh_b1, approximate=False) @ sh_w2 + sh_b2
            logits = an @ router_w + router_b
            aff = jax.nn.softmax(logits, axis=-1)
            topv, topi = jax.lax.top_k(aff, K_ACT)
            gates = jnp.sum(jax.nn.one_hot(topi, E_R, dtype=aff.dtype) * topv[..., None], axis=-2)
            h = jax.nn.gelu(jnp.einsum('bsd,edh->besh', an, re_w1) + re_b1[None, :, None, :], approximate=False)
            routed = jnp.einsum('bse,besh,ehd->bsd', gates, h, re_w2) + jnp.einsum('bse,ed->bsd', gates, re_b2)
            return shared + routed + an + attn_out
        key = jax.random.key(seed)
        ks = jax.random.split(key, 24)
        s = 0.02
        theta = BASE ** (-jnp.arange(HD // 2, dtype=jnp.float32) * 2.0 / HD)
        inp = {'x': jax.random.normal(ks[0], (B, S, D), jnp.float32), 'positions': jnp.arange(S, dtype=jnp.int32), 'theta': theta, 'gamma1': jnp.ones((D,), jnp.float32), 'gamma2': jnp.ones((D,), jnp.float32), 'q_w': jax.random.normal(ks[1], (D, H * HD), jnp.float32) * s, 'q_b': jnp.zeros((H * HD,), jnp.float32), 'k_w': jax.random.normal(ks[2], (D, H * HD), jnp.float32) * s, 'k_b': jnp.zeros((H * HD,), jnp.float32), 'v_w': jax.random.normal(ks[3], (D, H * HD), jnp.float32) * s, 'v_b': jnp.zeros((H * HD,), jnp.float32), 'o_w': jax.random.normal(ks[4], (H * HD, D), jnp.float32) * s, 'o_b': jnp.zeros((D,), jnp.float32), 'router_w': jax.random.normal(ks[5], (D, E_R), jnp.float32) * s, 'router_b': jnp.zeros((E_R,), jnp.float32), 'sh_w1': jax.random.normal(ks[6], (D, INTER), jnp.float32) * s, 'sh_b1': jnp.zeros((INTER,), jnp.float32), 'sh_w2': jax.random.normal(ks[7], (INTER, D), jnp.float32) * s, 'sh_b2': jnp.zeros((D,), jnp.float32), 're_w1': jax.random.normal(ks[8], (E_R, D, INTER), jnp.float32) * s, 're_b1': jnp.zeros((E_R, INTER), jnp.float32), 're_w2': jax.random.normal(ks[9], (E_R, INTER, D), jnp.float32) * s, 're_b2': jnp.zeros((E_R, D), jnp.float32)}
        return inp
    _L0_ffn_in = _L0_ffn_setup()
    _d = {'L0_attn_x': _L0_attn_in['x'], 'L0_attn_Wq': _L0_attn_in['Wq'], 'L0_attn_Wk': _L0_attn_in['Wk'], 'L0_attn_Wv': _L0_attn_in['Wv'], 'L0_attn_Wg': _L0_attn_in['Wg'], 'L0_attn_Wo': _L0_attn_in['Wo'], 'L0_attn_gn_weight': _L0_attn_in['gn_weight'], 'L0_attn_gn_bias': _L0_attn_in['gn_bias'], 'L0_ffn_positions': _L0_ffn_in['positions'], 'L0_ffn_theta': _L0_ffn_in['theta'], 'L0_ffn_gamma1': _L0_ffn_in['gamma1'], 'L0_ffn_gamma2': _L0_ffn_in['gamma2'], 'L0_ffn_q_w': _L0_ffn_in['q_w'], 'L0_ffn_q_b': _L0_ffn_in['q_b'], 'L0_ffn_k_w': _L0_ffn_in['k_w'], 'L0_ffn_k_b': _L0_ffn_in['k_b'], 'L0_ffn_v_w': _L0_ffn_in['v_w'], 'L0_ffn_v_b': _L0_ffn_in['v_b'], 'L0_ffn_o_w': _L0_ffn_in['o_w'], 'L0_ffn_o_b': _L0_ffn_in['o_b'], 'L0_ffn_router_w': _L0_ffn_in['router_w'], 'L0_ffn_router_b': _L0_ffn_in['router_b'], 'L0_ffn_sh_w1': _L0_ffn_in['sh_w1'], 'L0_ffn_sh_b1': _L0_ffn_in['sh_b1'], 'L0_ffn_sh_w2': _L0_ffn_in['sh_w2'], 'L0_ffn_sh_b2': _L0_ffn_in['sh_b2'], 'L0_ffn_re_w1': _L0_ffn_in['re_w1'], 'L0_ffn_re_b1': _L0_ffn_in['re_b1'], 'L0_ffn_re_w2': _L0_ffn_in['re_w2'], 'L0_ffn_re_b2': _L0_ffn_in['re_b2']}
    _x0 = _d['L0_attn_x']
    _d['L0_attn_x'] = jax.random.normal(jax.random.fold_in(jax.random.key(seed), 1), (16, 256, 128), dtype=_x0.dtype)
    del _x0
    return _d

def reference(L0_attn_x, L0_attn_Wq, L0_attn_Wk, L0_attn_Wv, L0_attn_Wg, L0_attn_Wo, L0_attn_gn_weight, L0_attn_gn_bias, L0_ffn_positions, L0_ffn_theta, L0_ffn_gamma1, L0_ffn_gamma2, L0_ffn_q_w, L0_ffn_q_b, L0_ffn_k_w, L0_ffn_k_b, L0_ffn_v_w, L0_ffn_v_b, L0_ffn_o_w, L0_ffn_o_b, L0_ffn_router_w, L0_ffn_router_b, L0_ffn_sh_w1, L0_ffn_sh_b1, L0_ffn_sh_w2, L0_ffn_sh_b2, L0_ffn_re_w1, L0_ffn_re_b1, L0_ffn_re_w2, L0_ffn_re_b2):

    def _L0_attn_ref(x, Wq, Wk, Wv, Wg, Wo, gn_weight, gn_bias):
        import jax, jax.numpy as jnp
        import numpy as np
        B, T, HID = (4, 256, 128)
        H, D, V = (8, 64, 128)
        EPS = 1e-05

        def _rotary(x, T, D):
            inv_freq = 1.0 / 10000.0 ** (jnp.arange(0, D, 2, dtype=jnp.float32) / D)
            t = jnp.arange(T, dtype=jnp.float32)
            freqs = t[:, None] * inv_freq[None, :]
            emb = jnp.concatenate([freqs, freqs], axis=-1)
            cos = jnp.cos(emb)[None, None, :, :]
            sin = jnp.sin(emb)[None, None, :, :]
            x1, x2 = jnp.split(x, 2, axis=-1)
            rot = jnp.concatenate([-x2, x1], axis=-1)
            return x * cos + rot * sin
        Bx, Tx, _ = x.shape
        q = jnp.einsum('bti,oi->bto', x, Wq).reshape(Bx, Tx, H, D).transpose(0, 2, 1, 3)
        k = jnp.einsum('bti,oi->bto', x, Wk).reshape(Bx, Tx, H, D).transpose(0, 2, 1, 3)
        v = jnp.einsum('bti,oi->bto', x, Wv).reshape(Bx, Tx, H, V).transpose(0, 2, 1, 3)
        g = jnp.einsum('bti,oi->bto', x, Wg)
        q = _rotary(q, Tx, D)
        k = _rotary(k, Tx, D)
        gamma = 1.0 - jnp.exp2(-5.0 - jnp.arange(H, dtype=jnp.float32))
        s = jnp.log2(gamma)
        n = jnp.arange(Tx, dtype=jnp.float32)
        rel = n[:, None] - n[None, :]
        causal = rel >= 0
        decay = jnp.where(causal[None, :, :], jnp.exp2(rel[None, :, :] * s[:, None, None]), 0.0)
        scores = jnp.einsum('bhtd,bhsd->bhts', q, k) * D ** (-0.5)
        scores = scores * decay[None]
        o = jnp.einsum('bhts,bhsv->bhtv', scores, v)
        o = o.transpose(0, 2, 1, 3)
        mean = jnp.mean(o, axis=-1, keepdims=True)
        var = jnp.var(o, axis=-1, keepdims=True)
        o = (o - mean) * jax.lax.rsqrt(var + EPS)
        o = o * gn_weight.reshape(H, V) + gn_bias.reshape(H, V)
        o = o.reshape(Bx, Tx, H * V)
        o = o * jax.nn.silu(g)
        return jnp.einsum('btc,oc->bto', o, Wo)

    def _L0_ffn_ref(x, positions, theta, gamma1, gamma2, q_w, q_b, k_w, k_b, v_w, v_b, o_w, o_b, router_w, router_b, sh_w1, sh_b1, sh_w2, sh_b2, re_w1, re_b1, re_w2, re_b2):
        import jax, jax.numpy as jnp
        import numpy as np
        B, S, D = (2, 128, 128)
        H, HD = (16, 64)
        E_R = 31
        K_ACT = 3
        INTER = 128
        EPS = 1e-05
        BASE = 10000.0

        def _rmsnorm(x, gamma):
            rms = jnp.sqrt(jnp.mean(x * x, axis=-1, keepdims=True) + EPS)
            return x / rms * gamma

        def _rope(x, theta):
            seq = x.shape[2]
            angles = jnp.arange(seq, dtype=theta.dtype)[:, None] * theta
            cos = jnp.cos(angles)[None, None]
            sin = jnp.sin(angles)[None, None]
            x1, x2 = (x[..., 0::2], x[..., 1::2])
            return jnp.concatenate([x1 * cos - x2 * sin, x1 * sin + x2 * cos], axis=-1)

        def _forward(x, theta, gamma1, gamma2, q_w, q_b, k_w, k_b, v_w, v_b, o_w, o_b, router_w, router_b, sh_w1, sh_b1, sh_w2, sh_b2, re_w1, re_b1, re_w2, re_b2):
            b, s, d = x.shape
            xn = _rmsnorm(x, gamma1)
            q = (xn @ q_w + q_b).reshape(b, s, H, HD).transpose(0, 2, 1, 3)
            k = (xn @ k_w + k_b).reshape(b, s, H, HD).transpose(0, 2, 1, 3)
            v = (xn @ v_w + v_b).reshape(b, s, H, HD).transpose(0, 2, 1, 3)
            q = _rope(q, theta)
            k = _rope(k, theta)
            scale = 1.0 / np.sqrt(HD)
            scores = jnp.einsum('bhqd,bhkd->bhqk', q, k) * scale
            causal = jnp.tril(jnp.ones((s, s), dtype=bool))
            scores = jnp.where(causal, scores, -jnp.inf)
            attn = jax.nn.softmax(scores, axis=-1)
            ctx = jnp.einsum('bhqk,bhkd->bhqd', attn, v)
            ctx = ctx.transpose(0, 2, 1, 3).reshape(b, s, H * HD)
            attn_out = ctx @ o_w + o_b + xn
            an = _rmsnorm(attn_out, gamma2)
            shared = jax.nn.gelu(an @ sh_w1 + sh_b1, approximate=False) @ sh_w2 + sh_b2
            logits = an @ router_w + router_b
            aff = jax.nn.softmax(logits, axis=-1)
            topv, topi = jax.lax.top_k(aff, K_ACT)
            gates = jnp.sum(jax.nn.one_hot(topi, E_R, dtype=aff.dtype) * topv[..., None], axis=-2)
            h = jax.nn.gelu(jnp.einsum('bsd,edh->besh', an, re_w1) + re_b1[None, :, None, :], approximate=False)
            routed = jnp.einsum('bse,besh,ehd->bsd', gates, h, re_w2) + jnp.einsum('bse,ed->bsd', gates, re_b2)
            return shared + routed + an + attn_out
        del positions
        return _forward(x, theta, gamma1, gamma2, q_w, q_b, k_w, k_b, v_w, v_b, o_w, o_b, router_w, router_b, sh_w1, sh_b1, sh_w2, sh_b2, re_w1, re_b1, re_w2, re_b2)
    x = L0_attn_x
    x = x + 0.5 * _L0_ffn_ref(_layernorm(x, axis=-1), L0_ffn_positions, L0_ffn_theta, L0_ffn_gamma1, L0_ffn_gamma2, L0_ffn_q_w, L0_ffn_q_b, L0_ffn_k_w, L0_ffn_k_b, L0_ffn_v_w, L0_ffn_v_b, L0_ffn_o_w, L0_ffn_o_b, L0_ffn_router_w, L0_ffn_router_b, L0_ffn_sh_w1, L0_ffn_sh_b1, L0_ffn_sh_w2, L0_ffn_sh_b2, L0_ffn_re_w1, L0_ffn_re_b1, L0_ffn_re_w2, L0_ffn_re_b2)
    x = x + _L0_attn_ref(_layernorm(x, axis=-1), L0_attn_Wq, L0_attn_Wk, L0_attn_Wv, L0_attn_Wg, L0_attn_Wo, L0_attn_gn_weight, L0_attn_gn_bias)
    x = x + 0.5 * _L0_ffn_ref(_layernorm(x, axis=-1), L0_ffn_positions, L0_ffn_theta, L0_ffn_gamma1, L0_ffn_gamma2, L0_ffn_q_w, L0_ffn_q_b, L0_ffn_k_w, L0_ffn_k_b, L0_ffn_v_w, L0_ffn_v_b, L0_ffn_o_w, L0_ffn_o_b, L0_ffn_router_w, L0_ffn_router_b, L0_ffn_sh_w1, L0_ffn_sh_b1, L0_ffn_sh_w2, L0_ffn_sh_b2, L0_ffn_re_w1, L0_ffn_re_b1, L0_ffn_re_w2, L0_ffn_re_b2)
    return x

_drawn_inputs = setup_inputs


def setup_inputs(seed=0):
    import zlib

    import numpy as np

    out = dict(_drawn_inputs(seed))
    spreads = {'L0_attn_gn_weight': (1.0, 0.6),
     'L0_attn_gn_bias': (0.0, 2.0),
     'L0_ffn_gamma1': (1.0, 0.2),
     'L0_ffn_gamma2': (1.0, 0.2),
     'L0_ffn_q_b': (0.0, 0.8),
     'L0_ffn_k_b': (0.0, 0.8),
     'L0_ffn_v_b': (0.0, 0.1),
     'L0_ffn_o_b': (0.0, 0.1),
     'L0_ffn_router_b': (0.0, 0.8),
     'L0_ffn_sh_b1': (0.0, 0.8),
     'L0_ffn_sh_b2': (0.0, 0.1),
     'L0_ffn_re_b1': (0.0, 0.8),
     'L0_ffn_re_b2': (0.0, 0.8)}
    factors = {'L0_ffn_theta': 8.0,
     'L0_ffn_q_w': 8.0,
     'L0_ffn_k_w': 8.0,
     'L0_ffn_v_w': 2.929,
     'L0_ffn_router_w': 8.0,
     'L0_ffn_sh_w1': 5.009,
     'L0_ffn_sh_w2': 4.631,
     'L0_ffn_re_w1': 8.0,
     'L0_ffn_re_w2': 8.0}
    for name, (base, spread) in spreads.items():
        noise = np.random.default_rng([zlib.crc32(name.encode()), seed]).standard_normal(out[name].shape)
        drawn = base * np.exp(spread * noise) if base else spread * noise
        out[name] = jnp.asarray(drawn.astype(out[name].dtype))
    for name, factor in factors.items():
        out[name] = (out[name] * factor).astype(out[name].dtype)
    return out
```

```python
from contextlib import ExitStack

import concourse.bass as bass
import numpy as np
from concourse import mybir
from concourse.alu_op_type import AluOpType as ALU

F32 = mybir.dt.float32
F32R = mybir.dt.float32r
BF16 = mybir.dt.bfloat16
ACT = mybir.ActivationFunctionType
AX_X = mybir.AxisListType.X

P = 128
SEQ = 256
NTOK = 16 * SEQ
CB = 2
T = CB * SEQ
TT = T // P
NCHUNK = NTOK // T
HD = 64
HEADS = 16
HP = HEADS // 2
RHEADS = 8
RHP = RHEADS // 2
FEAT = HEADS * HD
RFEAT = RHEADS * HD
EXPERTS = 31
SLOT = 32
TOPK = 3
AW = 40
EPS = 1e-5
SC = SEQ + P
RLAG = 3
LAG = 3
NPB = LAG + 1
CALLS = 3
FFN0, RET, FFN1 = range(CALLS)


class Signal:

    def __init__(self, sem, per_layer):
        self.sem, self.per_layer = sem, per_layer
        self.per_chunk = sum(per_layer)

    def at(self, i, layer, n):
        return i * self.per_chunk + (sum(self.per_layer[:layer]) + n)


LOADED = {
    "ow": (P, HP * P), "rwo": (P, RHEADS * P), "shw2": (P, P), "rew2": (P, EXPERTS * P),
    "decay": (P, RHEADS * SEQ), "rcos": (P, SEQ), "rsin": (P, SEQ),
    "identf": (P, P), "g1row": (P, P), "g2row": (P, P), "obrow": (P, P),
    "cols": (P, 100),
}
IN_BF16 = {"identb": (P, P), "maskneg": (P, P), "sel": (3 * SLOT, SLOT)}
SPLIT = {
    "wq": FEAT, "wk": FEAT, "wv": FEAT, "router": P, "shw1": P,
    "rwq": RFEAT, "rwk": RFEAT, "rwv": FEAT, "rwg": FEAT, "rew1": EXPERTS * P,
}
COL = {}
_at = 0
for _n, _w in (("g1", 1), ("g2", 1), ("qb", HP), ("qbs", HP), ("kb", HP), ("kbs", HP), ("vb", HP),
               ("shb1", 1), ("shb2", 1), ("reb1", EXPERTS), ("gnw", RHEADS), ("gnb", RHEADS),
               ("rb", 1), ("theta", 1), ("sign", 1)):
    COL[_n] = (_at, _w)
    _at += _w
COLS = _at

TWO_PI_1 = 6.28125
TWO_PI_2 = float(np.float32(np.round((2 * np.pi - TWO_PI_1) * 2**21) / 2**21))
TWO_PI_3 = float(np.float32(2 * np.pi - TWO_PI_1 - TWO_PI_2))
MAGIC = 12582912.0
PI_IN = 3.1415925


def build(nc, x_in, ins, out):
    ctx = ExitStack()
    with ctx:
        def sb(name, shape, dt=F32):
            return ctx.enter_context(nc.sbuf_tensor(name, list(shape), dt))

        def sem(name):
            return ctx.enter_context(nc.semaphore(name))

        def signal(name, ffn=0, ret=0):
            return Signal(sem(name), [ffn, ret, ffn])

        W = {n: sb("c_" + n, s) for n, s in LOADED.items()}
        W.update({n: sb("c_" + n, s, BF16) for n, s in IN_BF16.items()})
        HI = {n: sb("hi_" + n, (P, c), F32R) for n, c in SPLIT.items()}
        LO = {n: sb("lo_" + n, (P, c), F32R) for n, c in SPLIT.items()}
        cosT, sinT = sb("cosT", (P, SEQ)), sb("sinT", (P, SEQ))
        b2p = [sb(f"b2p{j}", (3 * SLOT, P), BF16) for j in range(3)]
        half_neg = sb("half_neg", (P, TT))
        shb2h = sb("shb2h", (P, 1))
        qbh = sb("qbh", (P, 2 * HP))

        def col(name, k=0):
            a = COL[name][0] + k
            return W["cols"][:, a:a + 1]

        xin = sb("xin", (P, TT, P))
        x = sb("x", (P, TT, P))
        actH, actL = sb("actH", (P, T), F32R), sb("actL", (P, T), F32R)
        V = sb("V", (P, TT, FEAT))
        C = sb("C", (P, HP, T))
        G = sb("G", (P, NPB * 2 * SC))
        E_ = sb("E", (P, 8 * T))
        N_ = sb("N", (P, 4 * T))
        pos, b2x = N_[:, 5 * SEQ:6 * SEQ], N_[0:3 * SLOT, 6 * SEQ:6 * SEQ + P]
        PT = sb("PT", (P, 2, 2, SC))
        stat = sb("stat", (P, TT, 6))
        mv = sb("mv", (P, TT, 2))
        wv_, rs = sb("wv", (P, TT)), sb("rs", (P, TT))
        negm = sb("negm", (P, 2, 2, 2))
        rsum = sb("rsum", (P, NPB, 2, 2))
        rinv = sb("rinv", (P, NPB, 2, 2))
        rstat = sb("rstat", (P, 2, 4, 6))
        rmv = sb("rmv", (P, 2, 4, 2))
        rw_, rrs = sb("rw", (P, 2, 4)), sb("rrs", (P, 2, 4))
        rnm, rnb = sb("rnm", (P, 2, 4)), sb("rnb", (P, 2, 4))
        aff = sb("aff", (P, TT, AW))
        rest = sb("rest", (P, TT, AW))
        top = sb("top", (P, TT, 8))
        lmx, lsum, linv = sb("lmx", (P, TT)), sb("lsum", (P, TT)), sb("linv", (P, TT))
        g3 = sb("g3", (P, TT, 3 * SLOT), BF16)
        gT = sb("gT", (3 * SLOT, T), BF16)

        prob = G[:, :].rearrange("p (u h s) -> p u h s", u=NPB, h=2)
        qT = [E_[:, k * T:(k + 1) * T] for k in (0, 1)]
        kT = [E_[:, k * T:(k + 1) * T] for k in (2, 3)]
        rc = [E_[:, k * T:(k + 1) * T] for k in (4, 5)]
        rsw = [E_[:, k * T:(k + 1) * T] for k in (6, 7)]
        hsb = [E_[:, k * T:(k + 1) * T] for k in (0, 1, 2)]
        hg = [E_[:, k * T:(k + 1) * T] for k in (3, 4)]
        yT = E_[:, 5 * T:6 * T]
        lgT = E_[0:SLOT, 6 * T:7 * T]
        small = E_[:, 7 * T:8 * T]
        lg = small[:, 0:TT * EXPERTS].rearrange("p (t e) -> p t e", t=TT)
        ex = small[:, P:P + TT * EXPERTS].rearrange("p (t e) -> p t e", t=TT)
        gate = small[:, 2 * P:3 * P].rearrange("p (t e) -> p t e", t=TT)
        gres = small[:, 3 * P:4 * P].rearrange("p (t e) -> p t e", t=TT)
        tiles = lambda k: N_[:, k * T:(k + 1) * T].rearrange("p (t d) -> p t d", t=TT)
        xnb, ao, res, z = tiles(0), tiles(1), tiles(2), tiles(3)
        xout = tiles(1)
        onrm = [N_[:, k * T:(k + 1) * T].rearrange("p (h q v) -> p h q v", h=2, q=2) for k in (0, 1)]
        og_in = [N_[:, k * T:(k + 1) * T].rearrange("p (h s) -> p h s", h=2) for k in (2, 3)]

        BK = [ctx.enter_context(nc.psum_tensor(f"bank{j}", [P, 512], F32)) for j in range(2)]
        SP2 = ctx.enter_context(nc.psum_tensor("scores", [P, 4, 512], F32))
        BL = [ctx.enter_context(nc.psum_tensor(f"bank{j}", [P, 512], F32)) for j in (6, 7)]
        proj_ps, ctx_ps = BK
        S = [SP2[:, 0:2, :], SP2[:, 2:4, :]]
        four = [SP2[:, j, :] for j in range(4)]
        pt_ps = BL

        s_w = {n: sem("s_ld_" + n) for n in ("const", "attn", "expert", "ret")}
        s_stage = [sem(f"s_stage{j}") for j in range(3)]
        s_hi = sem("s_hi")
        s_lo = sem("s_lo")
        s_prep = sem("s_prep")
        s_angle = sem("s_angle")
        s_sin = sem("s_sin")
        s_ready = sem("s_ready")
        s_pool0 = sem("s_pool0")
        s_taken, s_taken_pe, s_taken_pool = sem("s_taken"), sem("s_taken_pe"), sem("s_taken_pool")
        s_xin = sem("s_xin")
        s_out = sem("s_out")

        n_stat = Signal(sem("n_stat"), [2 * TT, 2 * TT, 2 * TT])
        n_var = Signal(sem("n_var"), [2, 1, 2])
        n_rs = Signal(sem("n_rs"), [2, 1, 2])
        n_z = Signal(sem("n_z"), [2 * TT, TT, 2 * TT])
        n_zT = Signal(sem("n_zT"), [2, 1, 2])
        n_hi = Signal(sem("n_hi"), [2, 1, 2])
        n_lo = Signal(sem("n_lo"), [2, 1, 2])
        x_new = Signal(sem("x_new"), [1, 1, 1])
        xn_step = signal("xn_step", 1)
        xn_ready = signal("xn_ready", 1)
        ao_ready = signal("ao_ready", 1)
        ss_ready = signal("ss_ready", 1)
        res_step = signal("res_step", 3)
        res_ready = signal("res_ready", 1)
        v_acc, v_out = signal("v_acc", 2 * TT, 4 * TT), signal("v_out", 2 * TT, 4 * TT)
        qk_acc = signal("qk_acc", 2 * HP, 2 * RHP)
        qk_read = signal("qk_read", 2 * HP, 2 * RHP)
        qk_mul = signal("qk_mul", 2 * HP, 2 * RHP)
        qk_rot = signal("qk_rot", 2 * HP, 2 * RHP)
        s_acc = signal("s_acc", 2 * HP, 2 * RHP)
        mx = signal("mx", 2 * HP)
        p_exp = signal("p_exp", 2 * HP)
        p_inv = signal("p_inv", 2 * HP)
        p_norm = signal("p_norm", 2 * HP)
        pt0, pt1 = signal("pt0", 2 * HP), signal("pt1", 2 * HP)
        pt0_out, pt1_out = signal("pt0_out", 2 * HP), signal("pt1_out", 2 * HP)
        c_acc, c_out = signal("c_acc", 2 * HP), signal("c_out", 2 * HP)
        o_acc = signal("o_acc", 1, 1)
        lg_acc, lg_out = signal("lg_acc", 1), signal("lg_out", 1)
        lg_tm = signal("lg_tm", 1)
        rt_step = signal("rt_step", 17)
        lg_sub, lg_exp = signal("lg_sub", 1), signal("lg_exp", 1)
        g_ready, gT_acc, gT_out = signal("g_ready", 1), signal("gT_acc", 1), signal("gT_out", 1)
        h_acc, h_out = signal("h_acc", EXPERTS + 1), signal("h_out", EXPERTS + 1)
        gb_acc, hg_out = signal("gb_acc", EXPERTS), signal("hg_out", EXPERTS)
        y_acc, y_out, yt_acc = signal("y_acc", 1), signal("y_out", 1), signal("yt_acc", 1)
        a_out = signal("a_out", 0, 2 * RHP)
        ro_acc = signal("ro_acc", 0, 2 * RHP)
        ro_stat = signal("ro_stat", 0, 16 * RHP)
        ro_var, ro_rs = signal("ro_var", 0, 2 * RHP), signal("ro_rs", 0, 4 * RHP)
        on_out = signal("on_out", 0, 2 * RHP)
        ot_acc, ot_out = signal("ot_acc", 0, 2 * RHP), signal("ot_out", 0, 2 * RHP)
        og_out = signal("og_out", 0, 2 * RHP)

        reduced = [N_[:, 0:SEQ], N_[:, SEQ:2 * SEQ]]
        ang, turn, part = N_[:, 2 * SEQ:3 * SEQ], N_[:, 3 * SEQ:4 * SEQ], N_[:, 4 * SEQ:5 * SEQ]

        mask_in, sel_in = E_[:, 0:P], E_[0:3 * SLOT, P:P + SLOT]
        room = [V[:, :, :].rearrange("p t f -> p (t f)"), C[:, :, :].rearrange("p h t -> p (h t)")]

        x_v = x_in.rearrange("(c t p) d -> c p t d", t=TT, p=P)
        out_v = out.rearrange("(c t p) d -> c p t d", t=TT, p=P)

        block = ctx.enter_context(nc.Block())

        place = {"wq": (0, 0), "wk": (0, FEAT), "wv": (0, 2 * FEAT), "router": (0, 3 * FEAT),
                 "shw1": (0, 3 * FEAT + P), "rwq": (1, 0), "rwk": (1, RFEAT), "rwv": (1, 2 * RFEAT),
                 "rwg": (1, 2 * RFEAT + FEAT), "rew1": (0, 0)}
        order = list(SPLIT)
        raw = {n: room[r][:, o:o + SPLIT[n]] for n, (r, o) in place.items()}
        N_CONST = len(LOADED) + 4

        @block.sync
        def _(sp):
            for n in order[:3]:
                sp.dma_start(raw[n], ins[n]).then_inc(s_stage[0], 16)
            sp.dma_start(W["cols"][:, :], ins["cols"]).then_inc(s_w["const"], 16)
            sp.dma_start(pos, ins["pos"]).then_inc(s_w["const"], 16)
            sp.dma_start(b2x, ins["b2x"]).then_inc(s_w["const"], 16)
            sp.dma_start(mask_in, ins["maskneg"]).then_inc(s_w["const"], 16)
            sp.dma_start(sel_in, ins["sel"]).then_inc(s_w["const"], 16)
            for n in ("identf", "g1row", "g2row", "obrow", "rcos", "rsin",
                      "ow", "shw2"):
                sp.dma_start(W[n][:, :], ins[n]).then_inc(s_w["const"], 16)
            for n in order[3:9]:
                sp.dma_start(raw[n], ins[n]).then_inc(s_stage[1], 16)
            for n in ("decay", "rwo", "rew2"):
                sp.dma_start(W[n][:, :], ins[n]).then_inc(s_w["const"], 16)
            sp.wait_ge(s_lo, 5)
            sp.dma_start(raw["rew1"], ins["rew1"]).then_inc(s_stage[2], 16)
            sp.sem_inc(s_out, 16)
            sp.dma_start(xin[:, :, :], x_v[0]).then_inc(s_xin, 16)
            with sp.Fori(0, NCHUNK - 1) as i:
                sp.wait_ge(res_ready.sem, res_ready.at(i, FFN0, 1))
                sp.dma_start(xin[:, :, :], x_v[i + 1]).then_inc(s_xin, 16)
                sp.wait_ge(x_new.sem, x_new.at(i, FFN1, 1))
                sp.dma_start(out_v[i], xout).then_inc(s_out, 16)
            sp.wait_ge(x_new.sem, x_new.at(NCHUNK - 1, FFN1, 1))
            sp.dma_start(out_v[NCHUNK - 1], xout).then_inc(s_out, 16)
            sp.wait_ge(s_out, 16 * (NCHUNK + 1))

        @block.gpsimd
        def _(pool):
            pool.memset(half_neg[:, :], -0.5).then_inc(s_pool0, 1)
            pool.memset(g3[:, :, :], 0.0).then_inc(s_pool0, 1)
            pool.memset(aff[:, :, :], -1.0).then_inc(s_pool0, 1)
            pool.wait_ge(s_w["const"], 16 * N_CONST)
            pool.wait_ge(s_pool0, 3)

            def row(name):
                r = W[name]
                return r[:, :].unsqueeze(1).broadcast_to((P, TT, P))

            def rsqrt(i, layer, n):
                pool.wait_ge(n_var.sem, n_var.at(i, layer, n + 1))
                pool.tensor_tensor(rs[:, :], wv_[:, :], half_neg[:, :], ALU.pow).then_inc(n_rs.sem, 1)

            def rotated(i, layer, j, hps):
                hp = j // 2
                dst = (qT, kT)[j % 2][hp % 2]
                pool.wait_ge(qk_mul.sem, qk_mul.at(i, layer, j + 1))
                if hp >= 2:
                    pool.wait_ge(s_acc.sem, s_acc.at(i, layer, 2 * (hp - 1)))
                pool.tensor_tensor(dst, rc[j % 2], rsw[j % 2], ALU.add).then_inc(qk_rot.sem, 1)

            def ffn(i, layer, src):
                rsqrt(i, layer, 0)
                pool.wait_ge(n_z.sem, n_z.at(i, layer, TT))
                pool.tensor_tensor(xnb, z, row("g1row"), ALU.mult).then_inc(xn_step.sem, 1)
                pool.wait_ge(xn_step.sem, xn_step.at(i, layer, 1))
                pool.tensor_tensor(xnb, xnb, row("obrow"), ALU.add).then_inc(xn_ready.sem, 1)
                rotated(i, layer, 0, HP)
                rotated(i, layer, 1, HP)
                for u in range(2 * HP + 1):
                    if u + 2 < 2 * HP:
                        rotated(i, layer, u + 2, HP)
                    if u >= 1:
                        n = u - 1
                        pool.wait_ge(p_inv.sem, p_inv.at(i, layer, n + 1))
                        pool.sem_inc(s_taken_pool, 1)
                        for h in range(2):
                            for q, (a, b) in enumerate(((0, P), (P, SC))):
                                w = prob[:, n % NPB, h, a:b]
                                last = pool.tensor_scalar(w, w, rinv[:, n % NPB, q, h:h + 1], 1.0, ALU.mult, ALU.mult)
                        last.then_inc(p_norm.sem, 1)
                rsqrt(i, layer, 1)
                pool.wait_ge(n_z.sem, n_z.at(i, layer, 2 * TT))
                pool.tensor_tensor(res, z, row("g2row"), ALU.mult).then_inc(res_step.sem, 1)
                pool.wait_ge(res_step.sem, res_step.at(i, layer, 1))
                pool.tensor_tensor(res, res, ao, ALU.add).then_inc(res_step.sem, 1)
                pool.wait_ge(res_step.sem, res_step.at(i, layer, 2))
                pool.sem_inc(s_taken_pool, 1)
                pool.tensor_scalar(res, res, 0.5, 1.0, ALU.mult, ALU.mult).then_inc(res_step.sem, 1)
                pool.wait_ge(res_step.sem, res_step.at(i, layer, 3))
                pool.tensor_tensor(res, res, src[:, :, :], ALU.add).then_inc(res_ready.sem, 1)

            def retention(i):
                rsqrt(i, RET, 0)
                rotated(i, RET, 0, RHP)
                rotated(i, RET, 1, RHP)
                for u in range(2 * RHP + RLAG):
                    if u + 2 < 2 * RHP:
                        rotated(i, RET, u + 2, RHP)
                    if 1 <= u <= 2 * RHP:
                        n = u - 1
                        pool.wait_ge(ro_var.sem, ro_var.at(i, RET, n + 1))
                        pool.tensor_tensor(rrs[:, n % 2, :], rw_[:, n % 2, :], half_neg[:, :], ALU.pow)\
                            .then_inc(ro_rs.sem, 1)
                        pool.wait_ge(ro_rs.sem, ro_rs.at(i, RET, 2 * n + 1))
                        pool.tensor_tensor(rnb[:, n % 2, :], rnm[:, n % 2, :], rrs[:, n % 2, :], ALU.mult)\
                            .then_inc(ro_rs.sem, 1)
                    if u >= RLAG:
                        n = u - RLAG
                        hp, b = n // 2, n % 2
                        pool.wait_ge(ot_out.sem, ot_out.at(i, RET, n + 1))
                        for h in range(2):
                            c = C[:, 2 * hp + h, b * SEQ:(b + 1) * SEQ]
                            last = pool.tensor_tensor(c, og_in[n % 2][:, h, :], c, ALU.mult)
                        last.then_inc(og_out.sem, 1)

            with pool.Fori(0, NCHUNK) as i:
                ffn(i, FFN0, xin)
                retention(i)
                ffn(i, FFN1, x)

        @block.scalar
        def _(act):
            act.wait_ge(s_w["const"], 16 * N_CONST)
            for k, n in enumerate(order):
                act.wait_ge(s_stage[0 if k < 3 else 1 if k < 9 else 2], 16 * (3 if k < 3 else 6 if k < 9 else 1))
                act.activation(HI[n][:, :], raw[n], ACT.Copy, scale=HD ** -0.5 if n == "wq" else 1.0).then_inc(s_hi, 1)
                if n == "wv":
                    act.wait_ge(s_angle, 2)
                    act.activation(cosT[:, :], reduced[0], ACT.Sin).then_inc(s_sin, 1)
                    act.activation(sinT[:, :], reduced[1], ACT.Sin).then_inc(s_sin, 1)

            def values(i, layer):
                for j in range(2 * TT):
                    act.wait_ge(v_acc.sem, v_acc.at(i, layer, j + 1))
                    act.activation(V[:, j // 2, (j % 2) * 512:(j % 2 + 1) * 512], four[j % 4], ACT.Copy)\
                        .then_inc(v_out.sem, 1)

            def ffn(i, layer):
                act.wait_ge(n_zT.sem, n_zT.at(i, layer, 1))
                act.activation(actH[:, :], ctx_ps[:, :], ACT.Copy, scale=col("g1")).then_inc(n_hi.sem, 1)
                values(i, layer)
                for u in range(2 * HP + LAG):
                    n = u - LAG
                    if n >= 0:
                        act.wait_ge(pt1.sem, pt1.at(i, layer, n + 1))
                        act.activation(PT[:, n % 2, 1, :], pt_ps[1][:, 0:SC], ACT.Copy).then_inc(pt1_out.sem, 1)
                    if u < 2 * HP:
                        act.wait_ge(mx.sem, mx.at(i, layer, u + 1))
                        for h in range(2):
                            for q, (a, b) in enumerate(((0, P), (P, SC))):
                                last = act.activation(prob[:, u % NPB, h, a:b], S[u % 2][:, h, a:b], ACT.Exp,
                                                      bias=negm[:, u % 2, q, h:h + 1],
                                                      accum_out=rsum[:, u % NPB, q, h:h + 1])
                        last.then_inc(p_exp.sem, 1)
                    if n >= 0:
                        act.wait_ge(c_acc.sem, c_acc.at(i, layer, n + 1))
                        act.activation(C[:, n // 2, (n % 2) * SEQ:(n % 2 + 1) * SEQ], ctx_ps[:, 0:SEQ], ACT.Identity,
                                       bias=col("vb", n // 2)).then_inc(c_out.sem, 1)
                act.wait_ge(ao_ready.sem, ao_ready.at(i, layer, 1))
                for t in range(TT):
                    last = act.activation(z[:, t, :], ao[:, t, :], ACT.Square, accum_out=wv_[:, t:t + 1])
                last.then_inc(ss_ready.sem, 1)
                act.wait_ge(n_zT.sem, n_zT.at(i, layer, 2))
                act.activation(actH[:, :], ctx_ps[:, :], ACT.Copy, scale=col("g2")).then_inc(n_hi.sem, 1)
                act.wait_ge(lg_acc.sem, lg_acc.at(i, layer, 1))
                act.activation(lgT, proj_ps[0:SLOT, :], ACT.Identity, bias=W["cols"][0:SLOT, COL["rb"][0]:COL["rb"][0] + 1])\
                    .then_inc(lg_out.sem, 1)
                act.wait_ge(lg_sub.sem, lg_sub.at(i, layer, 1))
                act.activation(ex, lg, ACT.Exp).then_inc(lg_exp.sem, 1)
                for k in range(EXPERTS + 1):
                    act.wait_ge(h_acc.sem, h_acc.at(i, layer, k + 1))
                    if k >= 4:
                        act.wait_ge(hg_out.sem, hg_out.at(i, layer, k - 3))
                    act.activation(hsb[k % 3], four[k % 2], ACT.Gelu,
                                   bias=col("shb1") if k == 0 else col("reb1", k - 1)).then_inc(h_out.sem, 1)
                act.wait_ge(y_acc.sem, y_acc.at(i, layer, 1))
                act.activation(yT, pt_ps[0][:, :], ACT.Identity, bias=shb2h[:, 0:1], scale=0.5).then_inc(y_out.sem, 1)

            def retention(i):
                act.wait_ge(n_zT.sem, n_zT.at(i, RET, 1))
                act.activation(actH[:, :], ctx_ps[:, :], ACT.Copy).then_inc(n_hi.sem, 1)
                values(i, RET)
                for c in range(RHEADS):
                    j = 2 * TT + c
                    act.wait_ge(v_acc.sem, v_acc.at(i, RET, j + 1))
                    act.activation(C[:, c, :], four[j % 4], ACT.Silu).then_inc(v_out.sem, 1)

                for u in range(2, 2 * RHP + RLAG):
                    if u >= RLAG:
                        n = u - RLAG
                        act.wait_ge(ot_acc.sem, ot_acc.at(i, RET, n + 1))
                        if n >= 2:
                            act.wait_ge(og_out.sem, og_out.at(i, RET, n - 1))
                        for h in range(2):
                            c = 2 * (n // 2) + h
                            last = act.activation(og_in[n % 2][:, h, :], ctx_ps[:, h * SEQ:(h + 1) * SEQ], ACT.Identity,
                                                  bias=col("gnb", c), scale=col("gnw", c))
                        last.then_inc(ot_out.sem, 1)
                    if u - 2 < 2 * RHP:
                        n = u - 2
                        act.wait_ge(ro_rs.sem, ro_rs.at(i, RET, 2 * n + 2))
                        for hq in range(4):
                            last = act.activation(onrm[n % 2][:, hq // 2, hq % 2, :], pt_ps[n % 2][:, hq * P:(hq + 1) * P],
                                                  ACT.Identity, bias=rnb[:, n % 2, hq:hq + 1], scale=rrs[:, n % 2, hq:hq + 1])
                        last.then_inc(on_out.sem, 1)

            with act.Fori(0, NCHUNK) as i:
                ffn(i, FFN0)
                retention(i)
                ffn(i, FFN1)

        @block.tensor
        def _(pe):
            pe.wait_ge(s_w["const"], 16 * N_CONST)
            pe.wait_ge(s_lo, len(order))
            pe.wait_ge(s_ready, 1)

            def product(dst, wn, a, b, tok=None, low=None):
                for k, (w, y) in enumerate(((HI, actH), (LO, actH), (HI, actL))):
                    w = w[wn][:, a:b]
                    if k == 2 and low is not None:
                        pe.wait_ge(n_lo.sem, low)
                    y = y[:, :] if tok is None else y[:, tok * P:(tok + 1) * P]
                    last = pe.matmul(dst, w if tok is None else y, y if tok is None else w, start=k == 0, stop=k == 2)
                return last

            def transposed(i, layer, n):
                for t in range(TT):
                    pe.wait_ge(n_z.sem, n_z.at(i, layer, n * TT + t + 1))
                    last = pe.transpose(ctx_ps[:, t * P:(t + 1) * P], z[:, t, :], W["identf"][:, :])
                last.then_inc(n_zT.sem, 1)
                pe.wait_ge(n_hi.sem, n_hi.at(i, layer, n + 1))
                pe.wait_ge(n_lo.sem, n_lo.at(i, layer, n + 1))

            def values(i, layer, wn):
                for j in range(2 * TT):
                    if j >= 4:
                        pe.wait_ge(v_out.sem, v_out.at(i, layer, j - 3))
                    product(four[j % 4], wn, (j % 2) * 512, (j % 2 + 1) * 512, tok=j // 2).then_inc(v_acc.sem, 1)

            def project(i, layer, j, wq, wk):
                if j >= 1:
                    pe.wait_ge(qk_read.sem, qk_read.at(i, layer, j))
                hp = j // 2
                product(proj_ps[:, :], (wq, wk)[j % 2], hp * P, (hp + 1) * P).then_inc(qk_acc.sem, 1)

            def output(i, layer, w):
                for t in range(TT):
                    for c in range(HP):
                        last = pe.matmul(pt_ps[0][:, t * P:(t + 1) * P], C[:, c, t * P:(t + 1) * P],
                                         w[:, c * P:(c + 1) * P], start=c == 0, stop=c == HP - 1)
                last.then_inc(o_acc.sem, 1)

            def ffn(i, layer):
                transposed(i, layer, 0)
                project(i, layer, 0, "wq", "wk")
                values(i, layer, "wv")
                project(i, layer, 1, "wq", "wk")
                pe.wait_ge(v_out.sem, v_out.at(i, layer, 2 * TT))
                for u in range(2 * HP + LAG):
                    n = u - LAG
                    if n >= 0:
                        pe.wait_ge(p_norm.sem, p_norm.at(i, layer, n + 1))
                        for h, (acc, free) in enumerate(((pt0, pt0_out), (pt1, pt1_out))):
                            if n >= 1:
                                pe.wait_ge(free.sem, free.at(i, layer, n))
                            w = prob[:, n % NPB, h, :]
                            for dst, src in ((0, 0), (P, P), (2 * P, 2 * P)):
                                last = pe.transpose(pt_ps[h][:, dst:dst + P], w[:, src:src + P], W["identf"][:, :])
                            last.then_inc(acc.sem, 1)
                    if u + 2 < 2 * HP:
                        project(i, layer, u + 2, "wq", "wk")
                    if u < 2 * HP:
                        hp, b = u // 2, u % 2
                        pe.wait_ge(qk_rot.sem, qk_rot.at(i, layer, 2 * hp + 2))
                        if u >= 2:
                            pe.wait_ge(p_exp.sem, p_exp.at(i, layer, u - 1))
                        for h in range(2):
                            r = slice(HD * h, HD * (h + 1))
                            q, k = qT[hp % 2][r, b * SEQ:(b + 1) * SEQ], kT[hp % 2][r, b * SEQ:(b + 1) * SEQ]
                            dst = S[u % 2][:, h, :]
                            pe.matmul(dst[:, 0:P], q[:, 0:P], k[:, 0:P], start=True, stop=False)
                            pe.matmul(dst[:, 0:P], W["identb"][:, :], W["maskneg"][:, :], start=False, stop=True)
                            pe.matmul(dst[:, P:SC], q[:, P:SEQ], k, start=True, stop=False)
                            last = pe.matmul(dst[:, 2 * P:SC], W["identb"][:, :], W["maskneg"][:, :], start=False, stop=True)
                        last.then_inc(s_acc.sem, 1)
                    if n >= 0:
                        hp, b = n // 2, n % 2
                        pe.wait_ge(pt0_out.sem, pt0_out.at(i, layer, n + 1))
                        pe.wait_ge(pt1_out.sem, pt1_out.at(i, layer, n + 1))
                        if n >= 1:
                            pe.wait_ge(c_out.sem, c_out.at(i, layer, n))
                        for h in range(2):
                            dst = ctx_ps[HD * h:HD * (h + 1), :]
                            f = slice((2 * hp + h) * HD, (2 * hp + h + 1) * HD)
                            w = PT[:, n % 2, h, :]
                            pe.matmul(dst[:, 0:SEQ], V[:, 2 * b, f], w[:, 0:SEQ], start=True, stop=False)
                            last = pe.matmul(dst[:, P:SEQ], V[:, 2 * b + 1, f], w[:, SEQ:SC], start=False, stop=True)
                        last.then_inc(c_acc.sem, 1)
                pe.wait_ge(c_out.sem, c_out.at(i, layer, 2 * HP))
                output(i, layer, W["ow"])
                transposed(i, layer, 1)
                product(proj_ps[:, :], "router", 0, P).then_inc(lg_acc.sem, 1)

                def expert_in(k):
                    if k >= 2:
                        pe.wait_ge(h_out.sem, h_out.at(i, layer, k - 1))
                    if k == 0:
                        last = product(four[0], "shw1", 0, P)
                    else:
                        last = product(four[k % 2], "rew1", (k - 1) * P, k * P)
                    last.then_inc(h_acc.sem, 1)

                def spread(k):
                    if k >= 3:
                        pe.wait_ge(hg_out.sem, hg_out.at(i, layer, k - 2))
                    pe.matmul(four[2 + k % 2], W["sel"][:, k - 1:k].broadcast_to((3 * SLOT, P)), gT[:, :],
                              start=True, stop=True).then_inc(gb_acc.sem, 1)

                def expert_out(k):
                    if k == 0:
                        pe.wait_ge(h_out.sem, h_out.at(i, layer, 1))
                        pe.matmul(pt_ps[0][:, :], W["shw2"][:, :], hsb[0], start=True, stop=False)
                    else:
                        pe.wait_ge(hg_out.sem, hg_out.at(i, layer, k))
                        pe.matmul(pt_ps[0][:, :], W["rew2"][:, (k - 1) * P:k * P], hg[k % 2], start=False, stop=False)

                expert_in(0)
                expert_in(1)
                pe.wait_ge(lg_out.sem, lg_out.at(i, layer, 1))
                pe.sem_inc(s_taken_pe, 1)
                for t in range(TT):
                    last = pe.transpose(ctx_ps[:, t * SLOT:(t + 1) * SLOT], lgT[:, t * P:(t + 1) * P],
                                        W["identf"][0:SLOT, 0:SLOT])
                last.then_inc(lg_tm.sem, 1)
                expert_out(0)
                pe.wait_ge(g_ready.sem, g_ready.at(i, layer, 1))
                for t in range(TT):
                    last = pe.transpose(pt_ps[1].bitcast(BF16)[0:3 * SLOT, t * P:(t + 1) * P], g3[:, t, :], W["identb"][:, :])
                last.then_inc(gT_acc.sem, 1)
                pe.wait_ge(gT_out.sem, gT_out.at(i, layer, 1))
                spread(1)
                for k in range(1, EXPERTS + 1):
                    if k + 1 <= EXPERTS:
                        expert_in(k + 1)
                        spread(k + 1)
                    expert_out(k)
                for j in range(3):
                    last = pe.matmul(pt_ps[0][:, :], b2p[j][:, :], gT[:, :], start=False, stop=j == 2)
                last.then_inc(y_acc.sem, 1)
                pe.wait_ge(y_out.sem, y_out.at(i, layer, 1))
                for t in range(TT):
                    last = pe.transpose(pt_ps[1][:, t * P:(t + 1) * P], yT[:, t * P:(t + 1) * P], W["identf"][:, :])
                last.then_inc(yt_acc.sem, 1)

            def retention(i):
                transposed(i, RET, 0)
                project(i, RET, 0, "rwq", "rwk")
                values(i, RET, "rwv")
                project(i, RET, 1, "rwq", "rwk")
                for c in range(RHEADS):
                    j = 2 * TT + c
                    pe.wait_ge(v_out.sem, v_out.at(i, RET, j - 3))
                    product(four[j % 4], "rwg", c * P, (c + 1) * P).then_inc(v_acc.sem, 1)
                for u in range(2 * RHP + RLAG):
                    if u >= RLAG:
                        n = u - RLAG
                        pe.wait_ge(on_out.sem, on_out.at(i, RET, n + 1))
                        if n >= 1:
                            pe.wait_ge(ot_out.sem, ot_out.at(i, RET, n))
                        for h in range(2):
                            for q in range(2):
                                a = h * SEQ + q * P
                                last = pe.transpose(ctx_ps[:, a:a + P], onrm[n % 2][:, h, q, :], W["identf"][:, :])
                        last.then_inc(ot_acc.sem, 1)
                    if u + 2 < 2 * RHP:
                        project(i, RET, u + 2, "rwq", "rwk")
                    if u == 0:
                        pe.wait_ge(v_out.sem, v_out.at(i, RET, 4 * TT))
                    if u < 2 * RHP:
                        hp, b = u // 2, u % 2
                        pe.wait_ge(qk_rot.sem, qk_rot.at(i, RET, 2 * hp + 2))
                        if u >= 2:
                            pe.wait_ge(a_out.sem, a_out.at(i, RET, u - 1))
                        for h in range(2):
                            r = slice(HD * h, HD * (h + 1))
                            q, k = qT[hp % 2][r, b * SEQ:(b + 1) * SEQ], kT[hp % 2][r, b * SEQ:(b + 1) * SEQ]
                            dst = S[u % 2][:, h, :]
                            pe.matmul(dst[:, 0:SEQ], k[:, 0:P], q, start=True, stop=True)
                            last = pe.matmul(dst[:, SEQ:SC], k[:, P:SEQ], q[:, P:SEQ], start=True, stop=True)
                        last.then_inc(s_acc.sem, 1)
                    if 1 <= u <= 2 * RHP:
                        n = u - 1
                        hp, b = n // 2, n % 2
                        pe.wait_ge(a_out.sem, a_out.at(i, RET, n + 1))
                        if n >= 2:
                            pe.wait_ge(on_out.sem, on_out.at(i, RET, n - 1))
                        for h in range(2):
                            f = slice((2 * hp + h) * P, (2 * hp + h + 1) * P)
                            w = PT[:, n % 2, h, :]
                            d = pt_ps[n % 2]
                            a = h * SEQ
                            pe.matmul(d[:, a:a + P], w[:, 0:P], V[:, 2 * b, f], start=True, stop=True)
                            pe.matmul(d[:, a + P:a + SEQ], w[:, P:SEQ], V[:, 2 * b, f], start=True, stop=False)
                            last = pe.matmul(d[:, a + P:a + SEQ], w[:, SEQ:SC], V[:, 2 * b + 1, f], start=False, stop=True)
                        last.then_inc(ro_acc.sem, 1)
                pe.wait_ge(og_out.sem, og_out.at(i, RET, 2 * RHP))
                output(i, RET, W["rwo"])

            with pe.Fori(0, NCHUNK) as i:
                ffn(i, FFN0)
                retention(i)
                ffn(i, FFN1)

        @block.vector
        def _(dve):
            count = [0]

            def link(ins):
                count[0] += 1
                ins.then_inc(s_prep, 1)
                dve.wait_ge(s_prep, count[0])

            dve.wait_ge(s_w["const"], 16 * N_CONST)
            link(dve.tensor_scalar(ang, pos, col("theta"), None, ALU.mult))
            for j, shift in ((0, 0.25), (1, 0.0)):
                link(dve.tensor_scalar(turn, ang, float(np.float32(1 / (2 * np.pi))), shift, ALU.mult, ALU.add))
                link(dve.tensor_scalar(part, turn, MAGIC, None, ALU.add))
                link(dve.tensor_scalar(turn, part, -MAGIC, None, ALU.add))
                src = ang
                for c in (TWO_PI_1, TWO_PI_2, TWO_PI_3):
                    link(dve.scalar_tensor_tensor(out=part, in0=turn, scalar=-c, in1=src, op0=ALU.mult, op1=ALU.add))
                    src = part
                if shift:
                    link(dve.tensor_scalar(part, part, float(np.float32(np.pi / 2)), None, ALU.add))
                link(dve.tensor_scalar(reduced[j], part, PI_IN, -PI_IN, ALU.min, ALU.max))
                dve.sem_inc(s_angle, 1)
            for k, n in enumerate(order):
                dve.wait_ge(s_hi, k + 1)
                dve.scalar_tensor_tensor(out=LO[n][:, :], in0=raw[n], scalar=HD ** -0.5 if n == "wq" else 1.0,
                                         in1=HI[n][:, :].bitcast(F32), op0=ALU.mult, op1=ALU.subtract).then_inc(s_lo, 1)
            for n, v in (("identb", W["identf"][:, :]), ("maskneg", mask_in), ("sel", sel_in)):
                link(dve.tensor_copy(W[n][:, :], v))
            dve.wait_ge(s_sin, 2)
            link(dve.tensor_scalar(sinT[:, :], sinT[:, :], col("sign"), None, ALU.mult))
            link(dve.tensor_scalar(shb2h[:, :], col("shb2"), 0.5, None, ALU.mult))
            a = COL["qb"][0]
            link(dve.tensor_scalar(qbh[:, :], W["cols"][:, a:a + 2 * HP], HD ** -0.5, None, ALU.mult))
            b2 = b2x
            for j in range(3):
                link(dve.tensor_copy(b2p[j][:, :], b2))
                if j < 2:
                    link(dve.tensor_tensor(b2, b2, b2p[j][:, :], ALU.subtract))
            dve.wait_ge(s_pool0, 3)
            dve.sem_inc(s_ready, 1)
            swap = [p ^ 1 for p in range(32)]

            def table(tb):
                return tb[:, :].unsqueeze(1).broadcast_to((P, CB, SEQ))

            def by_batch(ap):
                return ap.rearrange("p (b s) -> p b s", b=CB)

            def apart():
                dve.sem_inc(s_taken, 1)

            def layer_norm(i, layer, src, ffn):
                for t in range(TT):
                    dve.bn_stats(stat[:, t, :], src[:, t, :]).then_inc(n_stat.sem, 1)
                dve.wait_ge(n_stat.sem, n_stat.at(i, layer, TT))
                apart()
                for t in range(TT):
                    dve.bn_aggr(mv[:, t, :], stat[:, t, :]).then_inc(n_stat.sem, 1)
                dve.wait_ge(n_stat.sem, n_stat.at(i, layer, 2 * TT))
                mul, add = (1.0 + EPS, EPS * EPS) if ffn else (1.0, EPS)
                dve.tensor_scalar(wv_[:, :], mv[:, :, 1], mul, add, ALU.mult, ALU.add).then_inc(n_var.sem, 1)
                dve.wait_ge(n_rs.sem, n_rs.at(i, layer, 1))
                for t in range(TT):
                    dve.tensor_scalar(z[:, t, :], src[:, t, :], mv[:, t, 0:1], rs[:, t:t + 1],
                                      ALU.subtract, ALU.mult).then_inc(n_z.sem, 1)

            def low_part(i, layer, n, gamma):
                dve.wait_ge(n_hi.sem, n_hi.at(i, layer, n + 1))
                dve.scalar_tensor_tensor(out=actL[:, :], in0=ctx_ps[:, :], scalar=gamma, in1=actH[:, :].bitcast(F32),
                                         op0=ALU.mult, op1=ALU.subtract).then_inc(n_lo.sem, 1)

            def rotate(i, layer, j):
                hp = j // 2
                cos_, sin_ = (W["rcos"], W["rsin"]) if layer == RET else (cosT, sinT)
                dve.wait_ge(qk_acc.sem, qk_acc.at(i, layer, j + 1))
                if j >= 2:
                    dve.wait_ge(qk_rot.sem, qk_rot.at(i, layer, j - 1))
                if layer == RET:
                    b, bs = 0.0, 0.0
                elif j % 2 == 0:
                    b, bs = qbh[:, hp:hp + 1], qbh[:, HP + hp:HP + hp + 1]
                else:
                    b, bs = col("kb", hp), col("kbs", hp)
                dve.scalar_tensor_tensor(out=by_batch(rc[j % 2]), in0=by_batch(proj_ps[:, :]), scalar=b, in1=table(cos_),
                                         op0=ALU.add, op1=ALU.mult)
                dve.stream_shuffle(rsw[j % 2], proj_ps[:, :], swap).then_inc(qk_read.sem, 1)
                dve.wait_ge(qk_read.sem, qk_read.at(i, layer, j + 1))
                dve.scalar_tensor_tensor(out=by_batch(rsw[j % 2]), in0=by_batch(rsw[j % 2]), scalar=bs, in1=table(sin_),
                                         op0=ALU.add, op1=ALU.mult).then_inc(qk_mul.sem, 1)

            def ffn(i, layer, src, dst):
                if layer == FFN0:
                    dve.wait_ge(s_xin, i * 16 + 16)
                layer_norm(i, layer, src, True)
                low_part(i, layer, 0, col("g1"))
                rotate(i, layer, 0)
                rotate(i, layer, 1)
                for u in range(2 * HP + LAG):
                    n = u - LAG
                    if n >= 0:
                        dve.wait_ge(pt0.sem, pt0.at(i, layer, n + 1))
                        dve.tensor_copy(PT[:, n % 2, 0, :], pt_ps[0][:, 0:SC]).then_inc(pt0_out.sem, 1)
                    if u + 2 < 2 * HP:
                        rotate(i, layer, u + 2)
                    if u < 2 * HP:
                        dve.wait_ge(s_acc.sem, s_acc.at(i, layer, u + 1))
                        dve.tensor_reduce(negm[:, u % 2, 0, :], S[u % 2][:, :, 0:P], AX_X, ALU.max, negate=True)
                        dve.tensor_reduce(negm[:, u % 2, 1, :], S[u % 2][:, :, P:SC], AX_X, ALU.max, negate=True)\
                            .then_inc(mx.sem, 1)
                    if 1 <= u <= 2 * HP:
                        dve.wait_ge(p_exp.sem, p_exp.at(i, layer, u))
                        dve.reciprocal(rinv[:, (u - 1) % NPB, :, :], rsum[:, (u - 1) % NPB, :, :]).then_inc(p_inv.sem, 1)
                dve.wait_ge(o_acc.sem, o_acc.at(i, layer, 1))
                dve.wait_ge(xn_ready.sem, xn_ready.at(i, layer, 1))
                if layer == FFN0:
                    dve.wait_ge(s_out, i * 16 + 16)
                dve.tensor_tensor(ao, pt_ps[0][:, :].rearrange("p (t d) -> p t d", t=TT), xnb, ALU.add)\
                    .then_inc(ao_ready.sem, 1)
                dve.wait_ge(ss_ready.sem, ss_ready.at(i, layer, 1))
                dve.tensor_scalar(wv_[:, :], wv_[:, :], 1.0 / P, EPS, ALU.mult, ALU.add).then_inc(n_var.sem, 1)
                dve.wait_ge(n_rs.sem, n_rs.at(i, layer, 2))
                for t in range(TT):
                    dve.tensor_scalar(z[:, t, :], ao[:, t, :], rs[:, t:t + 1], None, ALU.mult).then_inc(n_z.sem, 1)
                low_part(i, layer, 1, col("g2"))

                steps = [0]

                def step(ins):
                    steps[0] += 1
                    ins.then_inc(rt_step.sem, 1)
                    dve.wait_ge(rt_step.sem, rt_step.at(i, layer, steps[0]))

                def note(ins):
                    steps[0] += 1
                    ins.then_inc(rt_step.sem, 1)

                def wide(ap):
                    return ap[:, :].unsqueeze(2).broadcast_to((P, TT, EXPERTS))

                dve.wait_ge(lg_tm.sem, lg_tm.at(i, layer, 1))
                logits = ctx_ps[:, 0:TT * SLOT].rearrange("p (t e) -> p t e", t=TT)[:, :, 0:EXPERTS]
                step(dve.tensor_reduce(lmx[:, :], logits, AX_X, ALU.max, negate=True))
                dve.tensor_tensor(lg, logits, wide(lmx), ALU.add).then_inc(lg_sub.sem, 1)
                dve.wait_ge(lg_exp.sem, lg_exp.at(i, layer, 1))
                step(dve.tensor_reduce(lsum[:, :], ex, AX_X, ALU.add))
                step(dve.reciprocal(linv[:, :], lsum[:, :]))
                step(dve.tensor_tensor(aff[:, :, 0:EXPERTS], ex, wide(linv), ALU.mult))
                apart()
                for t in range(TT):
                    note(dve.max(top[:, t, :], aff[:, t, :]))
                dve.wait_ge(rt_step.sem, rt_step.at(i, layer, steps[0]))
                step(dve.memset(top[:, :, TOPK:8], -1.0))
                apart()
                for t in range(TT):
                    note(dve.match_replace(rest[:, t, :], top[:, t, :], aff[:, t, :], 0.0))
                dve.wait_ge(rt_step.sem, rt_step.at(i, layer, steps[0]))
                step(dve.tensor_tensor(gate[:, :, 0:EXPERTS], aff[:, :, 0:EXPERTS], rest[:, :, 0:EXPERTS], ALU.subtract))
                part_ = [g3[:, :, j * SLOT:j * SLOT + EXPERTS] for j in range(3)]
                g_, r_ = gate[:, :, 0:EXPERTS], gres[:, :, 0:EXPERTS]
                step(dve.tensor_copy(part_[0], g_))
                step(dve.tensor_tensor(r_, g_, part_[0], ALU.subtract))
                step(dve.tensor_copy(part_[1], r_))
                dve.tensor_tensor(part_[2], r_, part_[1], ALU.subtract).then_inc(g_ready.sem, 1)
                assert steps[0] == rt_step.per_layer[layer], steps[0]
                dve.wait_ge(gT_acc.sem, gT_acc.at(i, layer, 1))
                dve.tensor_copy(gT[:, :], pt_ps[1].bitcast(BF16)[0:3 * SLOT, 0:T]).then_inc(gT_out.sem, 1)
                for k in range(1, EXPERTS + 1):
                    dve.wait_ge(gb_acc.sem, gb_acc.at(i, layer, k))
                    dve.wait_ge(h_out.sem, h_out.at(i, layer, k + 1))
                    dve.tensor_tensor(hg[k % 2], hsb[k % 3], four[2 + k % 2], ALU.mult).then_inc(hg_out.sem, 1)
                dve.wait_ge(yt_acc.sem, yt_acc.at(i, layer, 1))
                dve.wait_ge(res_ready.sem, res_ready.at(i, layer, 1))
                dve.tensor_tensor(dst, pt_ps[1][:, :].rearrange("p (t d) -> p t d", t=TT), res, ALU.add)\
                    .then_inc(x_new.sem, 1)
                dve.wait_ge(x_new.sem, x_new.at(i, layer, 1))

            def retention(i):
                layer_norm(i, RET, x, False)
                low_part(i, RET, 0, 1.0)
                rotate(i, RET, 0)
                rotate(i, RET, 1)
                for u in range(2 * RHP + 1):
                    if u + 2 < 2 * RHP:
                        rotate(i, RET, u + 2)
                    if u < 2 * RHP:
                        hp = u // 2
                        dve.wait_ge(s_acc.sem, s_acc.at(i, RET, u + 1))
                        dec = W["decay"][:, :].rearrange("p (h s) -> p h s", h=RHEADS)[:, 2 * hp:2 * hp + 2, :]
                        dve.tensor_tensor(PT[:, u % 2, :, 0:SEQ], S[u % 2][:, :, 0:SEQ], dec, ALU.mult)
                        dve.tensor_tensor(PT[:, u % 2, :, SEQ:SC], S[u % 2][:, :, SEQ:SC], dec[:, :, 0:P], ALU.mult)\
                            .then_inc(a_out.sem, 1)
                    if 1 <= u <= 2 * RHP:
                        n = u - 1
                        dve.wait_ge(ro_acc.sem, ro_acc.at(i, RET, n + 1))
                        for hq in range(4):
                            dve.bn_stats(rstat[:, n % 2, hq, :], pt_ps[n % 2][:, hq * P:(hq + 1) * P]).then_inc(ro_stat.sem, 1)
                        dve.wait_ge(ro_stat.sem, ro_stat.at(i, RET, 8 * n + 4))
                        apart()
                        for hq in range(4):
                            dve.bn_aggr(rmv[:, n % 2, hq, :], rstat[:, n % 2, hq, :]).then_inc(ro_stat.sem, 1)
                        dve.wait_ge(ro_stat.sem, ro_stat.at(i, RET, 8 * n + 8))
                        dve.tensor_scalar(rnm[:, n % 2, :], rmv[:, n % 2, :, 0], -1.0, None, ALU.mult)
                        dve.tensor_scalar(rw_[:, n % 2, :], rmv[:, n % 2, :, 1], 1.0, EPS, ALU.mult, ALU.add)\
                            .then_inc(ro_var.sem, 1)
                dve.wait_ge(o_acc.sem, o_acc.at(i, RET, 1))
                dve.tensor_tensor(x[:, :, :], pt_ps[0][:, :].rearrange("p (t d) -> p t d", t=TT), x[:, :, :], ALU.add)\
                    .then_inc(x_new.sem, 1)
                dve.wait_ge(x_new.sem, x_new.at(i, RET, 1))

            with dve.Fori(0, NCHUNK) as i:
                ffn(i, FFN0, xin, x[:, :, :])
                retention(i)
                ffn(i, FFN1, x, xout)


def shape_constants():
    f = np.float32
    c = {"identf": np.eye(P, dtype=f), }
    rows = np.arange(P)
    c["maskneg"] = np.where(rows[None, :] > rows[:, None], -1e30, 0.0).astype(f)
    sel = np.zeros((3 * SLOT, SLOT), f)
    for j in range(3):
        sel[j * SLOT + np.arange(EXPERTS), np.arange(EXPERTS)] = 1
    c["sel"] = sel
    c["pos"] = np.broadcast_to(np.arange(SEQ, dtype=f), (P, SEQ)).copy()
    gamma = f(1) - np.exp2(f(-5) - np.arange(RHEADS, dtype=f))
    s = np.log2(gamma).astype(f)
    rel = (np.arange(SEQ, dtype=f)[None, :] - rows[:, None].astype(f))
    d = np.where(rel[:, None, :] >= 0, np.exp2(rel[:, None, :] * s[None, :, None]), f(0)) * f(HD ** -0.5)
    c["decay"] = d.astype(f).reshape(P, RHEADS * SEQ)
    inv = (f(1) / np.power(f(10000), np.arange(0, HD, 2, dtype=f) / f(HD))).astype(f)
    ang = (np.arange(SEQ, dtype=f)[None, :] * inv[:, None]).astype(f)
    sign = np.where(rows % 2 == 0, -1, 1).astype(f)
    pair = (rows % HD) // 2
    c["rcos"] = np.cos(ang)[pair].astype(f)
    c["rsin"] = (np.sin(ang)[pair] * sign[:, None]).astype(f)
    return c, sign


def kernel(**inputs):
    import concourse.bacc as bacc
    from concourse.bass_utils import run_bass_kernel_spmd

    a = {k.replace("L0_ffn_", "f_").replace("L0_attn_", "r_"): np.asarray(v) for k, v in inputs.items()}
    arrays, sign = shape_constants()
    pairs = lambda v: v.reshape(-1, P).T
    by_pair = lambda w: w.reshape(-1, P, P).transpose(1, 0, 2).reshape(P, -1)
    swap = np.arange(P) ^ 1
    arrays["wq"], arrays["wk"], arrays["wv"] = a["f_q_w"], a["f_k_w"], a["f_v_w"]
    router = np.zeros((P, P), np.float32)
    router[:, :EXPERTS] = a["f_router_w"]
    arrays["router"] = router
    arrays["shw1"], arrays["shw2"] = a["f_sh_w1"], a["f_sh_w2"]
    arrays["rew1"] = a["f_re_w1"].transpose(1, 0, 2).reshape(P, -1)
    arrays["rew2"] = a["f_re_w2"].transpose(1, 0, 2).reshape(P, -1)
    arrays["ow"] = by_pair(a["f_o_w"])
    mix = np.arange(RFEAT).reshape(RHEADS, 2, HD // 2).transpose(0, 2, 1).reshape(-1)
    arrays["rwq"], arrays["rwk"] = a["r_Wq"][mix].T, a["r_Wk"][mix].T
    arrays["rwv"], arrays["rwg"] = a["r_Wv"].T, a["r_Wg"].T
    arrays["rwo"] = by_pair(a["r_Wo"].T)
    for name, key in (("g1row", "f_gamma1"), ("g2row", "f_gamma2"), ("obrow", "f_o_b")):
        arrays[name] = np.broadcast_to(a[key][None, :], (P, P))
    b2x = np.zeros((3, SLOT, P), np.float32)
    b2x[:, :EXPERTS] = a["f_re_b2"][None]
    arrays["b2x"] = b2x.reshape(3 * SLOT, P)
    rb = np.zeros((P, 1), np.float32)
    rb[:EXPERTS, 0] = a["f_router_b"]
    vec = {"g1": a["f_gamma1"][:, None], "g2": a["f_gamma2"][:, None],
           "qb": pairs(a["f_q_b"]), "qbs": pairs(a["f_q_b"])[swap], "kb": pairs(a["f_k_b"]),
           "kbs": pairs(a["f_k_b"])[swap], "vb": pairs(a["f_v_b"]), "shb1": a["f_sh_b1"][:, None],
           "shb2": a["f_sh_b2"][:, None], "reb1": a["f_re_b1"].T, "gnw": pairs(a["r_gn_weight"]),
           "gnb": pairs(a["r_gn_bias"]), "rb": rb, "theta": a["f_theta"][(np.arange(P) % HD) // 2][:, None],
           "sign": sign[:, None]}
    cols = np.zeros((P, LOADED["cols"][1]), np.float32)
    for n, (at, w) in COL.items():
        cols[:, at:at + w] = vec[n]
    arrays["cols"] = cols

    nc = bacc.Bacc("TRN2", target_bir_lowering=False, num_devices=1)
    feeds, ins = {}, {}
    arrays["x"] = a["r_x"].reshape(NTOK, P)
    for n, v in arrays.items():
        v = np.ascontiguousarray(v)
        feeds["in_" + n] = v
        ins[n] = nc.dram_tensor("in_" + n, v.shape, mybir.dt.from_np(v.dtype), kind="ExternalInput").ap()
    out = nc.dram_tensor("out_x", (NTOK, P), F32, kind="ExternalOutput").ap()
    build(nc, ins["x"], ins, out)
    r = run_bass_kernel_spmd(nc, [feeds], core_ids=[0])
    return r.results[0]["out_x"].reshape(16, SEQ, P)
```

```python
from contextlib import ExitStack

import concourse.bass as bass
import numpy as np
from concourse import mybir
from concourse.alu_op_type import AluOpType as ALU

F32 = mybir.dt.float32
F32R = mybir.dt.float32r
BF16 = mybir.dt.bfloat16
ACT = mybir.ActivationFunctionType
AX_X = mybir.AxisListType.X

P = 128
SEQ = 256
NTOK = 16 * SEQ
CB = 2
T = CB * SEQ
TT = T // P
NCHUNK = NTOK // T
HD = 64
HEADS = 16
HP = HEADS // 2
RHEADS = 8
RHP = RHEADS // 2
FEAT = HEADS * HD
RFEAT = RHEADS * HD
EXPERTS = 31
SLOT = 32
TOPK = 3
AW = 40
EPS = 1e-5
SC = SEQ + P
RLAG = 3
LAG = 3
NPB = LAG + 1
FFN0, RET, FFN1 = range(3)
GT = TT // CB
AHEAD = 8
LATE = 8


class Signal:

    def __init__(self, sem, per_layer):
        self.sem, self.per_layer = sem, per_layer
        self.per_chunk = sum(per_layer)

    def at(self, i, layer, n):
        return i * self.per_chunk + (sum(self.per_layer[:layer]) + n)


LOADED = {
    "ow": (P, HP * P), "rwo": (P, RHEADS * P), "shw2": (P, P), "rew2": (P, EXPERTS * P),
    "decay": (P, RHEADS * SEQ), "rcos": (P, SEQ), "rsin": (P, SEQ),
    "identf": (P, P), "g1row": (P, P), "g2row": (P, P), "obrow": (P, P),
    "cols": (P, 100),
}
IN_BF16 = {"identb": (P, P), "maskneg": (P, P), "sel": (3 * SLOT, SLOT)}
SPLIT = {
    "wq": FEAT, "wk": FEAT, "wv": FEAT, "router": P, "shw1": P,
    "rwq": RFEAT, "rwk": RFEAT, "rwv": FEAT, "rwg": FEAT, "rew1": EXPERTS * P,
}
COL = {}
_at = 0
for _n, _w in (("g1", 1), ("g2", 1), ("qb", HP), ("qbs", HP), ("kb", HP), ("kbs", HP), ("vb", HP),
               ("shb1", 1), ("shb2", 1), ("reb1", EXPERTS), ("gnw", RHEADS), ("gnb", RHEADS),
               ("rb", 1), ("theta", 1), ("sign", 1)):
    COL[_n] = (_at, _w)
    _at += _w
COLS = _at

TWO_PI_1 = 6.28125
TWO_PI_2 = float(np.float32(np.round((2 * np.pi - TWO_PI_1) * 2**21) / 2**21))
TWO_PI_3 = float(np.float32(2 * np.pi - TWO_PI_1 - TWO_PI_2))
MAGIC = 12582912.0
PI_IN = 3.1415925


def build(nc, x_in, ins, out):
    ctx = ExitStack()
    with ctx:
        def sb(name, shape, dt=F32):
            return ctx.enter_context(nc.sbuf_tensor(name, list(shape), dt))

        def sem(name):
            return ctx.enter_context(nc.semaphore(name))

        def signal(name, ffn=0, ret=0):
            return Signal(sem(name), [ffn, ret, ffn])

        W = {n: sb("c_" + n, s) for n, s in LOADED.items()}
        W.update({n: sb("c_" + n, s, BF16) for n, s in IN_BF16.items()})
        HI = {n: sb("hi_" + n, (P, c), F32R) for n, c in SPLIT.items()}
        LO = {n: sb("lo_" + n, (P, c), F32R) for n, c in SPLIT.items()}
        cosT, sinT = sb("cosT", (P, SEQ)), sb("sinT", (P, SEQ))
        b2p = [sb(f"b2p{j}", (3 * SLOT, P), BF16) for j in range(3)]
        half_neg = sb("half_neg", (P, TT))
        shb2h = sb("shb2h", (P, 1))
        qbh = sb("qbh", (P, 2 * HP))

        def col(name, k=0):
            a = COL[name][0] + k
            return W["cols"][:, a:a + 1]

        xin = sb("xin", (P, TT, P))
        x = sb("x", (P, TT, P))
        actH, actL = sb("actH", (P, T), F32R), sb("actL", (P, T), F32R)
        V = sb("V", (P, TT, FEAT))
        C = sb("C", (P, HP, T))
        G = sb("G", (P, NPB * 2 * SC))
        E_ = sb("E", (P, 8 * T))
        N_ = sb("N", (P, 4 * T))
        pos, b2x = N_[:, 5 * SEQ:6 * SEQ], N_[0:3 * SLOT, 6 * SEQ:6 * SEQ + P]
        PT = sb("PT", (P, 2, 2, SC))
        stat = sb("stat", (P, TT, 6))
        mv = sb("mv", (P, TT, 2))
        wv_, rs = sb("wv", (P, TT)), sb("rs", (P, TT))
        negm = sb("negm", (P, 2, 2, 2))
        rsum = sb("rsum", (P, NPB, 2, 2))
        rinv = sb("rinv", (P, NPB, 2, 2))
        rstat = sb("rstat", (P, 2, 4, 6))
        rmv = sb("rmv", (P, 2, 4, 2))
        rw_, rrs = sb("rw", (P, 2, 4)), sb("rrs", (P, 2, 4))
        rnm, rnb = sb("rnm", (P, 2, 4)), sb("rnb", (P, 2, 4))
        aff = sb("aff", (P, TT, AW))
        rest = sb("rest", (P, TT, AW))
        top = sb("top", (P, TT, 8))
        lmx, lsum, linv = sb("lmx", (P, TT)), sb("lsum", (P, TT)), sb("linv", (P, TT))
        g3 = sb("g3", (P, TT, 3 * SLOT), BF16)
        gT = sb("gT", (3 * SLOT, T), BF16)

        prob = G[:, :].rearrange("p (u h s) -> p u h s", u=NPB, h=2)
        qT = [E_[:, k * T:(k + 1) * T] for k in (0, 1)]
        kT = [E_[:, k * T:(k + 1) * T] for k in (2, 3)]
        rc = [E_[:, k * T:(k + 1) * T] for k in (4, 5)]
        rsw = [E_[:, k * T:(k + 1) * T] for k in (6, 7)]
        hsb = [V[:, k // 2, (k % 2) * T:(k % 2 + 1) * T] for k in range(AHEAD)]
        hg = [C[:, k, :] for k in range(HP)]
        yT = E_[:, 5 * T:6 * T]
        lgT = E_[0:SLOT, 6 * T:7 * T]
        small = E_[:, 7 * T:8 * T]
        lg = small[:, 0:TT * EXPERTS].rearrange("p (t e) -> p t e", t=TT)
        ex = small[:, P:P + TT * EXPERTS].rearrange("p (t e) -> p t e", t=TT)
        gate = small[:, 2 * P:3 * P].rearrange("p (t e) -> p t e", t=TT)
        gres = small[:, 3 * P:4 * P].rearrange("p (t e) -> p t e", t=TT)
        tiles = lambda k: N_[:, k * T:(k + 1) * T].rearrange("p (t d) -> p t d", t=TT)
        xnb, ao, res, z = tiles(0), tiles(1), tiles(2), tiles(3)
        xout = tiles(1)
        onrm = [N_[:, k * T:(k + 1) * T].rearrange("p (h q v) -> p h q v", h=2, q=2) for k in (0, 1)]
        og_in = [N_[:, k * T:(k + 1) * T].rearrange("p (h s) -> p h s", h=2) for k in (2, 3)]

        BK = [ctx.enter_context(nc.psum_tensor(f"bank{j}", [P, 512], F32)) for j in range(2)]
        SP2 = ctx.enter_context(nc.psum_tensor("scores", [P, 4, 512], F32))
        BL = [ctx.enter_context(nc.psum_tensor(f"bank{j}", [P, 512], F32)) for j in (6, 7)]
        proj_ps, ctx_ps = BK
        S = [SP2[:, 0:2, :], SP2[:, 2:4, :]]
        four = [SP2[:, j, :] for j in range(4)]
        pt_ps = BL
        batch = [slice(g * SEQ, (g + 1) * SEQ) for g in range(CB)]
        tiles_of = [range(g * GT, (g + 1) * GT) for g in range(CB)]
        zt_ps = [proj_ps[:, 0:SEQ], ctx_ps[:, 0:SEQ]]
        o_ps = [four[0][:, 0:SEQ], pt_ps[1][:, 0:SEQ]]
        y_ps = [pt_ps[g][:, 0:SEQ] for g in range(CB)]
        yt_ps = y_ps
        by_tile = lambda ap: ap.rearrange("p (t d) -> p t d", t=GT)

        h_ps = lambda k: four[k % 4 if k < AHEAD else k % 2]

        s_w = {n: sem("s_ld_" + n) for n in ("const", "attn", "expert", "ret")}
        s_stage = [sem(f"s_stage{j}") for j in range(3)]
        s_hi = sem("s_hi")
        s_lo = sem("s_lo")
        s_prep = sem("s_prep")
        s_angle = sem("s_angle")
        s_sin = sem("s_sin")
        s_ready = sem("s_ready")
        s_pool0 = sem("s_pool0")
        s_taken, s_taken_pe, s_taken_pool = sem("s_taken"), sem("s_taken_pe"), sem("s_taken_pool")
        s_xin = sem("s_xin")
        s_out = sem("s_out")

        n_stat = Signal(sem("n_stat"), [2 * TT, 2 * TT, 2 * TT])
        by_batch_and_norm = [2 * CB, CB, 2 * CB]
        n_var = Signal(sem("n_var"), by_batch_and_norm)
        n_rs = Signal(sem("n_rs"), by_batch_and_norm)
        n_z = Signal(sem("n_z"), [2 * TT, TT, 2 * TT])
        n_zT = Signal(sem("n_zT"), by_batch_and_norm)
        n_hi = Signal(sem("n_hi"), by_batch_and_norm)
        n_lo = Signal(sem("n_lo"), by_batch_and_norm)
        x_new = Signal(sem("x_new"), [CB, CB, CB])
        xn_step = signal("xn_step", 1)
        xn_ready = signal("xn_ready", 1)
        ao_ready = signal("ao_ready", CB)
        ss_ready = signal("ss_ready", CB)
        res_step = signal("res_step", 3)
        res_ready = signal("res_ready", 1)
        v_acc, v_out = signal("v_acc", 2 * TT, 4 * TT), signal("v_out", 2 * TT, 4 * TT)
        qk_acc = signal("qk_acc", 2 * HP, 2 * RHP)
        qk_read = signal("qk_read", 2 * HP, 2 * RHP)
        qk_mul = signal("qk_mul", 2 * HP, 2 * RHP)
        qk_rot = signal("qk_rot", 2 * HP, 2 * RHP)
        s_acc = signal("s_acc", 2 * HP, 2 * RHP)
        mx = signal("mx", 2 * HP)
        p_exp = signal("p_exp", 2 * HP)
        p_inv = signal("p_inv", 2 * HP)
        p_norm = signal("p_norm", 2 * HP)
        pt0, pt1 = signal("pt0", 2 * HP), signal("pt1", 2 * HP)
        pt0_out, pt1_out = signal("pt0_out", 2 * HP), signal("pt1_out", 2 * HP)
        c_acc, c_out = signal("c_acc", 2 * HP), signal("c_out", 2 * HP)
        o_acc = signal("o_acc", CB, CB)
        lg_acc, lg_out = signal("lg_acc", 1), signal("lg_out", 1)
        lg_tm = signal("lg_tm", 1)
        rt_step = signal("rt_step", 17)
        lg_sub, lg_exp = signal("lg_sub", 1), signal("lg_exp", 1)
        g_ready, gT_acc, gT_out = signal("g_ready", 1), signal("gT_acc", 1), signal("gT_out", 1)
        h_acc, h_out = signal("h_acc", EXPERTS + 1), signal("h_out", EXPERTS + 1)
        gb_acc, hg_out = signal("gb_acc", EXPERTS), signal("hg_out", EXPERTS)
        y_acc, y_out, yt_acc = signal("y_acc", CB), signal("y_out", CB), signal("yt_acc", CB)
        a_out = signal("a_out", 0, 2 * RHP)
        ro_acc = signal("ro_acc", 0, 2 * RHP)
        ro_stat = signal("ro_stat", 0, 16 * RHP)
        ro_var, ro_rs = signal("ro_var", 0, 2 * RHP), signal("ro_rs", 0, 4 * RHP)
        on_out = signal("on_out", 0, 2 * RHP)
        ot_acc, ot_out = signal("ot_acc", 0, 2 * RHP), signal("ot_out", 0, 2 * RHP)
        og_out = signal("og_out", 0, 2 * RHP)

        reduced = [N_[:, 0:SEQ], N_[:, SEQ:2 * SEQ]]
        ang, turn, part = N_[:, 2 * SEQ:3 * SEQ], N_[:, 3 * SEQ:4 * SEQ], N_[:, 4 * SEQ:5 * SEQ]

        mask_in, sel_in = E_[:, 0:P], E_[0:3 * SLOT, P:P + SLOT]
        room = [V[:, :, :].rearrange("p t f -> p (t f)"), C[:, :, :].rearrange("p h t -> p (h t)")]

        x_v = x_in.rearrange("(c t p) d -> c p t d", t=TT, p=P)
        out_v = out.rearrange("(c t p) d -> c p t d", t=TT, p=P)

        block = ctx.enter_context(nc.Block())

        place = {"wq": (0, 0), "wk": (0, FEAT), "wv": (0, 2 * FEAT), "router": (0, 3 * FEAT),
                 "shw1": (0, 3 * FEAT + P), "rwq": (1, 0), "rwk": (1, RFEAT), "rwv": (1, 2 * RFEAT),
                 "rwg": (1, 2 * RFEAT + FEAT), "rew1": (0, 0)}
        order = list(SPLIT)
        raw = {n: room[r][:, o:o + SPLIT[n]] for n, (r, o) in place.items()}
        N_CONST = len(LOADED) + 4

        @block.sync
        def _(sp):
            for n in order[:3]:
                sp.dma_start(raw[n], ins[n]).then_inc(s_stage[0], 16)
            sp.dma_start(W["cols"][:, :], ins["cols"]).then_inc(s_w["const"], 16)
            sp.dma_start(pos, ins["pos"]).then_inc(s_w["const"], 16)
            sp.dma_start(b2x, ins["b2x"]).then_inc(s_w["const"], 16)
            sp.dma_start(mask_in, ins["maskneg"]).then_inc(s_w["const"], 16)
            sp.dma_start(sel_in, ins["sel"]).then_inc(s_w["const"], 16)
            for n in ("identf", "g1row", "g2row", "obrow", "rcos", "rsin",
                      "ow", "shw2"):
                sp.dma_start(W[n][:, :], ins[n]).then_inc(s_w["const"], 16)
            for n in order[3:9]:
                sp.dma_start(raw[n], ins[n]).then_inc(s_stage[1], 16)
            for n in ("decay", "rwo", "rew2"):
                sp.dma_start(W[n][:, :], ins[n]).then_inc(s_w["const"], 16)
            sp.wait_ge(s_lo, 5)
            sp.dma_start(raw["rew1"], ins["rew1"]).then_inc(s_stage[2], 16)
            sp.sem_inc(s_out, 16)
            sp.dma_start(xin[:, :, :], x_v[0]).then_inc(s_xin, 16)
            with sp.Fori(0, NCHUNK - 1) as i:
                sp.wait_ge(res_ready.sem, res_ready.at(i, FFN0, 1))
                sp.dma_start(xin[:, :, :], x_v[i + 1]).then_inc(s_xin, 16)
                sp.wait_ge(x_new.sem, x_new.at(i, FFN1, CB))
                sp.dma_start(out_v[i], xout).then_inc(s_out, 16)
            sp.wait_ge(x_new.sem, x_new.at(NCHUNK - 1, FFN1, CB))
            sp.dma_start(out_v[NCHUNK - 1], xout).then_inc(s_out, 16)
            sp.wait_ge(s_out, 16 * (NCHUNK + 1))

        @block.gpsimd
        def _(pool):
            pool.memset(half_neg[:, :], -0.5).then_inc(s_pool0, 1)
            pool.memset(g3[:, :, :], 0.0).then_inc(s_pool0, 1)
            pool.memset(aff[:, :, :], -1.0).then_inc(s_pool0, 1)
            pool.wait_ge(s_w["const"], 16 * N_CONST)
            pool.wait_ge(s_pool0, 3)

            def row(name):
                r = W[name]
                return r[:, :].unsqueeze(1).broadcast_to((P, TT, P))

            def rsqrt(i, layer, n):
                for g in range(CB):
                    w = slice(g * GT, (g + 1) * GT)
                    pool.wait_ge(n_var.sem, n_var.at(i, layer, n * CB + g + 1))
                    pool.tensor_tensor(rs[:, w], wv_[:, w], half_neg[:, w], ALU.pow).then_inc(n_rs.sem, 1)

            def rotated(i, layer, j, hps):
                hp = j // 2
                dst = (qT, kT)[j % 2][hp % 2]
                pool.wait_ge(qk_mul.sem, qk_mul.at(i, layer, j + 1))
                if hp >= 2:
                    pool.wait_ge(s_acc.sem, s_acc.at(i, layer, 2 * (hp - 1)))
                pool.tensor_tensor(dst, rc[j % 2], rsw[j % 2], ALU.add).then_inc(qk_rot.sem, 1)

            def ffn(i, layer, src, following=None):
                if layer == FFN1:
                    rsqrt(i, FFN1, 0)
                pool.wait_ge(n_z.sem, n_z.at(i, layer, TT))
                pool.tensor_tensor(xnb, z, row("g1row"), ALU.mult).then_inc(xn_step.sem, 1)
                pool.wait_ge(xn_step.sem, xn_step.at(i, layer, 1))
                pool.tensor_tensor(xnb, xnb, row("obrow"), ALU.add).then_inc(xn_ready.sem, 1)
                rotated(i, layer, 0, HP)
                rotated(i, layer, 1, HP)
                for u in range(2 * HP + 1):
                    if u + 2 < 2 * HP:
                        rotated(i, layer, u + 2, HP)
                    if u >= 1:
                        n = u - 1
                        pool.wait_ge(p_inv.sem, p_inv.at(i, layer, n + 1))
                        pool.sem_inc(s_taken_pool, 1)
                        for h in range(2):
                            for q, (a, b) in enumerate(((0, P), (P, SC))):
                                w = prob[:, n % NPB, h, a:b]
                                last = pool.tensor_scalar(w, w, rinv[:, n % NPB, q, h:h + 1], 1.0, ALU.mult, ALU.mult)
                        last.then_inc(p_norm.sem, 1)
                rsqrt(i, layer, 1)
                pool.wait_ge(n_z.sem, n_z.at(i, layer, 2 * TT))
                pool.tensor_tensor(res, z, row("g2row"), ALU.mult).then_inc(res_step.sem, 1)
                pool.wait_ge(res_step.sem, res_step.at(i, layer, 1))
                pool.tensor_tensor(res, res, ao, ALU.add).then_inc(res_step.sem, 1)
                pool.wait_ge(res_step.sem, res_step.at(i, layer, 2))
                pool.sem_inc(s_taken_pool, 1)
                pool.tensor_scalar(res, res, 0.5, 1.0, ALU.mult, ALU.mult).then_inc(res_step.sem, 1)
                pool.wait_ge(res_step.sem, res_step.at(i, layer, 3))
                pool.tensor_tensor(res, res, src[:, :, :], ALU.add).then_inc(res_ready.sem, 1)
                if following is not None:
                    rsqrt(following, FFN0, 0)

            def retention(i):
                rsqrt(i, RET, 0)
                rotated(i, RET, 0, RHP)
                rotated(i, RET, 1, RHP)
                for u in range(2 * RHP + RLAG):
                    if u + 2 < 2 * RHP:
                        rotated(i, RET, u + 2, RHP)
                    if 1 <= u <= 2 * RHP:
                        n = u - 1
                        pool.wait_ge(ro_var.sem, ro_var.at(i, RET, n + 1))
                        pool.tensor_tensor(rrs[:, n % 2, :], rw_[:, n % 2, :], half_neg[:, :], ALU.pow)\
                            .then_inc(ro_rs.sem, 1)
                        pool.wait_ge(ro_rs.sem, ro_rs.at(i, RET, 2 * n + 1))
                        pool.tensor_tensor(rnb[:, n % 2, :], rnm[:, n % 2, :], rrs[:, n % 2, :], ALU.mult)\
                            .then_inc(ro_rs.sem, 1)
                    if u >= RLAG:
                        n = u - RLAG
                        hp, b = n // 2, n % 2
                        pool.wait_ge(ot_out.sem, ot_out.at(i, RET, n + 1))
                        for h in range(2):
                            c = C[:, 2 * hp + h, b * SEQ:(b + 1) * SEQ]
                            last = pool.tensor_tensor(c, og_in[n % 2][:, h, :], c, ALU.mult)
                        last.then_inc(og_out.sem, 1)

            def chunk(i, following):
                ffn(i, FFN0, xin)
                retention(i)
                ffn(i, FFN1, x, following)

            rsqrt(0, FFN0, 0)
            with pool.Fori(0, NCHUNK - 1) as i:
                chunk(i, i + 1)
            chunk(NCHUNK - 1, None)

        @block.scalar
        def _(act):
            act.wait_ge(s_w["const"], 16 * N_CONST)
            for k, n in enumerate(order):
                act.wait_ge(s_stage[0 if k < 3 else 1 if k < 9 else 2], 16 * (3 if k < 3 else 6 if k < 9 else 1))
                act.activation(HI[n][:, :], raw[n], ACT.Copy, scale=HD ** -0.5 if n == "wq" else 1.0).then_inc(s_hi, 1)
                if n == "wv":
                    act.wait_ge(s_angle, 2)
                    act.activation(cosT[:, :], reduced[0], ACT.Sin).then_inc(s_sin, 1)
                    act.activation(sinT[:, :], reduced[1], ACT.Sin).then_inc(s_sin, 1)

            def high_part(i, layer, n, g, gamma):
                act.wait_ge(n_zT.sem, n_zT.at(i, layer, n * CB + g + 1))
                act.activation(actH[:, batch[g]], zt_ps[g], ACT.Copy, scale=gamma).then_inc(n_hi.sem, 1)

            def values(i, layer, gamma=1.0):
                for j in range(2 * TT):
                    if j < CB and layer != FFN0:
                        high_part(i, layer, 0, j, gamma)
                    act.wait_ge(v_acc.sem, v_acc.at(i, layer, j + 1))
                    act.activation(V[:, j // 2, (j % 2) * 512:(j % 2 + 1) * 512], four[j % 4], ACT.Copy)\
                        .then_inc(v_out.sem, 1)

            def ffn(i, layer, following=None):
                values(i, layer, col("g1"))
                for u in range(2 * HP + LAG):
                    n = u - LAG
                    if n >= 0:
                        act.wait_ge(pt1.sem, pt1.at(i, layer, n + 1))
                        act.activation(PT[:, n % 2, 1, :], pt_ps[1][:, 0:SC], ACT.Copy).then_inc(pt1_out.sem, 1)
                    if u < 2 * HP:
                        act.wait_ge(mx.sem, mx.at(i, layer, u + 1))
                        for h in range(2):
                            for q, (a, b) in enumerate(((0, P), (P, SC))):
                                last = act.activation(prob[:, u % NPB, h, a:b], S[u % 2][:, h, a:b], ACT.Exp,
                                                      bias=negm[:, u % 2, q, h:h + 1],
                                                      accum_out=rsum[:, u % NPB, q, h:h + 1])
                        last.then_inc(p_exp.sem, 1)
                    if n >= 0:
                        act.wait_ge(c_acc.sem, c_acc.at(i, layer, n + 1))
                        act.activation(C[:, n // 2, (n % 2) * SEQ:(n % 2 + 1) * SEQ], ctx_ps[:, 0:SEQ], ACT.Identity,
                                       bias=col("vb", n // 2)).then_inc(c_out.sem, 1)
                for g in range(CB):
                    act.wait_ge(ao_ready.sem, ao_ready.at(i, layer, g + 1))
                    for t in tiles_of[g]:
                        last = act.activation(z[:, t, :], ao[:, t, :], ACT.Square, accum_out=wv_[:, t:t + 1])
                    last.then_inc(ss_ready.sem, 1)
                    high_part(i, layer, 1, g, col("g2"))
                act.wait_ge(lg_acc.sem, lg_acc.at(i, layer, 1))
                act.activation(lgT, proj_ps[0:SLOT, :], ACT.Identity, bias=W["cols"][0:SLOT, COL["rb"][0]:COL["rb"][0] + 1])\
                    .then_inc(lg_out.sem, 1)
                act.wait_ge(lg_sub.sem, lg_sub.at(i, layer, 1))
                act.activation(ex, lg, ACT.Exp).then_inc(lg_exp.sem, 1)
                for k in range(EXPERTS + 1):
                    act.wait_ge(h_acc.sem, h_acc.at(i, layer, k + 1))
                    if k > AHEAD:
                        act.wait_ge(hg_out.sem, hg_out.at(i, layer, k - AHEAD))
                    act.activation(hsb[k % AHEAD], h_ps(k), ACT.Gelu,
                                   bias=col("shb1") if k == 0 else col("reb1", k - 1)).then_inc(h_out.sem, 1)
                if following is not None:
                    for g in range(CB):
                        high_part(following, FFN0, 0, g, col("g1"))
                for g in range(CB):
                    act.wait_ge(y_acc.sem, y_acc.at(i, layer, g + 1))
                    act.activation(yT[:, batch[g]], y_ps[g], ACT.Identity, bias=shb2h[:, 0:1], scale=0.5)\
                        .then_inc(y_out.sem, 1)

            def retention(i):
                values(i, RET)
                for c in range(RHEADS):
                    j = 2 * TT + c
                    act.wait_ge(v_acc.sem, v_acc.at(i, RET, j + 1))
                    act.activation(C[:, c, :], four[j % 4], ACT.Silu).then_inc(v_out.sem, 1)

                for u in range(2, 2 * RHP + RLAG):
                    if u >= RLAG:
                        n = u - RLAG
                        act.wait_ge(ot_acc.sem, ot_acc.at(i, RET, n + 1))
                        if n >= 2:
                            act.wait_ge(og_out.sem, og_out.at(i, RET, n - 1))
                        for h in range(2):
                            c = 2 * (n // 2) + h
                            last = act.activation(og_in[n % 2][:, h, :], ctx_ps[:, h * SEQ:(h + 1) * SEQ], ACT.Identity,
                                                  bias=col("gnb", c), scale=col("gnw", c))
                        last.then_inc(ot_out.sem, 1)
                    if u - 2 < 2 * RHP:
                        n = u - 2
                        act.wait_ge(ro_rs.sem, ro_rs.at(i, RET, 2 * n + 2))
                        for hq in range(4):
                            last = act.activation(onrm[n % 2][:, hq // 2, hq % 2, :], pt_ps[n % 2][:, hq * P:(hq + 1) * P],
                                                  ACT.Identity, bias=rnb[:, n % 2, hq:hq + 1], scale=rrs[:, n % 2, hq:hq + 1])
                        last.then_inc(on_out.sem, 1)

            def chunk(i, following):
                ffn(i, FFN0)
                retention(i)
                ffn(i, FFN1, following)

            for g in range(CB):
                high_part(0, FFN0, 0, g, col("g1"))
            with act.Fori(0, NCHUNK - 1) as i:
                chunk(i, i + 1)
            chunk(NCHUNK - 1, None)

        @block.tensor
        def _(pe):
            pe.wait_ge(s_w["const"], 16 * N_CONST)
            pe.wait_ge(s_lo, len(order))
            pe.wait_ge(s_ready, 1)

            def product(dst, wn, a, b, tok=None, act=slice(0, T)):
                for k, (w, y) in enumerate(((HI, actH), (LO, actH), (HI, actL))):
                    w = w[wn][:, a:b]
                    y = y[:, act] if tok is None else y[:, tok * P:(tok + 1) * P]
                    last = pe.matmul(dst, w if tok is None else y, y if tok is None else w, start=k == 0, stop=k == 2)
                return last

            def transposed(i, layer, n, g):
                for k, t in enumerate(tiles_of[g]):
                    pe.wait_ge(n_z.sem, n_z.at(i, layer, n * TT + t + 1))
                    last = pe.transpose(zt_ps[g][:, k * P:(k + 1) * P], z[:, t, :], W["identf"][:, :])
                last.then_inc(n_zT.sem, 1)

            def split(i, layer, n, g):
                pe.wait_ge(n_hi.sem, n_hi.at(i, layer, n * CB + g + 1))
                pe.wait_ge(n_lo.sem, n_lo.at(i, layer, n * CB + g + 1))

            def first_products(i, layer, wq, wk, wv):
                if layer == FFN0:
                    split(i, layer, 0, 0)
                    split(i, layer, 0, 1)
                else:
                    if layer == RET:
                        transposed(i, layer, 0, 0)
                    split(i, layer, 0, 0)
                for j in range(2 * TT):
                    if j == 1 and layer != FFN0:
                        transposed(i, layer, 0, 1)
                    if j == 2 * GT:
                        if layer != FFN0:
                            split(i, layer, 0, 1)
                        project(i, layer, 0, wq, wk)
                    if j == 3 * GT:
                        project(i, layer, 1, wq, wk)
                    if j >= 4:
                        pe.wait_ge(v_out.sem, v_out.at(i, layer, j - 3))
                    product(four[j % 4], wv, (j % 2) * 512, (j % 2 + 1) * 512, tok=j // 2).then_inc(v_acc.sem, 1)

            def project(i, layer, j, wq, wk):
                if j >= 1:
                    pe.wait_ge(qk_read.sem, qk_read.at(i, layer, j))
                hp = j // 2
                product(proj_ps[:, :], (wq, wk)[j % 2], hp * P, (hp + 1) * P).then_inc(qk_acc.sem, 1)

            def output(i, layer, w, g, midway=None):
                for k, t in enumerate(tiles_of[g]):
                    for c in range(HP):
                        if midway is not None and (k, c) == (GT - 1, HP // 2):
                            midway()
                        last = pe.matmul(o_ps[g][:, k * P:(k + 1) * P], C[:, c, t * P:(t + 1) * P],
                                         w[:, c * P:(c + 1) * P], start=c == 0, stop=c == HP - 1)
                last.then_inc(o_acc.sem, 1)

            def ffn(i, layer, following=None):
                first_products(i, layer, "wq", "wk", "wv")
                pe.wait_ge(v_out.sem, v_out.at(i, layer, 2 * TT))
                for u in range(2 * HP + LAG):
                    n = u - LAG
                    if n >= 0:
                        pe.wait_ge(p_norm.sem, p_norm.at(i, layer, n + 1))
                        for h, (acc, free) in enumerate(((pt0, pt0_out), (pt1, pt1_out))):
                            if n >= 1:
                                pe.wait_ge(free.sem, free.at(i, layer, n))
                            w = prob[:, n % NPB, h, :]
                            for dst, src in ((0, 0), (P, P), (2 * P, 2 * P)):
                                last = pe.transpose(pt_ps[h][:, dst:dst + P], w[:, src:src + P], W["identf"][:, :])
                            last.then_inc(acc.sem, 1)
                    if n == 2 * HP - 1:
                        pe.wait_ge(c_out.sem, c_out.at(i, layer, n))
                        output(i, layer, W["ow"], 0)
                    if u + 2 < 2 * HP:
                        project(i, layer, u + 2, "wq", "wk")
                    if u < 2 * HP:
                        hp, b = u // 2, u % 2
                        pe.wait_ge(qk_rot.sem, qk_rot.at(i, layer, 2 * hp + 2))
                        if u >= 2:
                            pe.wait_ge(p_exp.sem, p_exp.at(i, layer, u - 1))
                        for h in range(2):
                            r = slice(HD * h, HD * (h + 1))
                            q, k = qT[hp % 2][r, b * SEQ:(b + 1) * SEQ], kT[hp % 2][r, b * SEQ:(b + 1) * SEQ]
                            dst = S[u % 2][:, h, :]
                            pe.matmul(dst[:, 0:P], q[:, 0:P], k[:, 0:P], start=True, stop=False)
                            pe.matmul(dst[:, 0:P], W["identb"][:, :], W["maskneg"][:, :], start=False, stop=True)
                            pe.matmul(dst[:, P:SC], q[:, P:SEQ], k, start=True, stop=False)
                            last = pe.matmul(dst[:, 2 * P:SC], W["identb"][:, :], W["maskneg"][:, :], start=False, stop=True)
                        last.then_inc(s_acc.sem, 1)
                    if n >= 0:
                        hp, b = n // 2, n % 2
                        pe.wait_ge(pt0_out.sem, pt0_out.at(i, layer, n + 1))
                        pe.wait_ge(pt1_out.sem, pt1_out.at(i, layer, n + 1))
                        if n >= 1:
                            pe.wait_ge(c_out.sem, c_out.at(i, layer, n))
                        for h in range(2):
                            dst = ctx_ps[HD * h:HD * (h + 1), :]
                            f = slice((2 * hp + h) * HD, (2 * hp + h + 1) * HD)
                            w = PT[:, n % 2, h, :]
                            pe.matmul(dst[:, 0:SEQ], V[:, 2 * b, f], w[:, 0:SEQ], start=True, stop=False)
                            last = pe.matmul(dst[:, P:SEQ], V[:, 2 * b + 1, f], w[:, SEQ:SC], start=False, stop=True)
                        last.then_inc(c_acc.sem, 1)
                pe.wait_ge(c_out.sem, c_out.at(i, layer, 2 * HP))
                output(i, layer, W["ow"], 1, lambda: transposed(i, layer, 1, 0))

                def expert_in(k, act=slice(0, T)):
                    w, at = ("shw1", 0) if k == 0 else ("rew1", k - 1)
                    return product(h_ps(k)[:, act], w, at * P, (at + 1) * P, act=act)

                def spread(k):
                    if k >= 3:
                        pe.wait_ge(hg_out.sem, hg_out.at(i, layer, k - 2))
                    pe.matmul(four[2 + k % 2], W["sel"][:, k - 1:k].broadcast_to((3 * SLOT, P)), gT[:, :],
                              start=True, stop=True).then_inc(gb_acc.sem, 1)

                def expert_out(k, g):
                    w, h = (W["shw2"][:, :], hsb[0]) if k == 0 else (W["rew2"][:, (k - 1) * P:k * P], hg[k % HP])
                    pe.matmul(y_ps[g], w, h[:, batch[g]], start=k == 0, stop=False)

                def output_biases(g):
                    for j in range(3):
                        last = pe.matmul(y_ps[g], b2p[j][:, :], gT[:, batch[g]], start=False, stop=j == 2)
                    last.then_inc(y_acc.sem, 1)

                def y_transposed(g):
                    pe.wait_ge(y_out.sem, y_out.at(i, layer, g + 1))
                    for k, t in enumerate(tiles_of[g]):
                        last = pe.transpose(yt_ps[g][:, k * P:(k + 1) * P], yT[:, t * P:(t + 1) * P], W["identf"][:, :])
                    last.then_inc(yt_acc.sem, 1)

                for g in range(CB):
                    split(i, layer, 1, g)
                    last = product(proj_ps[:, batch[g]], "router", 0, P, act=batch[g])
                    if g == CB - 1:
                        last.then_inc(lg_acc.sem, 1)
                    for k in range(4):
                        last = expert_in(k, batch[g])
                        if g == CB - 1:
                            last.then_inc(h_acc.sem, 1)
                    if g == 0:
                        transposed(i, layer, 1, 1)
                pe.wait_ge(lg_out.sem, lg_out.at(i, layer, 1))
                pe.sem_inc(s_taken_pe, 1)
                for t in range(TT):
                    last = pe.transpose(ctx_ps[:, t * SLOT:(t + 1) * SLOT], lgT[:, t * P:(t + 1) * P],
                                        W["identf"][0:SLOT, 0:SLOT])
                last.then_inc(lg_tm.sem, 1)
                for k in range(4, AHEAD):
                    pe.wait_ge(h_out.sem, h_out.at(i, layer, k - 3))
                    expert_in(k).then_inc(h_acc.sem, 1)
                for g in range(CB):
                    expert_out(0, g)
                pe.wait_ge(g_ready.sem, g_ready.at(i, layer, 1))
                for t in range(TT):
                    last = pe.transpose(ctx_ps.bitcast(BF16)[0:3 * SLOT, t * P:(t + 1) * P], g3[:, t, :], W["identb"][:, :])
                last.then_inc(gT_acc.sem, 1)
                pe.wait_ge(gT_out.sem, gT_out.at(i, layer, 1))
                pe.wait_ge(h_out.sem, h_out.at(i, layer, AHEAD))
                spread(1)
                for k in range(1, EXPERTS + 1):
                    n = k + AHEAD - 1
                    if n <= EXPERTS:
                        if n >= AHEAD + 2:
                            pe.wait_ge(h_out.sem, h_out.at(i, layer, n - 1))
                        expert_in(n).then_inc(h_acc.sem, 1)
                    if k + 1 <= EXPERTS:
                        spread(k + 1)
                    pe.wait_ge(hg_out.sem, hg_out.at(i, layer, k))
                    expert_out(k, 0)
                    if k <= EXPERTS - LATE:
                        expert_out(k, 1)
                    if n == EXPERTS + 2 and following is not None:
                        for g in range(CB):
                            transposed(following, FFN0, 0, g)
                output_biases(0)
                for k in range(EXPERTS - LATE + 1, EXPERTS + 1):
                    if k == EXPERTS - LATE // 2:
                        y_transposed(0)
                    expert_out(k, 1)
                output_biases(1)
                y_transposed(1)

            def retention(i):
                first_products(i, RET, "rwq", "rwk", "rwv")
                for c in range(RHEADS):
                    j = 2 * TT + c
                    pe.wait_ge(v_out.sem, v_out.at(i, RET, j - 3))
                    product(four[j % 4], "rwg", c * P, (c + 1) * P).then_inc(v_acc.sem, 1)
                for u in range(2 * RHP + RLAG):
                    if u + 2 < 2 * RHP:
                        project(i, RET, u + 2, "rwq", "rwk")
                    if u == 0:
                        pe.wait_ge(v_out.sem, v_out.at(i, RET, 4 * TT))
                    if u < 2 * RHP:
                        hp, b = u // 2, u % 2
                        pe.wait_ge(qk_rot.sem, qk_rot.at(i, RET, 2 * hp + 2))
                        if u >= 2:
                            pe.wait_ge(a_out.sem, a_out.at(i, RET, u - 1))
                        for h in range(2):
                            r = slice(HD * h, HD * (h + 1))
                            q, k = qT[hp % 2][r, b * SEQ:(b + 1) * SEQ], kT[hp % 2][r, b * SEQ:(b + 1) * SEQ]
                            dst = S[u % 2][:, h, :]
                            pe.matmul(dst[:, 0:SEQ], k[:, 0:P], q, start=True, stop=True)
                            last = pe.matmul(dst[:, SEQ:SC], k[:, P:SEQ], q[:, P:SEQ], start=True, stop=True)
                        last.then_inc(s_acc.sem, 1)
                    if u >= RLAG:
                        n = u - RLAG
                        pe.wait_ge(on_out.sem, on_out.at(i, RET, n + 1))
                        if n >= 1:
                            pe.wait_ge(ot_out.sem, ot_out.at(i, RET, n))
                        for h in range(2):
                            for q in range(2):
                                a = h * SEQ + q * P
                                last = pe.transpose(ctx_ps[:, a:a + P], onrm[n % 2][:, h, q, :], W["identf"][:, :])
                        last.then_inc(ot_acc.sem, 1)
                    if 1 <= u <= 2 * RHP:
                        n = u - 1
                        hp, b = n // 2, n % 2
                        pe.wait_ge(a_out.sem, a_out.at(i, RET, n + 1))
                        if n >= 2:
                            pe.wait_ge(on_out.sem, on_out.at(i, RET, n - 1))
                        for h in range(2):
                            f = slice((2 * hp + h) * P, (2 * hp + h + 1) * P)
                            w = PT[:, n % 2, h, :]
                            d = pt_ps[n % 2]
                            a = h * SEQ
                            pe.matmul(d[:, a:a + P], w[:, 0:P], V[:, 2 * b, f], start=True, stop=True)
                            pe.matmul(d[:, a + P:a + SEQ], w[:, P:SEQ], V[:, 2 * b, f], start=True, stop=False)
                            last = pe.matmul(d[:, a + P:a + SEQ], w[:, SEQ:SC], V[:, 2 * b + 1, f], start=False, stop=True)
                        last.then_inc(ro_acc.sem, 1)
                pe.wait_ge(og_out.sem, og_out.at(i, RET, 2 * RHP - 1))
                output(i, RET, W["rwo"], 0)
                pe.wait_ge(og_out.sem, og_out.at(i, RET, 2 * RHP))
                output(i, RET, W["rwo"], 1, lambda: transposed(i, FFN1, 0, 0))

            def chunk(i, following):
                ffn(i, FFN0)
                retention(i)
                ffn(i, FFN1, following)

            for g in range(CB):
                transposed(0, FFN0, 0, g)
            with pe.Fori(0, NCHUNK - 1) as i:
                chunk(i, i + 1)
            chunk(NCHUNK - 1, None)

        @block.vector
        def _(dve):
            count = [0]

            def link(ins):
                count[0] += 1
                ins.then_inc(s_prep, 1)
                dve.wait_ge(s_prep, count[0])

            dve.wait_ge(s_w["const"], 16 * N_CONST)
            link(dve.tensor_scalar(ang, pos, col("theta"), None, ALU.mult))
            for j, shift in ((0, 0.25), (1, 0.0)):
                link(dve.tensor_scalar(turn, ang, float(np.float32(1 / (2 * np.pi))), shift, ALU.mult, ALU.add))
                link(dve.tensor_scalar(part, turn, MAGIC, None, ALU.add))
                link(dve.tensor_scalar(turn, part, -MAGIC, None, ALU.add))
                src = ang
                for c in (TWO_PI_1, TWO_PI_2, TWO_PI_3):
                    link(dve.scalar_tensor_tensor(out=part, in0=turn, scalar=-c, in1=src, op0=ALU.mult, op1=ALU.add))
                    src = part
                if shift:
                    link(dve.tensor_scalar(part, part, float(np.float32(np.pi / 2)), None, ALU.add))
                link(dve.tensor_scalar(reduced[j], part, PI_IN, -PI_IN, ALU.min, ALU.max))
                dve.sem_inc(s_angle, 1)
            for k, n in enumerate(order):
                dve.wait_ge(s_hi, k + 1)
                dve.scalar_tensor_tensor(out=LO[n][:, :], in0=raw[n], scalar=HD ** -0.5 if n == "wq" else 1.0,
                                         in1=HI[n][:, :].bitcast(F32), op0=ALU.mult, op1=ALU.subtract).then_inc(s_lo, 1)
            for n, v in (("identb", W["identf"][:, :]), ("maskneg", mask_in), ("sel", sel_in)):
                link(dve.tensor_copy(W[n][:, :], v))
            dve.wait_ge(s_sin, 2)
            link(dve.tensor_scalar(sinT[:, :], sinT[:, :], col("sign"), None, ALU.mult))
            link(dve.tensor_scalar(shb2h[:, :], col("shb2"), 0.5, None, ALU.mult))
            a = COL["qb"][0]
            link(dve.tensor_scalar(qbh[:, :], W["cols"][:, a:a + 2 * HP], HD ** -0.5, None, ALU.mult))
            b2 = b2x
            for j in range(3):
                link(dve.tensor_copy(b2p[j][:, :], b2))
                if j < 2:
                    link(dve.tensor_tensor(b2, b2, b2p[j][:, :], ALU.subtract))
            dve.wait_ge(s_pool0, 3)
            dve.sem_inc(s_ready, 1)
            swap = [p ^ 1 for p in range(32)]

            def table(tb):
                return tb[:, :].unsqueeze(1).broadcast_to((P, CB, SEQ))

            def by_batch(ap):
                return ap.rearrange("p (b s) -> p b s", b=CB)

            def apart():
                dve.sem_inc(s_taken, 1)

            def variance(i, layer, src, g):
                n = 2 * GT * g
                for t in tiles_of[g]:
                    dve.bn_stats(stat[:, t, :], src[:, t, :]).then_inc(n_stat.sem, 1)
                dve.wait_ge(n_stat.sem, n_stat.at(i, layer, n + GT))
                apart()
                for t in tiles_of[g]:
                    dve.bn_aggr(mv[:, t, :], stat[:, t, :]).then_inc(n_stat.sem, 1)
                dve.wait_ge(n_stat.sem, n_stat.at(i, layer, n + 2 * GT))
                mul, add = (1.0, EPS) if layer == RET else (1.0 + EPS, EPS * EPS)
                w = slice(g * GT, (g + 1) * GT)
                dve.tensor_scalar(wv_[:, w], mv[:, w, 1], mul, add, ALU.mult, ALU.add).then_inc(n_var.sem, 1)

            def normalised(i, layer, src, g):
                dve.wait_ge(n_rs.sem, n_rs.at(i, layer, g + 1))
                for t in tiles_of[g]:
                    dve.tensor_scalar(z[:, t, :], src[:, t, :], mv[:, t, 0:1], rs[:, t:t + 1],
                                      ALU.subtract, ALU.mult).then_inc(n_z.sem, 1)

            def low_part(i, layer, n, g, gamma):
                dve.wait_ge(n_hi.sem, n_hi.at(i, layer, n * CB + g + 1))
                dve.scalar_tensor_tensor(out=actL[:, batch[g]], in0=zt_ps[g], scalar=gamma,
                                         in1=actH[:, batch[g]].bitcast(F32),
                                         op0=ALU.mult, op1=ALU.subtract).then_inc(n_lo.sem, 1)

            def entry(i, layer, arrive, gamma):
                arrive(0)
                variance(i, layer, x, 0)
                normalised(i, layer, x, 0)
                arrive(1)
                variance(i, layer, x, 1)
                low_part(i, layer, 0, 0, gamma)
                normalised(i, layer, x, 1)
                low_part(i, layer, 0, 1, gamma)

            def rotate(i, layer, j):
                hp = j // 2
                cos_, sin_ = (W["rcos"], W["rsin"]) if layer == RET else (cosT, sinT)
                dve.wait_ge(qk_acc.sem, qk_acc.at(i, layer, j + 1))
                if j >= 2:
                    dve.wait_ge(qk_rot.sem, qk_rot.at(i, layer, j - 1))
                if layer == RET:
                    b, bs = 0.0, 0.0
                elif j % 2 == 0:
                    b, bs = qbh[:, hp:hp + 1], qbh[:, HP + hp:HP + hp + 1]
                else:
                    b, bs = col("kb", hp), col("kbs", hp)
                dve.scalar_tensor_tensor(out=by_batch(rc[j % 2]), in0=by_batch(proj_ps[:, :]), scalar=b, in1=table(cos_),
                                         op0=ALU.add, op1=ALU.mult)
                dve.stream_shuffle(rsw[j % 2], proj_ps[:, :], swap).then_inc(qk_read.sem, 1)
                dve.wait_ge(qk_read.sem, qk_read.at(i, layer, j + 1))
                dve.scalar_tensor_tensor(out=by_batch(rsw[j % 2]), in0=by_batch(rsw[j % 2]), scalar=bs, in1=table(sin_),
                                         op0=ALU.add, op1=ALU.mult).then_inc(qk_mul.sem, 1)

            def ffn(i, layer, following=None):
                rotate(i, layer, 0)
                rotate(i, layer, 1)
                for u in range(2 * HP + LAG):
                    n = u - LAG
                    if n >= 0:
                        dve.wait_ge(pt0.sem, pt0.at(i, layer, n + 1))
                        dve.tensor_copy(PT[:, n % 2, 0, :], pt_ps[0][:, 0:SC]).then_inc(pt0_out.sem, 1)
                    if u + 2 < 2 * HP:
                        rotate(i, layer, u + 2)
                    if u < 2 * HP:
                        dve.wait_ge(s_acc.sem, s_acc.at(i, layer, u + 1))
                        dve.tensor_reduce(negm[:, u % 2, 0, :], S[u % 2][:, :, 0:P], AX_X, ALU.max, negate=True)
                        dve.tensor_reduce(negm[:, u % 2, 1, :], S[u % 2][:, :, P:SC], AX_X, ALU.max, negate=True)\
                            .then_inc(mx.sem, 1)
                    if 1 <= u <= 2 * HP:
                        dve.wait_ge(p_exp.sem, p_exp.at(i, layer, u))
                        dve.reciprocal(rinv[:, (u - 1) % NPB, :, :], rsum[:, (u - 1) % NPB, :, :]).then_inc(p_inv.sem, 1)
                dve.wait_ge(xn_ready.sem, xn_ready.at(i, layer, 1))
                if layer == FFN0:
                    dve.wait_ge(s_out, i * 16 + 16)
                for g in range(CB):
                    w = slice(g * GT, (g + 1) * GT)
                    dve.wait_ge(o_acc.sem, o_acc.at(i, layer, g + 1))
                    dve.tensor_tensor(ao[:, w, :], by_tile(o_ps[g]), xnb[:, w, :], ALU.add).then_inc(ao_ready.sem, 1)
                    dve.wait_ge(ss_ready.sem, ss_ready.at(i, layer, g + 1))
                    dve.tensor_scalar(wv_[:, w], wv_[:, w], 1.0 / P, EPS, ALU.mult, ALU.add).then_inc(n_var.sem, 1)
                    dve.wait_ge(n_rs.sem, n_rs.at(i, layer, CB + g + 1))
                    for t in tiles_of[g]:
                        dve.tensor_scalar(z[:, t, :], ao[:, t, :], rs[:, t:t + 1], None, ALU.mult).then_inc(n_z.sem, 1)
                    low_part(i, layer, 1, g, col("g2"))

                steps = [0]

                def step(ins):
                    steps[0] += 1
                    ins.then_inc(rt_step.sem, 1)
                    dve.wait_ge(rt_step.sem, rt_step.at(i, layer, steps[0]))

                def note(ins):
                    steps[0] += 1
                    ins.then_inc(rt_step.sem, 1)

                def wide(ap):
                    return ap[:, :].unsqueeze(2).broadcast_to((P, TT, EXPERTS))

                dve.wait_ge(lg_tm.sem, lg_tm.at(i, layer, 1))
                logits = ctx_ps[:, 0:TT * SLOT].rearrange("p (t e) -> p t e", t=TT)[:, :, 0:EXPERTS]
                step(dve.tensor_reduce(lmx[:, :], logits, AX_X, ALU.max, negate=True))
                dve.tensor_tensor(lg, logits, wide(lmx), ALU.add).then_inc(lg_sub.sem, 1)
                dve.wait_ge(lg_exp.sem, lg_exp.at(i, layer, 1))
                step(dve.tensor_reduce(lsum[:, :], ex, AX_X, ALU.add))
                step(dve.reciprocal(linv[:, :], lsum[:, :]))
                step(dve.tensor_tensor(aff[:, :, 0:EXPERTS], ex, wide(linv), ALU.mult))
                apart()
                for t in range(TT):
                    note(dve.max(top[:, t, :], aff[:, t, :]))
                dve.wait_ge(rt_step.sem, rt_step.at(i, layer, steps[0]))
                step(dve.memset(top[:, :, TOPK:8], -1.0))
                apart()
                for t in range(TT):
                    note(dve.match_replace(rest[:, t, :], top[:, t, :], aff[:, t, :], 0.0))
                dve.wait_ge(rt_step.sem, rt_step.at(i, layer, steps[0]))
                step(dve.tensor_tensor(gate[:, :, 0:EXPERTS], aff[:, :, 0:EXPERTS], rest[:, :, 0:EXPERTS], ALU.subtract))
                part_ = [g3[:, :, j * SLOT:j * SLOT + EXPERTS] for j in range(3)]
                g_, r_ = gate[:, :, 0:EXPERTS], gres[:, :, 0:EXPERTS]
                step(dve.tensor_copy(part_[0], g_))
                step(dve.tensor_tensor(r_, g_, part_[0], ALU.subtract))
                step(dve.tensor_copy(part_[1], r_))
                dve.tensor_tensor(part_[2], r_, part_[1], ALU.subtract).then_inc(g_ready.sem, 1)
                assert steps[0] == rt_step.per_layer[layer], steps[0]
                dve.wait_ge(gT_acc.sem, gT_acc.at(i, layer, 1))
                dve.tensor_copy(gT[:, :], ctx_ps.bitcast(BF16)[0:3 * SLOT, 0:T]).then_inc(gT_out.sem, 1)
                for k in range(1, EXPERTS + 1):
                    dve.wait_ge(gb_acc.sem, gb_acc.at(i, layer, k))
                    dve.wait_ge(h_out.sem, h_out.at(i, layer, k + 1))
                    dve.tensor_tensor(hg[k % HP], hsb[k % AHEAD], four[2 + k % 2], ALU.mult).then_inc(hg_out.sem, 1)
                    if following is not None:
                        if k == EXPERTS // 4:
                            dve.wait_ge(s_xin, following * 16 + 16)
                            for g in range(CB):
                                variance(following, FFN0, xin, g)
                        if k == EXPERTS // 2:
                            dve.wait_ge(res_ready.sem, res_ready.at(i, layer, 1))
                            for g in range(CB):
                                normalised(following, FFN0, xin, g)
                        if k == EXPERTS - 2:
                            for g in range(CB):
                                low_part(following, FFN0, 0, g, col("g1"))
                dve.wait_ge(res_ready.sem, res_ready.at(i, layer, 1))

            def result(i, layer, dst, g):
                w = slice(g * GT, (g + 1) * GT)
                dve.wait_ge(yt_acc.sem, yt_acc.at(i, layer, g + 1))
                dve.tensor_tensor(dst[:, w, :], by_tile(yt_ps[g]), res[:, w, :], ALU.add).then_inc(x_new.sem, 1)
                dve.wait_ge(x_new.sem, x_new.at(i, layer, g + 1))

            def retained(i, g):
                w = slice(g * GT, (g + 1) * GT)
                dve.wait_ge(o_acc.sem, o_acc.at(i, RET, g + 1))
                dve.tensor_tensor(x[:, w, :], by_tile(o_ps[g]), x[:, w, :], ALU.add).then_inc(x_new.sem, 1)
                dve.wait_ge(x_new.sem, x_new.at(i, RET, g + 1))

            def retention(i):
                rotate(i, RET, 0)
                rotate(i, RET, 1)
                for u in range(2 * RHP + 1):
                    if u + 2 < 2 * RHP:
                        rotate(i, RET, u + 2)
                    if u < 2 * RHP:
                        hp = u // 2
                        dve.wait_ge(s_acc.sem, s_acc.at(i, RET, u + 1))
                        dec = W["decay"][:, :].rearrange("p (h s) -> p h s", h=RHEADS)[:, 2 * hp:2 * hp + 2, :]
                        dve.tensor_tensor(PT[:, u % 2, :, 0:SEQ], S[u % 2][:, :, 0:SEQ], dec, ALU.mult)
                        dve.tensor_tensor(PT[:, u % 2, :, SEQ:SC], S[u % 2][:, :, SEQ:SC], dec[:, :, 0:P], ALU.mult)\
                            .then_inc(a_out.sem, 1)
                    if 1 <= u <= 2 * RHP:
                        n = u - 1
                        dve.wait_ge(ro_acc.sem, ro_acc.at(i, RET, n + 1))
                        for hq in range(4):
                            dve.bn_stats(rstat[:, n % 2, hq, :], pt_ps[n % 2][:, hq * P:(hq + 1) * P]).then_inc(ro_stat.sem, 1)
                        dve.wait_ge(ro_stat.sem, ro_stat.at(i, RET, 8 * n + 4))
                        apart()
                        for hq in range(4):
                            dve.bn_aggr(rmv[:, n % 2, hq, :], rstat[:, n % 2, hq, :]).then_inc(ro_stat.sem, 1)
                        dve.wait_ge(ro_stat.sem, ro_stat.at(i, RET, 8 * n + 8))
                        dve.tensor_scalar(rnm[:, n % 2, :], rmv[:, n % 2, :, 0], -1.0, None, ALU.mult)
                        dve.tensor_scalar(rw_[:, n % 2, :], rmv[:, n % 2, :, 1], 1.0, EPS, ALU.mult, ALU.add)\
                            .then_inc(ro_var.sem, 1)

            def chunk(i, following):
                ffn(i, FFN0)
                entry(i, RET, lambda g: result(i, FFN0, x, g), 1.0)
                retention(i)
                entry(i, FFN1, lambda g: retained(i, g), col("g1"))
                ffn(i, FFN1, following)
                for g in range(CB):
                    result(i, FFN1, xout, g)

            dve.wait_ge(s_xin, 16)
            for g in range(CB):
                variance(0, FFN0, xin, g)
            for g in range(CB):
                normalised(0, FFN0, xin, g)
            for g in range(CB):
                low_part(0, FFN0, 0, g, col("g1"))
            with dve.Fori(0, NCHUNK - 1) as i:
                chunk(i, i + 1)
            chunk(NCHUNK - 1, None)


def shape_constants():
    f = np.float32
    c = {"identf": np.eye(P, dtype=f), }
    rows = np.arange(P)
    c["maskneg"] = np.where(rows[None, :] > rows[:, None], -1e30, 0.0).astype(f)
    sel = np.zeros((3 * SLOT, SLOT), f)
    for j in range(3):
        sel[j * SLOT + np.arange(EXPERTS), np.arange(EXPERTS)] = 1
    c["sel"] = sel
    c["pos"] = np.broadcast_to(np.arange(SEQ, dtype=f), (P, SEQ)).copy()
    gamma = f(1) - np.exp2(f(-5) - np.arange(RHEADS, dtype=f))
    s = np.log2(gamma).astype(f)
    rel = (np.arange(SEQ, dtype=f)[None, :] - rows[:, None].astype(f))
    d = np.where(rel[:, None, :] >= 0, np.exp2(rel[:, None, :] * s[None, :, None]), f(0)) * f(HD ** -0.5)
    c["decay"] = d.astype(f).reshape(P, RHEADS * SEQ)
    inv = (f(1) / np.power(f(10000), np.arange(0, HD, 2, dtype=f) / f(HD))).astype(f)
    ang = (np.arange(SEQ, dtype=f)[None, :] * inv[:, None]).astype(f)
    sign = np.where(rows % 2 == 0, -1, 1).astype(f)
    pair = (rows % HD) // 2
    c["rcos"] = np.cos(ang)[pair].astype(f)
    c["rsin"] = (np.sin(ang)[pair] * sign[:, None]).astype(f)
    return c, sign


def kernel(**inputs):
    import concourse.bacc as bacc
    from concourse.bass_utils import run_bass_kernel_spmd

    a = {k.replace("L0_ffn_", "f_").replace("L0_attn_", "r_"): np.asarray(v) for k, v in inputs.items()}
    arrays, sign = shape_constants()
    pairs = lambda v: v.reshape(-1, P).T
    by_pair = lambda w: w.reshape(-1, P, P).transpose(1, 0, 2).reshape(P, -1)
    swap = np.arange(P) ^ 1
    arrays["wq"], arrays["wk"], arrays["wv"] = a["f_q_w"], a["f_k_w"], a["f_v_w"]
    router = np.zeros((P, P), np.float32)
    router[:, :EXPERTS] = a["f_router_w"]
    arrays["router"] = router
    arrays["shw1"], arrays["shw2"] = a["f_sh_w1"], a["f_sh_w2"]
    arrays["rew1"] = a["f_re_w1"].transpose(1, 0, 2).reshape(P, -1)
    arrays["rew2"] = a["f_re_w2"].transpose(1, 0, 2).reshape(P, -1)
    arrays["ow"] = by_pair(a["f_o_w"])
    mix = np.arange(RFEAT).reshape(RHEADS, 2, HD // 2).transpose(0, 2, 1).reshape(-1)
    arrays["rwq"], arrays["rwk"] = a["r_Wq"][mix].T, a["r_Wk"][mix].T
    arrays["rwv"], arrays["rwg"] = a["r_Wv"].T, a["r_Wg"].T
    arrays["rwo"] = by_pair(a["r_Wo"].T)
    for name, key in (("g1row", "f_gamma1"), ("g2row", "f_gamma2"), ("obrow", "f_o_b")):
        arrays[name] = np.broadcast_to(a[key][None, :], (P, P))
    b2x = np.zeros((3, SLOT, P), np.float32)
    b2x[:, :EXPERTS] = a["f_re_b2"][None]
    arrays["b2x"] = b2x.reshape(3 * SLOT, P)
    rb = np.zeros((P, 1), np.float32)
    rb[:EXPERTS, 0] = a["f_router_b"]
    vec = {"g1": a["f_gamma1"][:, None], "g2": a["f_gamma2"][:, None],
           "qb": pairs(a["f_q_b"]), "qbs": pairs(a["f_q_b"])[swap], "kb": pairs(a["f_k_b"]),
           "kbs": pairs(a["f_k_b"])[swap], "vb": pairs(a["f_v_b"]), "shb1": a["f_sh_b1"][:, None],
           "shb2": a["f_sh_b2"][:, None], "reb1": a["f_re_b1"].T, "gnw": pairs(a["r_gn_weight"]),
           "gnb": pairs(a["r_gn_bias"]), "rb": rb, "theta": a["f_theta"][(np.arange(P) % HD) // 2][:, None],
           "sign": sign[:, None]}
    cols = np.zeros((P, LOADED["cols"][1]), np.float32)
    for n, (at, w) in COL.items():
        cols[:, at:at + w] = vec[n]
    arrays["cols"] = cols

    nc = bacc.Bacc("TRN2", target_bir_lowering=False, num_devices=1)
    feeds, ins = {}, {}
    arrays["x"] = a["r_x"].reshape(NTOK, P)
    for n, v in arrays.items():
        v = np.ascontiguousarray(v)
        feeds["in_" + n] = v
        ins[n] = nc.dram_tensor("in_" + n, v.shape, mybir.dt.from_np(v.dtype), kind="ExternalInput").ap()
    out = nc.dram_tensor("out_x", (NTOK, P), F32, kind="ExternalOutput").ap()
    build(nc, ins["x"], ins, out)
    r = run_bass_kernel_spmd(nc, [feeds], core_ids=[0])
    return r.results[0]["out_x"].reshape(16, SEQ, P)
```

```python
from contextlib import ExitStack

import concourse.bass as bass
import numpy as np
from concourse import mybir
from concourse.alu_op_type import AluOpType as ALU

F32 = mybir.dt.float32
F32R = mybir.dt.float32r
BF16 = mybir.dt.bfloat16
ACT = mybir.ActivationFunctionType
AX_X = mybir.AxisListType.X

P = 128
SEQ = 256
NTOK = 16 * SEQ
CB = 2
T = CB * SEQ
TT = T // P
NCHUNK = NTOK // T
HD = 64
HEADS = 16
HP = HEADS // 2
RHEADS = 8
RHP = RHEADS // 2
FEAT = HEADS * HD
RFEAT = RHEADS * HD
EXPERTS = 31
SLOT = 32
TOPK = 3
AW = 40
EPS = 1e-5
SC = SEQ + P
RLAG = 3
LAG = 3
NPB = LAG + 1
FFN0, RET, FFN1 = range(3)
GT = TT // CB
QK_FIRST = 4
GATES_FIRST = RHEADS - 2
MIDWAY = (2 * GT - 1) * HP // 2
AHEAD = 10
FIRST = 5
LEAD = 5
LATE = 11


class Signal:

    def __init__(self, sem, per_layer):
        self.sem, self.per_layer = sem, per_layer
        self.per_chunk = sum(per_layer)

    def at(self, i, layer, n):
        return i * self.per_chunk + (sum(self.per_layer[:layer]) + n)


LOADED = {
    "ow": (P, HP * P), "rwo": (P, RHEADS * P), "shw2": (P, P), "rew2": (P, EXPERTS * P),
    "decay": (P, RHEADS * SEQ), "rcos": (P, SEQ), "rsin": (P, SEQ),
    "identf": (P, P), "g1row": (P, P), "g2row": (P, P), "obrow": (P, P),
    "cols": (P, 100),
}
IN_BF16 = {"identb": (P, P), "maskneg": (P, P), "sel": (3 * SLOT, SLOT)}
SPLIT = {
    "wq": FEAT, "wk": FEAT, "wv": FEAT, "router": P, "shw1": P,
    "rwq": RFEAT, "rwk": RFEAT, "rwv": FEAT, "rwg": FEAT, "rew1": EXPERTS * P,
}
COL = {}
_at = 0
for _n, _w in (("g1", 1), ("g2", 1), ("qb", HP), ("qbs", HP), ("kb", HP), ("kbs", HP), ("vb", HP),
               ("shb1", 1), ("shb2", 1), ("reb1", EXPERTS), ("gnw", RHEADS), ("gnb", RHEADS),
               ("rb", 1), ("theta", 1), ("sign", 1)):
    COL[_n] = (_at, _w)
    _at += _w
COLS = _at

TWO_PI_1 = 6.28125
TWO_PI_2 = float(np.float32(np.round((2 * np.pi - TWO_PI_1) * 2**21) / 2**21))
TWO_PI_3 = float(np.float32(2 * np.pi - TWO_PI_1 - TWO_PI_2))
MAGIC = 12582912.0
PI_IN = 3.1415925


def build(nc, x_in, ins, out):
    ctx = ExitStack()
    with ctx:
        def sb(name, shape, dt=F32):
            return ctx.enter_context(nc.sbuf_tensor(name, list(shape), dt))

        def sem(name):
            return ctx.enter_context(nc.semaphore(name))

        def signal(name, ffn=0, ret=0):
            return Signal(sem(name), [ffn, ret, ffn])

        W = {n: sb("c_" + n, s) for n, s in LOADED.items()}
        W.update({n: sb("c_" + n, s, BF16) for n, s in IN_BF16.items()})
        HI = {n: sb("hi_" + n, (P, c), F32R) for n, c in SPLIT.items()}
        LO = {n: sb("lo_" + n, (P, c), F32R) for n, c in SPLIT.items()}
        cosT, sinT = sb("cosT", (P, SEQ)), sb("sinT", (P, SEQ))
        b2p = [sb(f"b2p{j}", (3 * SLOT, P), BF16) for j in range(3)]
        half_neg = sb("half_neg", (P, TT))
        shb2h = sb("shb2h", (P, 1))
        qbh = sb("qbh", (P, 2 * HP))

        def col(name, k=0):
            a = COL[name][0] + k
            return W["cols"][:, a:a + 1]

        xin = sb("xin", (P, TT, P))
        x = sb("x", (P, TT, P))
        actH, actL = sb("actH", (P, T), F32R), sb("actL", (P, T), F32R)
        V = sb("V", (P, TT, FEAT))
        C = sb("C", (P, HP, T))
        G = sb("G", (P, NPB * 2 * SC))
        E_ = sb("E", (P, 8 * T))
        N_ = sb("N", (P, 4 * T))
        pos, b2x = N_[:, 5 * SEQ:6 * SEQ], N_[0:3 * SLOT, 6 * SEQ:6 * SEQ + P]
        PT = sb("PT", (P, 2, 2, SC))
        stat = sb("stat", (P, TT, 6))
        mv = sb("mv", (P, TT, 2))
        wv_, rs = sb("wv", (P, TT)), sb("rs", (P, TT))
        negm = sb("negm", (P, 2, 2, 2))
        rsum = sb("rsum", (P, NPB, 2, 2))
        rinv = sb("rinv", (P, NPB, 2, 2))
        rstat = sb("rstat", (P, 3, 4, 6))
        rmv = sb("rmv", (P, 3, 4, 2))
        rw_, rrs = sb("rw", (P, 3, 4)), sb("rrs", (P, 3, 4))
        rnm, rnb = sb("rnm", (P, 3, 4)), sb("rnb", (P, 3, 4))
        aff = sb("aff", (P, TT, AW))
        rest = sb("rest", (P, TT, AW))
        top = sb("top", (P, TT, 8))
        lmx, lsum, linv = sb("lmx", (P, TT)), sb("lsum", (P, TT)), sb("linv", (P, TT))
        g3 = sb("g3", (P, TT, 3 * SLOT), BF16)
        gT = sb("gT", (3 * SLOT, T), BF16)

        prob = G[:, :].rearrange("p (u h s) -> p u h s", u=NPB, h=2)
        qT = [E_[:, k * T:(k + 1) * T] for k in (0, 1)]
        kT = [E_[:, k * T:(k + 1) * T] for k in (2, 3)]
        rc = [E_[:, k * T:(k + 1) * T] for k in (4, 5)]
        rsw = [E_[:, k * T:(k + 1) * T] for k in (6, 7)]
        rqk = [E_[:, k * T:(k + 1) * T] for k in range(2 * RHP)]
        rrc = [G[:, k * T:(k + 1) * T] for k in (0, 1)]
        rrsw = [G[:, k * T:(k + 1) * T] for k in (2, 3)]
        hsb = [V[:, k // 2, (k % 2) * T:(k % 2 + 1) * T] for k in range(2 * TT)]
        hsb += [E_[:, k * T:(k + 1) * T] for k in range(AHEAD - 2 * TT)]
        hg = [C[:, k, :] for k in range(HP)]
        hg += [E_[:, k * T:(k + 1) * T] for k in range(AHEAD - 2 * TT, 5)]
        yT = E_[:, 5 * T:6 * T]
        lgT = E_[0:SLOT, 6 * T:7 * T]
        small = E_[:, 7 * T:8 * T]
        lg = small[:, 0:TT * EXPERTS].rearrange("p (t e) -> p t e", t=TT)
        ex = small[:, P:P + TT * EXPERTS].rearrange("p (t e) -> p t e", t=TT)
        gate = small[:, 2 * P:3 * P].rearrange("p (t e) -> p t e", t=TT)
        gres = small[:, 3 * P:4 * P].rearrange("p (t e) -> p t e", t=TT)
        tiles = lambda k: N_[:, k * T:(k + 1) * T].rearrange("p (t d) -> p t d", t=TT)
        xnb, ao, res, z = tiles(0), tiles(1), tiles(2), tiles(3)
        xout = tiles(1)
        onrm = [N_[:, k * T:(k + 1) * T].rearrange("p (h q v) -> p h q v", h=2, q=2) for k in (0, 1)]
        og_in = [N_[:, k * T:(k + 1) * T].rearrange("p (h s) -> p h s", h=2) for k in (2, 3)]

        BK = [ctx.enter_context(nc.psum_tensor(f"bank{j}", [P, 512], F32)) for j in range(2)]
        SP2 = ctx.enter_context(nc.psum_tensor("scores", [P, 4, 512], F32))
        PT2 = ctx.enter_context(nc.psum_tensor("transposes", [P, 2, 512], F32))
        proj_ps, ctx_ps = BK
        S = [SP2[:, 0:2, :], SP2[:, 2:4, :]]
        four = [SP2[:, j, :] for j in range(4)]
        pt_ps = [PT2[:, j, :] for j in range(2)]
        batch = [slice(g * SEQ, (g + 1) * SEQ) for g in range(CB)]
        tiles_of = [range(g * GT, (g + 1) * GT) for g in range(CB)]
        zt_ps = [proj_ps[:, 0:SEQ], ctx_ps[:, 0:SEQ]]
        o_ps = [four[2 * g][:, 0:SEQ] for g in range(CB)]
        y_ps = [pt_ps[g][:, 0:SEQ] for g in range(CB)]
        yt_ps = y_ps
        by_tile = lambda ap: ap.rearrange("p (t d) -> p t d", t=GT)

        h_bank = [0, 1, 3, 4, 5, 2, 6, 0, 1, 3] + [k % 2 for k in range(AHEAD, EXPERTS + 1)]
        h_ps = lambda k: (four + pt_ps + [proj_ps[:, :]])[h_bank[k]]
        gate_bank = lambda k: 2 + (k + 1) % 2
        h_before = lambda k: max((n for n in range(k) if h_bank[n] == h_bank[k]), default=None)
        gate_ps = lambda c: four[(c + 2) % 4] if c < GATES_FIRST else four[1 + 2 * (c - GATES_FIRST)]
        ro_ps = pt_ps + [proj_ps[:, :]]
        qk_ps = lambda layer, j: ctx_ps if j % 2 and (layer == RET or j < QK_FIRST) else proj_ps

        def qk_bank(layer, j, g):
            if g is None:
                return qk_ps(layer, j)[:, :]
            return ((proj_ps, ctx_ps), pt_ps)[j][g][:, 0:SEQ]

        def qk_n(layer, j, g=None):
            if layer == FFN0:
                return j + 1
            return 2 * (0 if g == 0 else 1) + j + 1 if j < 2 else j + 3

        s_const, s_late = sem("s_const"), sem("s_late")
        s_stage = [sem(f"s_stage{j}") for j in range(3)]
        s_hi = sem("s_hi")
        s_lo = sem("s_lo")
        s_prep = sem("s_prep")
        s_angle = sem("s_angle")
        s_sin = sem("s_sin")
        s_ready = sem("s_ready")
        s_pool0 = sem("s_pool0")
        s_taken, s_taken_pe, s_taken_pool = sem("s_taken"), sem("s_taken_pe"), sem("s_taken_pool")
        s_xin = sem("s_xin")
        s_out = sem("s_out")

        n_stat = Signal(sem("n_stat"), [2 * TT, 2 * TT, 2 * TT])
        by_batch_and_norm = [2 * CB, CB, 2 * CB]
        n_var = Signal(sem("n_var"), by_batch_and_norm)
        n_rs = Signal(sem("n_rs"), by_batch_and_norm)
        n_z = Signal(sem("n_z"), [2 * TT, TT, 2 * TT])
        n_zT = Signal(sem("n_zT"), by_batch_and_norm)
        n_hi = Signal(sem("n_hi"), by_batch_and_norm)
        n_lo = Signal(sem("n_lo"), by_batch_and_norm)
        x_new = Signal(sem("x_new"), [CB, CB, CB])
        xn_step = signal("xn_step", 1)
        xn_ready = signal("xn_ready", 1)
        ao_ready = signal("ao_ready", CB)
        ss_ready = signal("ss_ready", CB)
        res_step = signal("res_step", 3)
        res_ready = signal("res_ready", 1)
        v_acc, v_out = signal("v_acc", 2 * TT, 4 * TT), signal("v_out", 2 * TT, 4 * TT)
        by_qk = [2 * HP, 2 * RHP + 2, 2 * HP + 2]
        qk_acc = Signal(sem("qk_acc"), by_qk)
        qk_read = Signal(sem("qk_read"), by_qk)
        qk_mul = Signal(sem("qk_mul"), by_qk)
        qk_rot = Signal(sem("qk_rot"), by_qk)
        s_acc = signal("s_acc", 2 * HP, 2 * RHP)
        mx = signal("mx", 2 * HP)
        p_exp = signal("p_exp", 2 * HP)
        p_inv = signal("p_inv", 2 * HP)
        p_norm = signal("p_norm", 2 * HP)
        pt, pt_out = signal("pt", 2 * HP), signal("pt_out", 2 * HP)
        c_acc, c_out = signal("c_acc", 2 * HP), signal("c_out", 2 * HP)
        o_acc = signal("o_acc", CB, CB)
        lg_acc, lg_out = signal("lg_acc", 1), signal("lg_out", 1)
        lg_tm = signal("lg_tm", 1)
        rt_step = signal("rt_step", 17)
        lg_sub, lg_exp = signal("lg_sub", 1), signal("lg_exp", 1)
        g_ready, gT_acc, gT_out = signal("g_ready", 1), signal("gT_acc", 1), signal("gT_out", 1)
        h_acc, h_out = signal("h_acc", EXPERTS + 1), signal("h_out", EXPERTS + 1)
        gb_acc, hg_out = signal("gb_acc", EXPERTS), signal("hg_out", EXPERTS)
        y_acc, y_out, yt_acc = signal("y_acc", CB), signal("y_out", CB), signal("yt_acc", CB)
        a_out = signal("a_out", 0, 2 * RHP)
        ro_acc = signal("ro_acc", 0, 2 * RHP)
        ro_stat = signal("ro_stat", 0, 16 * RHP)
        ro_var, ro_rs = signal("ro_var", 0, 2 * RHP), signal("ro_rs", 0, 4 * RHP)
        on_out = signal("on_out", 0, 2 * RHP)
        ot_acc, ot_out = signal("ot_acc", 0, 2 * RHP), signal("ot_out", 0, 2 * RHP)
        og_out = signal("og_out", 0, 2 * RHP)

        reduced = [N_[:, 0:SEQ], N_[:, SEQ:2 * SEQ]]
        ang, turn, part = N_[:, 2 * SEQ:3 * SEQ], N_[:, 3 * SEQ:4 * SEQ], N_[:, 4 * SEQ:5 * SEQ]

        mask_in, sel_in = E_[:, 0:P], E_[0:3 * SLOT, P:P + SLOT]
        room = [G[:, :], E_[:, 2 * P:4 * P], V[:, :, :].rearrange("p t f -> p (t f)"),
                C[:, :, :].rearrange("p h t -> p (h t)")]

        x_v = x_in.rearrange("(c t p) d -> c p t d", t=TT, p=P)
        out_v = out.rearrange("(c t p) d -> c p t d", t=TT, p=P)

        block = ctx.enter_context(nc.Block())

        place = {"wq": (0, 0), "wk": (0, FEAT), "wv": (0, 2 * FEAT), "router": (1, 0), "shw1": (1, P),
                 "rwq": (2, 0), "rwk": (2, RFEAT), "rwv": (2, 2 * RFEAT), "rwg": (2, 2 * RFEAT + FEAT),
                 "rew1": (3, 0)}
        order = list(SPLIT)
        raw = {n: room[r][:, o:o + SPLIT[n]] for n, (r, o) in place.items()}
        late = ("ow", "shw2", "decay", "rwo", "rew2")
        N_CONST = len(LOADED) - len(late) + 4

        @block.sync
        def _(sp):
            for n in order[:3]:
                sp.dma_start(raw[n], ins[n]).then_inc(s_stage[0], 16)
            sp.dma_start(pos, ins["pos"]).then_inc(s_const, 16)
            sp.dma_start(b2x, ins["b2x"]).then_inc(s_const, 16)
            sp.dma_start(mask_in, ins["maskneg"]).then_inc(s_const, 16)
            sp.dma_start(sel_in, ins["sel"]).then_inc(s_const, 16)
            for n in LOADED:
                if n not in late:
                    sp.dma_start(W[n][:, :], ins[n]).then_inc(s_const, 16)
            sp.dma_start(xin[:, :, :], x_v[0]).then_inc(s_xin, 16)
            for n in order[3:9]:
                sp.dma_start(raw[n], ins[n]).then_inc(s_stage[1], 16)
            sp.dma_start(raw["rew1"], ins["rew1"]).then_inc(s_stage[2], 16)
            for n in late:
                sp.dma_start(W[n][:, :], ins[n]).then_inc(s_late, 16)
            sp.sem_inc(s_out, 16)
            with sp.Fori(0, NCHUNK - 1) as i:
                sp.wait_ge(res_ready.sem, res_ready.at(i, FFN0, 1))
                sp.dma_start(xin[:, :, :], x_v[i + 1]).then_inc(s_xin, 16)
                sp.wait_ge(x_new.sem, x_new.at(i, FFN1, CB))
                sp.dma_start(out_v[i], xout).then_inc(s_out, 16)
            sp.wait_ge(x_new.sem, x_new.at(NCHUNK - 1, FFN1, CB))
            sp.dma_start(out_v[NCHUNK - 1], xout).then_inc(s_out, 16)
            sp.wait_ge(s_out, 16 * (NCHUNK + 1))

        @block.gpsimd
        def _(pool):
            pool.memset(half_neg[:, :], -0.5).then_inc(s_pool0, 1)
            pool.memset(g3[:, :, :], 0.0).then_inc(s_pool0, 1)
            pool.memset(aff[:, :, :], -1.0).then_inc(s_pool0, 1)
            pool.wait_ge(s_const, 16 * N_CONST)
            pool.wait_ge(s_pool0, 3)

            def row(name):
                r = W[name]
                return r[:, :].unsqueeze(1).broadcast_to((P, TT, P))

            def rsqrt(i, layer, n):
                for g in range(CB):
                    w = slice(g * GT, (g + 1) * GT)
                    pool.wait_ge(n_var.sem, n_var.at(i, layer, n * CB + g + 1))
                    pool.tensor_tensor(rs[:, w], wv_[:, w], half_neg[:, w], ALU.pow).then_inc(n_rs.sem, 1)

            def rotated(i, layer, j, g=None):
                hp = j // 2
                pool.wait_ge(qk_mul.sem, qk_mul.at(i, layer, qk_n(layer, j, g)))
                if layer == RET:
                    dst, a, b = rqk[j], rrc[j % 2], rrsw[j % 2]
                else:
                    dst, a, b = (qT, kT)[j % 2][hp % 2], rc[j % 2], rsw[j % 2]
                    if hp >= 2:
                        pool.wait_ge(s_acc.sem, s_acc.at(i, layer, 2 * (hp - 1)))
                w = slice(0, T) if g is None else batch[g]
                pool.tensor_tensor(dst[:, w], a[:, w], b[:, w], ALU.add).then_inc(qk_rot.sem, 1)

            def first_halves(i, layer):
                for g in range(CB):
                    for j in range(2):
                        rotated(i, layer, j, g)

            def ffn(i, layer, src, following=None):
                if layer == FFN1:
                    rsqrt(i, FFN1, 0)
                    first_halves(i, layer)
                for j in range(0 if layer == FFN0 else 2, QK_FIRST):
                    rotated(i, layer, j)
                for u in range(2 * HP + 1):
                    if QK_FIRST - 2 <= u < 2 * HP - 2:
                        rotated(i, layer, u + 2)
                    if u >= 1:
                        n = u - 1
                        pool.wait_ge(p_inv.sem, p_inv.at(i, layer, n + 1))
                        pool.sem_inc(s_taken_pool, 1)
                        for h in range(2):
                            for q, (a, b) in enumerate(((0, P), (P, SC))):
                                w = prob[:, n % NPB, h, a:b]
                                last = pool.tensor_scalar(w, w, rinv[:, n % NPB, q, h:h + 1], 1.0, ALU.mult, ALU.mult)
                        last.then_inc(p_norm.sem, 1)
                pool.wait_ge(n_z.sem, n_z.at(i, layer, TT))
                pool.tensor_tensor(xnb, z, row("g1row"), ALU.mult).then_inc(xn_step.sem, 1)
                pool.wait_ge(xn_step.sem, xn_step.at(i, layer, 1))
                pool.tensor_tensor(xnb, xnb, row("obrow"), ALU.add).then_inc(xn_ready.sem, 1)
                rsqrt(i, layer, 1)
                pool.wait_ge(n_z.sem, n_z.at(i, layer, 2 * TT))
                pool.tensor_tensor(res, z, row("g2row"), ALU.mult).then_inc(res_step.sem, 1)
                pool.wait_ge(res_step.sem, res_step.at(i, layer, 1))
                pool.tensor_tensor(res, res, ao, ALU.add).then_inc(res_step.sem, 1)
                pool.wait_ge(res_step.sem, res_step.at(i, layer, 2))
                pool.sem_inc(s_taken_pool, 1)
                pool.tensor_scalar(res, res, 0.5, 1.0, ALU.mult, ALU.mult).then_inc(res_step.sem, 1)
                pool.wait_ge(res_step.sem, res_step.at(i, layer, 3))
                pool.tensor_tensor(res, res, src[:, :, :], ALU.add).then_inc(res_ready.sem, 1)
                if following is not None:
                    rsqrt(following, FFN0, 0)

            def retention(i):
                rsqrt(i, RET, 0)
                first_halves(i, RET)
                for j in range(2, 2 * RHP):
                    rotated(i, RET, j)
                for u in range(2 * RHP + RLAG):
                    if 1 <= u <= 2 * RHP:
                        n = u - 1
                        pool.wait_ge(ro_var.sem, ro_var.at(i, RET, n + 1))
                        pool.tensor_tensor(rrs[:, n % 3, :], rw_[:, n % 3, :], half_neg[:, :], ALU.pow)\
                            .then_inc(ro_rs.sem, 1)
                        pool.wait_ge(ro_rs.sem, ro_rs.at(i, RET, 2 * n + 1))
                        pool.tensor_tensor(rnb[:, n % 3, :], rnm[:, n % 3, :], rrs[:, n % 3, :], ALU.mult)\
                            .then_inc(ro_rs.sem, 1)
                    if u >= RLAG:
                        n = u - RLAG
                        hp, b = n // 2, n % 2
                        pool.wait_ge(ot_out.sem, ot_out.at(i, RET, n + 1))
                        for h in range(2):
                            c = C[:, 2 * hp + h, b * SEQ:(b + 1) * SEQ]
                            last = pool.tensor_tensor(c, og_in[n % 2][:, h, :], c, ALU.mult)
                        last.then_inc(og_out.sem, 1)

            def chunk(i, following):
                ffn(i, FFN0, xin)
                retention(i)
                ffn(i, FFN1, x, following)

            rsqrt(0, FFN0, 0)
            with pool.Fori(0, NCHUNK - 1) as i:
                chunk(i, i + 1)
            chunk(NCHUNK - 1, None)

        @block.scalar
        def _(act):
            act.wait_ge(s_const, 16 * N_CONST)
            def high_weights(k):
                n = order[k]
                act.activation(HI[n][:, :], raw[n], ACT.Copy, scale=HD ** -0.5 if n == "wq" else 1.0).then_inc(s_hi, 1)

            act.wait_ge(s_stage[0], 16 * 3)
            for k in range(3):
                high_weights(k)
            act.wait_ge(s_angle, 2)
            act.activation(cosT[:, :], reduced[0], ACT.Sin).then_inc(s_sin, 1)
            act.activation(sinT[:, :], reduced[1], ACT.Sin).then_inc(s_sin, 1)
            act.wait_ge(s_stage[1], 16 * 6)
            for k in range(3, 9):
                high_weights(k)

            def high_part(i, layer, n, g, gamma):
                act.wait_ge(n_zT.sem, n_zT.at(i, layer, n * CB + g + 1))
                act.activation(actH[:, batch[g]], zt_ps[g], ACT.Copy, scale=gamma).then_inc(n_hi.sem, 1)

            def values(i, layer, gamma=1.0):
                for j in range(2 * TT):
                    if j < CB and layer != FFN0:
                        high_part(i, layer, 0, j, gamma)
                    act.wait_ge(v_acc.sem, v_acc.at(i, layer, j + 1))
                    act.activation(V[:, j // 2, (j % 2) * 512:(j % 2 + 1) * 512], four[j % 4], ACT.Copy)\
                        .then_inc(v_out.sem, 1)

            def ffn(i, layer, following=None):
                def context_out(n):
                    act.wait_ge(c_acc.sem, c_acc.at(i, layer, n + 1))
                    act.activation(C[:, n // 2, (n % 2) * SEQ:(n % 2 + 1) * SEQ], ctx_ps[:, 0:SEQ], ACT.Identity,
                                   bias=col("vb", n // 2)).then_inc(c_out.sem, 1)

                values(i, layer, col("g1"))
                for u in range(2 * HP + LAG + 1):
                    n, m = u - LAG, u - LAG - 1
                    if n == 2 * HP - 1:
                        context_out(m)
                    if 0 <= n < 2 * HP:
                        act.wait_ge(pt.sem, pt.at(i, layer, n + 1))
                        act.activation(PT[:, n % 2, :, :], PT2[:, :, 0:SC], ACT.Copy).then_inc(pt_out.sem, 1)
                    if m >= 0 and n != 2 * HP - 1:
                        context_out(m)
                    if u < 2 * HP:
                        act.wait_ge(mx.sem, mx.at(i, layer, u + 1))
                        for h in range(2):
                            for q, (a, b) in enumerate(((0, P), (P, SC))):
                                last = act.activation(prob[:, u % NPB, h, a:b], S[u % 2][:, h, a:b], ACT.Exp,
                                                      bias=negm[:, u % 2, q, h:h + 1],
                                                      accum_out=rsum[:, u % NPB, q, h:h + 1])
                        last.then_inc(p_exp.sem, 1)
                for g in range(CB):
                    act.wait_ge(ao_ready.sem, ao_ready.at(i, layer, g + 1))
                    for t in tiles_of[g]:
                        last = act.activation(z[:, t, :], ao[:, t, :], ACT.Square, accum_out=wv_[:, t:t + 1])
                    last.then_inc(ss_ready.sem, 1)
                    high_part(i, layer, 1, g, col("g2"))
                act.wait_ge(lg_acc.sem, lg_acc.at(i, layer, 1))
                act.activation(lgT, proj_ps[0:SLOT, :], ACT.Identity, bias=W["cols"][0:SLOT, COL["rb"][0]:COL["rb"][0] + 1])\
                    .then_inc(lg_out.sem, 1)
                act.wait_ge(lg_sub.sem, lg_sub.at(i, layer, 1))
                act.activation(ex, lg, ACT.Exp).then_inc(lg_exp.sem, 1)
                for k in range(EXPERTS + 1):
                    act.wait_ge(h_acc.sem, h_acc.at(i, layer, k + 1))
                    if k > AHEAD:
                        act.wait_ge(hg_out.sem, hg_out.at(i, layer, k - AHEAD))
                    act.activation(hsb[k % AHEAD], h_ps(k), ACT.Gelu,
                                   bias=col("shb1") if k == 0 else col("reb1", k - 1)).then_inc(h_out.sem, 1)
                if following is not None:
                    for g in range(CB):
                        high_part(following, FFN0, 0, g, col("g1"))
                for g in range(CB):
                    act.wait_ge(y_acc.sem, y_acc.at(i, layer, g + 1))
                    act.activation(yT[:, batch[g]], y_ps[g], ACT.Identity, bias=shb2h[:, 0:1], scale=0.5)\
                        .then_inc(y_out.sem, 1)

            def retention(i):
                values(i, RET)

                def gates(c):
                    act.wait_ge(v_acc.sem, v_acc.at(i, RET, 2 * TT + c + 1))
                    act.activation(C[:, c, :], gate_ps(c), ACT.Silu).then_inc(v_out.sem, 1)

                for c in range(GATES_FIRST):
                    gates(c)
                for u in range(2, 2 * RHP + RLAG):
                    if u - 2 < 2 * RHP:
                        n = u - 2
                        act.wait_ge(ro_rs.sem, ro_rs.at(i, RET, 2 * n + 2))
                        for hq in range(4):
                            last = act.activation(onrm[n % 2][:, hq // 2, hq % 2, :], ro_ps[n % 3][:, hq * P:(hq + 1) * P],
                                                  ACT.Identity, bias=rnb[:, n % 3, hq:hq + 1], scale=rrs[:, n % 3, hq:hq + 1])
                        last.then_inc(on_out.sem, 1)
                    if 2 * RHP <= u < 2 * RHP + RHEADS - GATES_FIRST:
                        gates(GATES_FIRST + u - 2 * RHP)
                    if u >= RLAG:
                        n = u - RLAG
                        act.wait_ge(ot_acc.sem, ot_acc.at(i, RET, n + 1))
                        if n >= 2:
                            act.wait_ge(og_out.sem, og_out.at(i, RET, n - 1))
                        for h in range(2):
                            c = 2 * (n // 2) + h
                            last = act.activation(og_in[n % 2][:, h, :], ctx_ps[:, h * SEQ:(h + 1) * SEQ], ACT.Identity,
                                                  bias=col("gnb", c), scale=col("gnw", c))
                        last.then_inc(ot_out.sem, 1)

            def chunk(i, following):
                ffn(i, FFN0)
                retention(i)
                ffn(i, FFN1, following)

            for g in range(CB):
                high_part(0, FFN0, 0, g, col("g1"))
            act.wait_ge(s_stage[2], 16)
            high_weights(9)
            with act.Fori(0, NCHUNK - 1) as i:
                chunk(i, i + 1)
            chunk(NCHUNK - 1, None)

        @block.tensor
        def _(pe):
            pe.wait_ge(s_const, 16 * N_CONST)
            pe.wait_ge(s_lo, 3)
            pe.wait_ge(s_ready, 1)

            def product(dst, wn, a, b, tok=None, act=slice(0, T)):
                for k, (w, y) in enumerate(((HI, actH), (LO, actH), (HI, actL))):
                    w = w[wn][:, a:b]
                    y = y[:, act] if tok is None else y[:, tok * P:(tok + 1) * P]
                    last = pe.matmul(dst, w if tok is None else y, y if tok is None else w, start=k == 0, stop=k == 2)
                return last

            def transposed(i, layer, n, g):
                for k, t in enumerate(tiles_of[g]):
                    pe.wait_ge(n_z.sem, n_z.at(i, layer, n * TT + t + 1))
                    last = pe.transpose(zt_ps[g][:, k * P:(k + 1) * P], z[:, t, :], W["identf"][:, :])
                last.then_inc(n_zT.sem, 1)

            def split(i, layer, n, g):
                pe.wait_ge(n_hi.sem, n_hi.at(i, layer, n * CB + g + 1))
                pe.wait_ge(n_lo.sem, n_lo.at(i, layer, n * CB + g + 1))

            def first_products(i, layer, wq, wk, wv):
                if layer == FFN0:
                    split(i, layer, 0, 0)
                    split(i, layer, 0, 1)
                else:
                    if layer == RET:
                        transposed(i, layer, 0, 0)
                    split(i, layer, 0, 0)
                qk_at = {0: (0, 1), 2: (2,), 4: (3,)} if layer == FFN0 else \
                    {0: (0, 1), 3: (0, 1), 5: (2,), 6: (3,)}
                for j in range(2 * TT):
                    if (layer, j) in ((RET, 1), (FFN1, 2)):
                        transposed(i, layer, 0, 1)
                    if (layer, j) == (FFN1, 2):
                        pe.wait_ge(x_new.sem, x_new.at(i, RET, CB))
                    if j == 3 and layer != FFN0:
                        split(i, layer, 0, 1)
                    for t in qk_at.get(j, ()):
                        if t < 2 and layer != FFN0:
                            project(i, layer, t, wq, wk, 0 if j == 0 else 1)
                        else:
                            project(i, layer, t, wq, wk)
                    if j >= 4:
                        pe.wait_ge(v_out.sem, v_out.at(i, layer, j - 3))
                    product(four[j % 4], wv, (j % 2) * 512, (j % 2 + 1) * 512, tok=j // 2).then_inc(v_acc.sem, 1)

            def project(i, layer, j, wq, wk, g=None):
                before, half = j - 2 if layer == RET or j <= QK_FIRST else j - 1, None
                if layer != FFN0 and before in (0, 1):
                    before, half = 0, before
                if before >= 0:
                    pe.wait_ge(qk_read.sem, qk_read.at(i, layer, qk_n(layer, before, half)))
                hp = j // 2
                product(qk_bank(layer, j, g), (wq, wk)[j % 2], hp * P, (hp + 1) * P,
                        act=slice(0, T) if g is None else batch[g]).then_inc(qk_acc.sem, 1)

            def output(layer, g, a, b):
                w = W["rwo"] if layer == RET else W["ow"]
                for n in range(a, b):
                    k, c = n // HP, n % HP
                    t = tiles_of[g][k]
                    last = pe.matmul(o_ps[g][:, k * P:(k + 1) * P], C[:, c, t * P:(t + 1) * P],
                                     w[:, c * P:(c + 1) * P], start=c == 0, stop=c == HP - 1)
                if b == GT * HP:
                    last.then_inc(o_acc.sem, 1)

            def scores(i, layer, u):
                hp, b = u // 2, u % 2
                pe.wait_ge(qk_rot.sem, qk_rot.at(i, layer, qk_n(layer, 2 * hp + 1)))
                if u < 2:
                    pe.wait_ge(v_out.sem, v_out.at(i, layer, 2 * TT - 2 + 2 * u))
                else:
                    pe.wait_ge(p_exp.sem, p_exp.at(i, layer, u - 1))
                for h in range(2):
                    r = slice(HD * h, HD * (h + 1))
                    q, k = qT[hp % 2][r, b * SEQ:(b + 1) * SEQ], kT[hp % 2][r, b * SEQ:(b + 1) * SEQ]
                    dst = S[u % 2][:, h, :]
                    diagonal = dst[:, :].rearrange("p (a s) -> p a s", a=2)[:, :, 0:P]
                    pe.matmul(diagonal, W["identb"][:, :], W["maskneg"][:, :].unsqueeze(1).broadcast_to((P, 2, P)),
                              start=True, stop=False)
                    pe.matmul(dst[:, 0:P], q[:, 0:P], k[:, 0:P], start=False, stop=False)
                    pe.matmul(dst[:, P:2 * P], q[:, P:SEQ], k[:, 0:P], start=False, stop=False)
                    last = pe.matmul(dst[:, 2 * P:SC], q[:, P:SEQ], k[:, P:SEQ], start=False, stop=True)
                last.then_inc(s_acc.sem, 1)

            def ffn(i, layer, following=None):
                first_products(i, layer, "wq", "wk", "wv")
                pe.wait_ge(s_late, 16 * len(late))

                def turned(n):
                    pe.wait_ge(p_norm.sem, p_norm.at(i, layer, n + 1))
                    if n >= 1:
                        pe.wait_ge(pt_out.sem, pt_out.at(i, layer, n))
                    for h in range(2):
                        w = prob[:, n % NPB, h, :]
                        for q in range(3):
                            last = pe.transpose(pt_ps[h][:, q * P:(q + 1) * P], w[:, q * P:(q + 1) * P], W["identf"][:, :])
                    last.then_inc(pt.sem, 1)

                def context(n):
                    hp, b = n // 2, n % 2
                    pe.wait_ge(pt_out.sem, pt_out.at(i, layer, n + 1))
                    if n >= 1:
                        pe.wait_ge(c_out.sem, c_out.at(i, layer, n))
                    for h in range(2):
                        dst = ctx_ps[HD * h:HD * (h + 1), :]
                        f = slice((2 * hp + h) * HD, (2 * hp + h + 1) * HD)
                        w = PT[:, n % 2, h, :]
                        pe.matmul(dst[:, 0:SEQ], V[:, 2 * b, f], w[:, 0:SEQ], start=True, stop=False)
                        last = pe.matmul(dst[:, P:SEQ], V[:, 2 * b + 1, f], w[:, SEQ:SC], start=False, stop=True)
                    last.then_inc(c_acc.sem, 1)

                for u in range(2 * HP + LAG - 1):
                    if u == 2 * HP + LAG - 2:
                        pe.wait_ge(p_exp.sem, p_exp.at(i, layer, 2 * HP - 1))
                        pe.wait_ge(c_out.sem, c_out.at(i, layer, 2 * HP - 5))
                        output(layer, 0, 0, HP - 2)
                    if u >= LAG:
                        turned(u - LAG)
                    if QK_FIRST - 2 <= u < 2 * HP - 2:
                        project(i, layer, u + 2, "wq", "wk")
                    if u < 2 * HP:
                        scores(i, layer, u)
                    if u > LAG:
                        context(u - LAG - 1)
                pe.wait_ge(p_exp.sem, p_exp.at(i, layer, 2 * HP))
                output(layer, 1, 0, HP - 2)
                context(2 * HP - 2)
                output(layer, 1, HP - 2, HP - 1)
                turned(2 * HP - 1)
                pe.wait_ge(c_out.sem, c_out.at(i, layer, 2 * HP - 1))
                output(layer, 0, HP - 2, GT * HP - HP // 2)
                context(2 * HP - 1)
                output(layer, 0, GT * HP - HP // 2, GT * HP)
                pe.wait_ge(c_out.sem, c_out.at(i, layer, 2 * HP))
                output(layer, 1, HP - 1, GT * HP)
                transposed(i, layer, 1, 0)

                def expert_in(k, act=slice(0, T)):
                    w, at = ("shw1", 0) if k == 0 else ("rew1", k - 1)
                    return product(h_ps(k)[:, act], w, at * P, (at + 1) * P, act=act)

                def spread(k):
                    if k >= 3:
                        pe.wait_ge(hg_out.sem, hg_out.at(i, layer, k - 2))
                    else:
                        before = max(n for n in range(AHEAD) if h_bank[n] == gate_bank(k))
                        pe.wait_ge(h_out.sem, h_out.at(i, layer, before + 1))
                    pe.matmul(four[gate_bank(k)], W["sel"][:, k - 1:k].broadcast_to((3 * SLOT, P)), gT[:, :],
                              start=True, stop=True).then_inc(gb_acc.sem, 1)

                def expert_out(k, g):
                    w, h = (W["shw2"][:, :], hsb[0]) if k == 0 else (W["rew2"][:, (k - 1) * P:k * P], hg[k % LATE])
                    last = pe.matmul(y_ps[g], w, h[:, batch[g]], start=k == 0, stop=k == EXPERTS)
                    if k == EXPERTS:
                        last.then_inc(y_acc.sem, 1)

                def output_biases(g):
                    for j in range(3):
                        pe.matmul(y_ps[g], b2p[j][:, :], gT[:, batch[g]], start=False, stop=False)

                def y_transposed(g):
                    pe.wait_ge(y_out.sem, y_out.at(i, layer, g + 1))
                    for k, t in enumerate(tiles_of[g]):
                        last = pe.transpose(yt_ps[g][:, k * P:(k + 1) * P], yT[:, t * P:(t + 1) * P], W["identf"][:, :])
                    last.then_inc(yt_acc.sem, 1)

                pe.wait_ge(s_lo, len(order))
                for g in range(CB):
                    split(i, layer, 1, g)
                    last = product(proj_ps[:, batch[g]], "router", 0, P, act=batch[g])
                    if g == CB - 1:
                        last.then_inc(lg_acc.sem, 1)
                    for k in range(FIRST):
                        last = expert_in(k, batch[g])
                        if g == CB - 1:
                            last.then_inc(h_acc.sem, 1)
                        if (g, k) == (CB - 1, 1):
                            pe.wait_ge(lg_out.sem, lg_out.at(i, layer, 1))
                            pe.sem_inc(s_taken_pe, 1)
                            for t in range(TT):
                                last = pe.transpose(ctx_ps[:, t * SLOT:(t + 1) * SLOT], lgT[:, t * P:(t + 1) * P],
                                                    W["identf"][0:SLOT, 0:SLOT])
                            last.then_inc(lg_tm.sem, 1)
                    if g == 0:
                        transposed(i, layer, 1, 1)
                for k in range(FIRST, AHEAD):
                    if h_before(k) is not None:
                        pe.wait_ge(h_out.sem, h_out.at(i, layer, h_before(k) + 1))
                    expert_in(k).then_inc(h_acc.sem, 1)
                pe.wait_ge(h_out.sem, h_out.at(i, layer, h_bank.index(5) + 1))
                for g in range(CB):
                    expert_out(0, g)
                pe.wait_ge(g_ready.sem, g_ready.at(i, layer, 1))
                for t in range(TT):
                    last = pe.transpose(ctx_ps.bitcast(BF16)[0:3 * SLOT, t * P:(t + 1) * P], g3[:, t, :], W["identb"][:, :])
                last.then_inc(gT_acc.sem, 1)
                pe.wait_ge(gT_out.sem, gT_out.at(i, layer, 1))
                spread(1)
                spread_to = 1
                for g in range(CB):
                    output_biases(g)
                for k in range(1, EXPERTS + 1):
                    n = k + AHEAD - 1
                    if n <= EXPERTS:
                        pe.wait_ge(h_out.sem, h_out.at(i, layer, h_before(n) + 1))
                        expert_in(n).then_inc(h_acc.sem, 1)
                    for _ in range(2):
                        if spread_to < min(k + LEAD, 2 * k, EXPERTS):
                            spread_to += 1
                            spread(spread_to)
                    pe.wait_ge(hg_out.sem, hg_out.at(i, layer, k))
                    expert_out(k, 0)
                    if k <= EXPERTS - LATE:
                        expert_out(k, 1)
                    if n == EXPERTS + 3 and following is not None:
                        for g in range(CB):
                            transposed(following, FFN0, 0, g)
                for k in range(EXPERTS - LATE + 1, EXPERTS + 1):
                    if k == EXPERTS - LATE // 2:
                        y_transposed(0)
                    expert_out(k, 1)
                y_transposed(1)

            def retention(i):
                first_products(i, RET, "rwq", "rwk", "rwv")

                def gates(c):
                    if c < GATES_FIRST:
                        pe.wait_ge(v_out.sem, v_out.at(i, RET, 2 * TT + c - (1 if c < 2 else 3)))
                    product(gate_ps(c), "rwg", c * P, (c + 1) * P).then_inc(v_acc.sem, 1)

                for c in range(GATES_FIRST):
                    if c < RHEADS - QK_FIRST:
                        project(i, RET, QK_FIRST + c, "rwq", "rwk")
                    gates(c)
                for u in range(2 * RHP + RLAG):
                    if u == 2 * RHP + RLAG - 1:
                        pe.wait_ge(og_out.sem, og_out.at(i, RET, 2 * RHP - 3))
                        output(RET, 0, 0, HP - 2)
                    if u < 2:
                        pe.wait_ge(v_out.sem, v_out.at(i, RET, 2 * TT + GATES_FIRST - 2 + 2 * u))
                    if u < 2 * RHP:
                        hp, b = u // 2, u % 2
                        pe.wait_ge(qk_rot.sem, qk_rot.at(i, RET, qk_n(RET, 2 * hp + 1)))
                        if u >= 2:
                            pe.wait_ge(a_out.sem, a_out.at(i, RET, u - 1))
                        for h in range(2):
                            r = slice(HD * h, HD * (h + 1))
                            q, k = rqk[2 * hp][r, b * SEQ:(b + 1) * SEQ], rqk[2 * hp + 1][r, b * SEQ:(b + 1) * SEQ]
                            dst = S[u % 2][:, h, :]
                            pe.matmul(dst[:, 0:SEQ], k[:, 0:P], q, start=True, stop=True)
                            last = pe.matmul(dst[:, SEQ:SC], k[:, P:SEQ], q[:, P:SEQ], start=True, stop=True)
                        last.then_inc(s_acc.sem, 1)
                    if 1 <= u <= 2 * RHP:
                        n = u - 1
                        hp, b = n // 2, n % 2
                        pe.wait_ge(a_out.sem, a_out.at(i, RET, n + 1))
                        if n >= 3:
                            pe.wait_ge(on_out.sem, on_out.at(i, RET, n - 2))
                        for h in range(2):
                            f = slice((2 * hp + h) * P, (2 * hp + h + 1) * P)
                            w = PT[:, n % 2, h, :]
                            d = ro_ps[n % 3]
                            a = h * SEQ
                            pe.matmul(d[:, a:a + P], w[:, 0:P], V[:, 2 * b, f], start=True, stop=True)
                            pe.matmul(d[:, a + P:a + SEQ], w[:, P:SEQ], V[:, 2 * b, f], start=True, stop=False)
                            last = pe.matmul(d[:, a + P:a + SEQ], w[:, SEQ:SC], V[:, 2 * b + 1, f], start=False, stop=True)
                        last.then_inc(ro_acc.sem, 1)
                    if 2 * RHP <= u < 2 * RHP + RHEADS - GATES_FIRST:
                        gates(GATES_FIRST + u - 2 * RHP)
                    if u >= RLAG:
                        n = u - RLAG
                        pe.wait_ge(on_out.sem, on_out.at(i, RET, n + 1))
                        if n >= 1:
                            pe.wait_ge(ot_out.sem, ot_out.at(i, RET, n))
                        for h in range(2):
                            for q in range(2):
                                a = h * SEQ + q * P
                                last = pe.transpose(ctx_ps[:, a:a + P], onrm[n % 2][:, h, q, :], W["identf"][:, :])
                        last.then_inc(ot_acc.sem, 1)
                pe.wait_ge(og_out.sem, og_out.at(i, RET, 2 * RHP - 1))
                output(RET, 0, HP - 2, GT * HP)
                pe.wait_ge(og_out.sem, og_out.at(i, RET, 2 * RHP))
                output(RET, 1, 0, MIDWAY)
                transposed(i, FFN1, 0, 0)
                output(RET, 1, MIDWAY, GT * HP)

            def chunk(i, following):
                ffn(i, FFN0)
                retention(i)
                ffn(i, FFN1, following)

            for g in range(CB):
                transposed(0, FFN0, 0, g)
            with pe.Fori(0, NCHUNK - 1) as i:
                chunk(i, i + 1)
            chunk(NCHUNK - 1, None)

        @block.vector
        def _(dve):
            count = [0]

            def link(ins):
                count[0] += 1
                ins.then_inc(s_prep, 1)
                dve.wait_ge(s_prep, count[0])

            dve.wait_ge(s_const, 16 * N_CONST)
            link(dve.tensor_scalar(ang, pos, col("theta"), None, ALU.mult))
            for j, shift in ((0, 0.25), (1, 0.0)):
                link(dve.tensor_scalar(turn, ang, float(np.float32(1 / (2 * np.pi))), shift, ALU.mult, ALU.add))
                link(dve.tensor_scalar(part, turn, MAGIC, None, ALU.add))
                link(dve.tensor_scalar(turn, part, -MAGIC, None, ALU.add))
                src = ang
                for c in (TWO_PI_1, TWO_PI_2, TWO_PI_3):
                    link(dve.scalar_tensor_tensor(out=part, in0=turn, scalar=-c, in1=src, op0=ALU.mult, op1=ALU.add))
                    src = part
                if shift:
                    link(dve.tensor_scalar(part, part, float(np.float32(np.pi / 2)), None, ALU.add))
                link(dve.tensor_scalar(reduced[j], part, PI_IN, -PI_IN, ALU.min, ALU.max))
                dve.sem_inc(s_angle, 1)
            def low_weights(k):
                n = order[k]
                dve.wait_ge(s_hi, k + 1)
                dve.scalar_tensor_tensor(out=LO[n][:, :], in0=raw[n], scalar=HD ** -0.5 if n == "wq" else 1.0,
                                         in1=HI[n][:, :].bitcast(F32), op0=ALU.mult, op1=ALU.subtract).then_inc(s_lo, 1)

            for k in range(3):
                low_weights(k)
            for n, v in (("identb", W["identf"][:, :]), ("maskneg", mask_in), ("sel", sel_in)):
                link(dve.tensor_copy(W[n][:, :], v))
            dve.wait_ge(s_sin, 2)
            link(dve.tensor_scalar(sinT[:, :], sinT[:, :], col("sign"), None, ALU.mult))
            link(dve.tensor_scalar(shb2h[:, :], col("shb2"), 0.5, None, ALU.mult))
            a = COL["qb"][0]
            link(dve.tensor_scalar(qbh[:, :], W["cols"][:, a:a + 2 * HP], HD ** -0.5, None, ALU.mult))
            b2 = b2x
            for j in range(3):
                link(dve.tensor_copy(b2p[j][:, :], b2))
                if j < 2:
                    link(dve.tensor_tensor(b2, b2, b2p[j][:, :], ALU.subtract))
            dve.wait_ge(s_pool0, 3)
            dve.sem_inc(s_ready, 1)
            swap = [p ^ 1 for p in range(32)]

            def table(tb):
                return tb[:, :].unsqueeze(1).broadcast_to((P, CB, SEQ))

            def by_batch(ap):
                return ap.rearrange("p (b s) -> p b s", b=CB)

            def apart():
                dve.sem_inc(s_taken, 1)

            def variance(i, layer, src, g):
                n = 2 * GT * g
                for t in tiles_of[g]:
                    dve.bn_stats(stat[:, t, :], src[:, t, :]).then_inc(n_stat.sem, 1)
                dve.wait_ge(n_stat.sem, n_stat.at(i, layer, n + GT))
                apart()
                for t in tiles_of[g]:
                    dve.bn_aggr(mv[:, t, :], stat[:, t, :]).then_inc(n_stat.sem, 1)
                dve.wait_ge(n_stat.sem, n_stat.at(i, layer, n + 2 * GT))
                mul, add = (1.0, EPS) if layer == RET else (1.0 + EPS, EPS * EPS)
                w = slice(g * GT, (g + 1) * GT)
                dve.tensor_scalar(wv_[:, w], mv[:, w, 1], mul, add, ALU.mult, ALU.add).then_inc(n_var.sem, 1)

            def normalised(i, layer, src, g):
                dve.wait_ge(n_rs.sem, n_rs.at(i, layer, g + 1))
                for t in tiles_of[g]:
                    dve.tensor_scalar(z[:, t, :], src[:, t, :], mv[:, t, 0:1], rs[:, t:t + 1],
                                      ALU.subtract, ALU.mult).then_inc(n_z.sem, 1)

            def low_part(i, layer, n, g, gamma):
                dve.wait_ge(n_hi.sem, n_hi.at(i, layer, n * CB + g + 1))
                dve.scalar_tensor_tensor(out=actL[:, batch[g]], in0=zt_ps[g], scalar=gamma,
                                         in1=actH[:, batch[g]].bitcast(F32),
                                         op0=ALU.mult, op1=ALU.subtract).then_inc(n_lo.sem, 1)

            def entry(i, layer, arrive, gamma):
                arrive(0)
                variance(i, layer, x, 0)
                normalised(i, layer, x, 0)
                if layer == FFN1:
                    low_part(i, layer, 0, 0, gamma)
                arrive(1)
                variance(i, layer, x, 1)
                if layer == RET:
                    low_part(i, layer, 0, 0, gamma)
                normalised(i, layer, x, 1)
                rotate(i, layer, 0, 0)
                low_part(i, layer, 0, 1, gamma)
                rotate(i, layer, 1, 0)

            def rotate(i, layer, j, g=None):
                hp = j // 2
                cos_, sin_ = (W["rcos"], W["rsin"]) if layer == RET else (cosT, sinT)
                dve.wait_ge(qk_acc.sem, qk_acc.at(i, layer, qk_n(layer, j, g)))
                if j >= 2:
                    dve.wait_ge(qk_rot.sem, qk_rot.at(i, layer, qk_n(layer, j - 2)))
                if layer == RET:
                    b, bs = 0.0, 0.0
                elif j % 2 == 0:
                    b, bs = qbh[:, hp:hp + 1], qbh[:, HP + hp:HP + hp + 1]
                else:
                    b, bs = col("kb", hp), col("kbs", hp)
                a, b_ = (rrc[j % 2], rrsw[j % 2]) if layer == RET else (rc[j % 2], rsw[j % 2])
                ps = qk_bank(layer, j, g)
                if g is None:
                    of, cos_, sin_ = by_batch, table(cos_), table(sin_)
                else:
                    a, b_ = a[:, batch[g]], b_[:, batch[g]]
                    of, cos_, sin_ = lambda ap: ap, cos_[:, :], sin_[:, :]
                dve.scalar_tensor_tensor(out=of(a), in0=of(ps), scalar=b, in1=cos_, op0=ALU.add, op1=ALU.mult)
                dve.stream_shuffle(b_, ps, swap).then_inc(qk_read.sem, 1)
                dve.wait_ge(qk_read.sem, qk_read.at(i, layer, qk_n(layer, j, g)))
                dve.scalar_tensor_tensor(out=of(b_), in0=of(b_), scalar=bs, in1=sin_, op0=ALU.add, op1=ALU.mult)\
                    .then_inc(qk_mul.sem, 1)

            def ffn(i, layer, following=None):
                if layer == FFN1:
                    for j in range(2):
                        rotate(i, layer, j, 1)
                for j in range(2 if layer == FFN1 else 0, QK_FIRST):
                    rotate(i, layer, j)
                for u in range(2 * HP + 1):
                    if QK_FIRST - 2 <= u < 2 * HP - 2:
                        rotate(i, layer, u + 2)
                    if u < 2 * HP:
                        dve.wait_ge(s_acc.sem, s_acc.at(i, layer, u + 1))
                        dve.tensor_reduce(negm[:, u % 2, 0, :], S[u % 2][:, :, 0:P], AX_X, ALU.max, negate=True)
                        dve.tensor_reduce(negm[:, u % 2, 1, :], S[u % 2][:, :, P:SC], AX_X, ALU.max, negate=True)\
                            .then_inc(mx.sem, 1)
                    if 1 <= u <= 2 * HP:
                        dve.wait_ge(p_exp.sem, p_exp.at(i, layer, u))
                        dve.reciprocal(rinv[:, (u - 1) % NPB, :, :], rsum[:, (u - 1) % NPB, :, :]).then_inc(p_inv.sem, 1)
                dve.wait_ge(xn_ready.sem, xn_ready.at(i, layer, 1))
                if layer == FFN0:
                    dve.wait_ge(s_out, i * 16 + 16)
                for g in range(CB):
                    w = slice(g * GT, (g + 1) * GT)
                    dve.wait_ge(o_acc.sem, o_acc.at(i, layer, g + 1))
                    dve.tensor_tensor(ao[:, w, :], by_tile(o_ps[g]), xnb[:, w, :], ALU.add).then_inc(ao_ready.sem, 1)
                    dve.wait_ge(ss_ready.sem, ss_ready.at(i, layer, g + 1))
                    dve.tensor_scalar(wv_[:, w], wv_[:, w], 1.0 / P, EPS, ALU.mult, ALU.add).then_inc(n_var.sem, 1)
                    dve.wait_ge(n_rs.sem, n_rs.at(i, layer, CB + g + 1))
                    for t in tiles_of[g]:
                        dve.tensor_scalar(z[:, t, :], ao[:, t, :], rs[:, t:t + 1], None, ALU.mult).then_inc(n_z.sem, 1)
                    low_part(i, layer, 1, g, col("g2"))

                steps = [0]

                def step(ins):
                    steps[0] += 1
                    ins.then_inc(rt_step.sem, 1)
                    dve.wait_ge(rt_step.sem, rt_step.at(i, layer, steps[0]))

                def note(ins):
                    steps[0] += 1
                    ins.then_inc(rt_step.sem, 1)

                def wide(ap):
                    return ap[:, :].unsqueeze(2).broadcast_to((P, TT, EXPERTS))

                dve.wait_ge(lg_tm.sem, lg_tm.at(i, layer, 1))
                logits = ctx_ps[:, 0:TT * SLOT].rearrange("p (t e) -> p t e", t=TT)[:, :, 0:EXPERTS]
                step(dve.tensor_reduce(lmx[:, :], logits, AX_X, ALU.max, negate=True))
                dve.tensor_tensor(lg, logits, wide(lmx), ALU.add).then_inc(lg_sub.sem, 1)
                dve.wait_ge(lg_exp.sem, lg_exp.at(i, layer, 1))
                step(dve.tensor_reduce(lsum[:, :], ex, AX_X, ALU.add))
                step(dve.reciprocal(linv[:, :], lsum[:, :]))
                step(dve.tensor_tensor(aff[:, :, 0:EXPERTS], ex, wide(linv), ALU.mult))
                apart()
                for t in range(TT):
                    note(dve.max(top[:, t, :], aff[:, t, :]))
                dve.wait_ge(rt_step.sem, rt_step.at(i, layer, steps[0]))
                step(dve.memset(top[:, :, TOPK:8], -1.0))
                apart()
                for t in range(TT):
                    note(dve.match_replace(rest[:, t, :], top[:, t, :], aff[:, t, :], 0.0))
                dve.wait_ge(rt_step.sem, rt_step.at(i, layer, steps[0]))
                step(dve.tensor_tensor(gate[:, :, 0:EXPERTS], aff[:, :, 0:EXPERTS], rest[:, :, 0:EXPERTS], ALU.subtract))
                part_ = [g3[:, :, j * SLOT:j * SLOT + EXPERTS] for j in range(3)]
                g_, r_ = gate[:, :, 0:EXPERTS], gres[:, :, 0:EXPERTS]
                step(dve.tensor_copy(part_[0], g_))
                step(dve.tensor_tensor(r_, g_, part_[0], ALU.subtract))
                step(dve.tensor_copy(part_[1], r_))
                dve.tensor_tensor(part_[2], r_, part_[1], ALU.subtract).then_inc(g_ready.sem, 1)
                assert steps[0] == rt_step.per_layer[layer], steps[0]
                dve.wait_ge(gT_acc.sem, gT_acc.at(i, layer, 1))
                dve.tensor_copy(gT[:, :], ctx_ps.bitcast(BF16)[0:3 * SLOT, 0:T]).then_inc(gT_out.sem, 1)
                for k in range(1, EXPERTS + 1):
                    dve.wait_ge(gb_acc.sem, gb_acc.at(i, layer, k))
                    dve.wait_ge(h_out.sem, h_out.at(i, layer, k + 1))
                    dve.tensor_tensor(hg[k % LATE], hsb[k % AHEAD], four[gate_bank(k)], ALU.mult).then_inc(hg_out.sem, 1)
                    if following is not None:
                        if k == EXPERTS // 2:
                            dve.wait_ge(s_xin, following * 16 + 16)
                            for g in range(CB):
                                variance(following, FFN0, xin, g)
                        if k == EXPERTS // 2 + 4:
                            dve.wait_ge(res_ready.sem, res_ready.at(i, layer, 1))
                            for g in range(CB):
                                normalised(following, FFN0, xin, g)
                        if k == EXPERTS - 2:
                            for g in range(CB):
                                low_part(following, FFN0, 0, g, col("g1"))
                dve.wait_ge(res_ready.sem, res_ready.at(i, layer, 1))

            def result(i, layer, dst, g):
                w = slice(g * GT, (g + 1) * GT)
                dve.wait_ge(yt_acc.sem, yt_acc.at(i, layer, g + 1))
                dve.tensor_tensor(dst[:, w, :], by_tile(yt_ps[g]), res[:, w, :], ALU.add).then_inc(x_new.sem, 1)
                dve.wait_ge(x_new.sem, x_new.at(i, layer, g + 1))

            def retained(i, g):
                w = slice(g * GT, (g + 1) * GT)
                dve.wait_ge(o_acc.sem, o_acc.at(i, RET, g + 1))
                dve.tensor_tensor(x[:, w, :], by_tile(o_ps[g]), x[:, w, :], ALU.add).then_inc(x_new.sem, 1)
                dve.wait_ge(x_new.sem, x_new.at(i, RET, g + 1))

            def retention(i):
                for j in range(2):
                    rotate(i, RET, j, 1)
                for j in range(2, 2 * RHP):
                    rotate(i, RET, j)
                dve.wait_ge(s_late, 16 * len(late))
                for u in range(2 * RHP + 1):
                    if u < 2 * RHP:
                        hp = u // 2
                        dve.wait_ge(s_acc.sem, s_acc.at(i, RET, u + 1))
                        dec = W["decay"][:, :].rearrange("p (h s) -> p h s", h=RHEADS)[:, 2 * hp:2 * hp + 2, :]
                        dve.tensor_tensor(PT[:, u % 2, :, 0:SEQ], S[u % 2][:, :, 0:SEQ], dec, ALU.mult)
                        dve.tensor_tensor(PT[:, u % 2, :, SEQ:SC], S[u % 2][:, :, SEQ:SC], dec[:, :, 0:P], ALU.mult)\
                            .then_inc(a_out.sem, 1)
                    if 1 <= u <= 2 * RHP:
                        n = u - 1
                        dve.wait_ge(ro_acc.sem, ro_acc.at(i, RET, n + 1))
                        for hq in range(4):
                            dve.bn_stats(rstat[:, n % 3, hq, :], ro_ps[n % 3][:, hq * P:(hq + 1) * P]).then_inc(ro_stat.sem, 1)
                        dve.wait_ge(ro_stat.sem, ro_stat.at(i, RET, 8 * n + 4))
                        apart()
                        for hq in range(4):
                            dve.bn_aggr(rmv[:, n % 3, hq, :], rstat[:, n % 3, hq, :]).then_inc(ro_stat.sem, 1)
                        dve.wait_ge(ro_stat.sem, ro_stat.at(i, RET, 8 * n + 8))
                        dve.tensor_scalar(rnm[:, n % 3, :], rmv[:, n % 3, :, 0], -1.0, None, ALU.mult)
                        dve.tensor_scalar(rw_[:, n % 3, :], rmv[:, n % 3, :, 1], 1.0, EPS, ALU.mult, ALU.add)\
                            .then_inc(ro_var.sem, 1)

            def chunk(i, following):
                ffn(i, FFN0)
                entry(i, RET, lambda g: result(i, FFN0, x, g), 1.0)
                retention(i)
                entry(i, FFN1, lambda g: retained(i, g), col("g1"))
                ffn(i, FFN1, following)
                for g in range(CB):
                    result(i, FFN1, xout, g)

            dve.wait_ge(s_xin, 16)
            for g in range(CB):
                variance(0, FFN0, xin, g)
            for g in range(CB):
                normalised(0, FFN0, xin, g)
            for k in range(3, 9):
                low_weights(k)
            for g in range(CB):
                low_part(0, FFN0, 0, g, col("g1"))
            low_weights(9)
            with dve.Fori(0, NCHUNK - 1) as i:
                chunk(i, i + 1)
            chunk(NCHUNK - 1, None)


def shape_constants():
    f = np.float32
    c = {"identf": np.eye(P, dtype=f), }
    rows = np.arange(P)
    c["maskneg"] = np.where(rows[None, :] > rows[:, None], -1e30, 0.0).astype(f)
    sel = np.zeros((3 * SLOT, SLOT), f)
    for j in range(3):
        sel[j * SLOT + np.arange(EXPERTS), np.arange(EXPERTS)] = 1
    c["sel"] = sel
    c["pos"] = np.broadcast_to(np.arange(SEQ, dtype=f), (P, SEQ)).copy()
    gamma = f(1) - np.exp2(f(-5) - np.arange(RHEADS, dtype=f))
    s = np.log2(gamma).astype(f)
    rel = (np.arange(SEQ, dtype=f)[None, :] - rows[:, None].astype(f))
    d = np.where(rel[:, None, :] >= 0, np.exp2(rel[:, None, :] * s[None, :, None]), f(0)) * f(HD ** -0.5)
    c["decay"] = d.astype(f).reshape(P, RHEADS * SEQ)
    inv = (f(1) / np.power(f(10000), np.arange(0, HD, 2, dtype=f) / f(HD))).astype(f)
    ang = (np.arange(SEQ, dtype=f)[None, :] * inv[:, None]).astype(f)
    sign = np.where(rows % 2 == 0, -1, 1).astype(f)
    pair = (rows % HD) // 2
    c["rcos"] = np.cos(ang)[pair].astype(f)
    c["rsin"] = (np.sin(ang)[pair] * sign[:, None]).astype(f)
    return c, sign


def kernel(**inputs):
    import concourse.bacc as bacc
    from concourse.bass_utils import run_bass_kernel_spmd

    a = {k.replace("L0_ffn_", "f_").replace("L0_attn_", "r_"): np.asarray(v) for k, v in inputs.items()}
    arrays, sign = shape_constants()
    pairs = lambda v: v.reshape(-1, P).T
    by_pair = lambda w: w.reshape(-1, P, P).transpose(1, 0, 2).reshape(P, -1)
    swap = np.arange(P) ^ 1
    arrays["wq"], arrays["wk"], arrays["wv"] = a["f_q_w"], a["f_k_w"], a["f_v_w"]
    router = np.zeros((P, P), np.float32)
    router[:, :EXPERTS] = a["f_router_w"]
    arrays["router"] = router
    arrays["shw1"], arrays["shw2"] = a["f_sh_w1"], a["f_sh_w2"]
    arrays["rew1"] = a["f_re_w1"].transpose(1, 0, 2).reshape(P, -1)
    arrays["rew2"] = a["f_re_w2"].transpose(1, 0, 2).reshape(P, -1)
    arrays["ow"] = by_pair(a["f_o_w"])
    mix = np.arange(RFEAT).reshape(RHEADS, 2, HD // 2).transpose(0, 2, 1).reshape(-1)
    arrays["rwq"], arrays["rwk"] = a["r_Wq"][mix].T, a["r_Wk"][mix].T
    arrays["rwv"], arrays["rwg"] = a["r_Wv"].T, a["r_Wg"].T
    arrays["rwo"] = by_pair(a["r_Wo"].T)
    for name, key in (("g1row", "f_gamma1"), ("g2row", "f_gamma2"), ("obrow", "f_o_b")):
        arrays[name] = np.broadcast_to(a[key][None, :], (P, P))
    b2x = np.zeros((3, SLOT, P), np.float32)
    b2x[:, :EXPERTS] = a["f_re_b2"][None]
    arrays["b2x"] = b2x.reshape(3 * SLOT, P)
    rb = np.zeros((P, 1), np.float32)
    rb[:EXPERTS, 0] = a["f_router_b"]
    vec = {"g1": a["f_gamma1"][:, None], "g2": a["f_gamma2"][:, None],
           "qb": pairs(a["f_q_b"]), "qbs": pairs(a["f_q_b"])[swap], "kb": pairs(a["f_k_b"]),
           "kbs": pairs(a["f_k_b"])[swap], "vb": pairs(a["f_v_b"]), "shb1": a["f_sh_b1"][:, None],
           "shb2": a["f_sh_b2"][:, None], "reb1": a["f_re_b1"].T, "gnw": pairs(a["r_gn_weight"]),
           "gnb": pairs(a["r_gn_bias"]), "rb": rb, "theta": a["f_theta"][(np.arange(P) % HD) // 2][:, None],
           "sign": sign[:, None]}
    cols = np.zeros((P, LOADED["cols"][1]), np.float32)
    for n, (at, w) in COL.items():
        cols[:, at:at + w] = vec[n]
    arrays["cols"] = cols

    nc = bacc.Bacc("TRN2", target_bir_lowering=False, num_devices=1)
    feeds, ins = {}, {}
    arrays["x"] = a["r_x"].reshape(NTOK, P)
    for n, v in arrays.items():
        v = np.ascontiguousarray(v)
        feeds["in_" + n] = v
        ins[n] = nc.dram_tensor("in_" + n, v.shape, mybir.dt.from_np(v.dtype), kind="ExternalInput").ap()
    out = nc.dram_tensor("out_x", (NTOK, P), F32, kind="ExternalOutput").ap()
    build(nc, ins["x"], ins, out)
    r = run_bass_kernel_spmd(nc, [feeds], core_ids=[0])
    return r.results[0]["out_x"].reshape(16, SEQ, P)
```
